# Optimizing a Trainium2 kernel written in Bass

```python
import numpy as np
import jax
import jax.numpy as jnp

def _softmax(x, axis=-1):
    return jax.nn.softmax(x, axis=axis)

def _gelu(x):
    return jax.nn.gelu(x, approximate=True)

def _silu(x):
    return jax.nn.silu(x)

def _sigmoid(x):
    return jax.nn.sigmoid(x)

def _layernorm(x, axis=-1, eps=1e-05):
    m = jnp.mean(x, axis=axis, keepdims=True)
    v = jnp.var(x, axis=axis, keepdims=True)
    return (x - m) / jnp.sqrt(v + eps)

def _scatter_add(tgt, idx, src, axis=0):
    return tgt.at[idx].add(src)

def _segment_sum(src, seg, n):
    return jax.ops.segment_sum(src, seg, n)
kernel_name = 'mk_seq_preln_d2_jaxref_r8_07df1a'

def setup_inputs(seed: int=0):
    np.random.seed(seed)
    _w = jnp.asarray

    def _L0_attn_setup():
        import jax, jax.numpy as jnp
        import numpy as np
        D_MODEL = 256
        N_HEADS = 16
        HEAD_DIM = D_MODEL // N_HEADS
        CAUSAL = True
        key = jax.random.key(seed)
        k1, k2, k3, k4, k5 = jax.random.split(key, 5)
        scale = 1.0 / np.sqrt(D_MODEL)
        x = jax.random.normal(k1, (1, 256, D_MODEL), dtype=jnp.float32)
        W_Q = jax.random.normal(k2, (D_MODEL, D_MODEL), dtype=jnp.float32) * scale
        W_K = jax.random.normal(k3, (D_MODEL, D_MODEL), dtype=jnp.float32) * scale
        W_V = jax.random.normal(k4, (D_MODEL, D_MODEL), dtype=jnp.float32) * scale
        W_O = jax.random.normal(k5, (D_MODEL, D_MODEL), dtype=jnp.float32) * scale
        return {'x': x, 'W_Q': W_Q, 'W_K': W_K, 'W_V': W_V, 'W_O': W_O}
    _L0_attn_in = _L0_attn_setup()

    def _L0_ffn_setup():
        import jax, jax.numpy as jnp
        import numpy as np
        H, LAT, INTER, E, G, TOPK_G, TOP_K = (256, 128, 128, 32, 4, 2, 8)
        SHARED_INTER = 512
        ROUTED_SCALE = 2.5
        B, S = (2, 128)

        def relu2(x):
            return jnp.square(jax.nn.relu(x))
        key = jax.random.key(seed)
        ks = jax.random.split(key, 9)
        w = 0.02
        return {'hidden_states': jax.random.normal(ks[0], (B, S, H), jnp.float32), 'gate_w': jax.random.normal(ks[1], (E, H), jnp.float32) * w, 'gate_bias': jax.random.normal(ks[2], (E,), jnp.float32) * w, 'fc1_w': jax.random.normal(ks[3], (LAT, H), jnp.float32) * w, 'fc2_w': jax.random.normal(ks[4], (H, LAT), jnp.float32) * w, 'w1': jax.random.normal(ks[5], (E, INTER, LAT), jnp.float32) * w, 'w2': jax.random.normal(ks[6], (E, LAT, INTER), jnp.float32) * w, 'shared_up_w': jax.random.normal(ks[7], (SHARED_INTER, H), jnp.float32) * w, 'shared_down_w': jax.random.normal(ks[8], (H, SHARED_INTER), jnp.float32) * w}
    _L0_ffn_in = _L0_ffn_setup()

    def _L1_attn_setup():
        import jax, jax.numpy as jnp
        import numpy as np
        B, N, HID, H, D = (2, 1024, 256, 16, 128)
        BLOCK = 32
        EPS = 1e-06

        def _alibi_slopes(h):
            start = 2.0 ** (-2.0 ** (-(np.log2(h) - 3)))
            return np.array([start * start ** i for i in range(h)], dtype=np.float32)

        def _lightning_attention(q, k, v, slope_rate):
            b, h, n, d = q.shape
            nb = n // BLOCK
            s = slope_rate.reshape(1, h, 1, 1).astype(q.dtype)
            arr = jnp.arange(1, BLOCK + 1, dtype=q.dtype)
            q_decay = jnp.exp(-s * arr[None, None, :, None])
            k_decay = jnp.exp(-s * (BLOCK - arr)[None, None, :, None])
            idx = arr[:, None] - arr[None, :]
            diag_decay = jnp.where(idx[None, None] >= 0, jnp.exp(-s * idx[None, None]), 0.0)
            block_decay = jnp.exp(-s * BLOCK)

            def to_blocks(x):
                return x.reshape(b, h, nb, BLOCK, d).transpose(2, 0, 1, 3, 4)
            qb, kb, vb = (to_blocks(q), to_blocks(k), to_blocks(v))

            def step(kv, blk):
                qi, ki, vi = blk
                inter = jnp.einsum('bhld,bhde->bhle', qi * q_decay, kv)
                qk = jnp.einsum('bhld,bhmd->bhlm', qi, ki) * diag_decay
                intra = jnp.einsum('bhlm,bhme->bhle', qk, vi)
                kv = block_decay * kv + jnp.einsum('bhld,bhle->bhde', ki * k_decay, vi)
                return (kv, inter + intra)
            kv0 = jnp.zeros((b, h, d, d), q.dtype)
            _, out = jax.lax.scan(step, kv0, (qb, kb, vb))
            return out.transpose(1, 2, 0, 3, 4).reshape(b, h, n, d)
        key = jax.random.key(seed)
        k1, k2, k3, k4 = jax.random.split(key, 4)
        scale = 0.02
        hidden_states = jax.random.normal(k1, (B, N, HID), jnp.float32)
        w_qkv = jax.random.normal(k2, (HID, 3 * H * D), jnp.float32) * scale
        w_gate = jax.random.normal(k3, (HID, H * D), jnp.float32) * scale
        w_out = jax.random.normal(k4, (H * D, HID), jnp.float32) * scale
        rms_weight = jnp.ones((H * D,), jnp.float32)
        slope_rate = jnp.asarray(_alibi_slopes(H)).reshape(H, 1, 1) * (1.0 + 1e-05)
        return dict(hidden_states=hidden_states, slope_rate=slope_rate, w_qkv=w_qkv, w_gate=w_gate, w_out=w_out, rms_weight=rms_weight)
    _L1_attn_in = _L1_attn_setup()

    def _L1_ffn_setup():
        import jax, jax.numpy as jnp
        import numpy as np
        NUM_EXPERTS = 128
        NUM_KEPT = 48
        TOP_K = 8
        HIDDEN = 256
        INTER = 96
        CAP = 96
        BATCH, SEQ = (2, 128)
        key = jax.random.key(seed)
        k1, k2, k3, k4 = jax.random.split(key, 4)
        hidden_states = jax.random.normal(k1, (BATCH, SEQ, HIDDEN), jnp.float32)
        gate_weight = jax.random.normal(k2, (NUM_EXPERTS, HIDDEN), jnp.float32) * 0.02
        gate_up_proj = jax.random.normal(k3, (NUM_KEPT, 2 * INTER, HIDDEN), jnp.float32) * 0.02
        down_proj = jax.random.normal(k4, (NUM_KEPT, HIDDEN, INTER), jnp.float32) * 0.02
        o2n = -np.ones(NUM_EXPERTS, np.int32)
        o2n[np.arange(NUM_KEPT) * 2] = np.arange(NUM_KEPT, dtype=np.int32)
        old_to_new = jnp.asarray(o2n)
        return {'hidden_states': hidden_states, 'gate_weight': gate_weight, 'gate_up_proj': gate_up_proj, 'down_proj': down_proj, 'old_to_new': old_to_new}
    _L1_ffn_in = _L1_ffn_setup()
    _d = {'L0_attn_x': _L0_attn_in['x'], 'L0_attn_W_Q': _L0_attn_in['W_Q'], 'L0_attn_W_K': _L0_attn_in['W_K'], 'L0_attn_W_V': _L0_attn_in['W_V'], 'L0_attn_W_O': _L0_attn_in['W_O'], 'L0_ffn_gate_w': _L0_ffn_in['gate_w'], 'L0_ffn_gate_bias': _L0_ffn_in['gate_bias'], 'L0_ffn_fc1_w': _L0_ffn_in['fc1_w'], 'L0_ffn_fc2_w': _L0_ffn_in['fc2_w'], 'L0_ffn_w1': _L0_ffn_in['w1'], 'L0_ffn_w2': _L0_ffn_in['w2'], 'L0_ffn_shared_up_w': _L0_ffn_in['shared_up_w'], 'L0_ffn_shared_down_w': _L0_ffn_in['shared_down_w'], 'L1_attn_slope_rate': _L1_attn_in['slope_rate'], 'L1_attn_w_qkv': _L1_attn_in['w_qkv'], 'L1_attn_w_gate': _L1_attn_in['w_gate'], 'L1_attn_w_out': _L1_attn_in['w_out'], 'L1_attn_rms_weight': _L1_attn_in['rms_weight'], 'L1_ffn_gate_weight': _L1_ffn_in['gate_weight'], 'L1_ffn_gate_up_proj': _L1_ffn_in['gate_up_proj'], 'L1_ffn_down_proj': _L1_ffn_in['down_proj'], 'L1_ffn_old_to_new': _L1_ffn_in['old_to_new']}
    _x0 = _d['L0_attn_x']
    _d['L0_attn_x'] = jax.random.normal(jax.random.fold_in(jax.random.key(seed), 1), (4, 1024, 256), dtype=_x0.dtype)
    del _x0
    return _d

def reference(L0_attn_x, L0_attn_W_Q, L0_attn_W_K, L0_attn_W_V, L0_attn_W_O, L0_ffn_gate_w, L0_ffn_gate_bias, L0_ffn_fc1_w, L0_ffn_fc2_w, L0_ffn_w1, L0_ffn_w2, L0_ffn_shared_up_w, L0_ffn_shared_down_w, L1_attn_slope_rate, L1_attn_w_qkv, L1_attn_w_gate, L1_attn_w_out, L1_attn_rms_weight, L1_ffn_gate_weight, L1_ffn_gate_up_proj, L1_ffn_down_proj, L1_ffn_old_to_new):

    def _L0_attn_ref(x, W_Q, W_K, W_V, W_O):
        import jax, jax.numpy as jnp
        import numpy as np
        D_MODEL = 256
        N_HEADS = 16
        HEAD_DIM = D_MODEL // N_HEADS
        CAUSAL = True
        B, T, D = x.shape
        H, h = (N_HEADS, HEAD_DIM)

        def proj(W):
            return (x @ W.T).reshape(B, T, H, h).transpose(0, 2, 1, 3)
        q = proj(W_Q)
        k = proj(W_K)
        v = proj(W_V)
        scores = jnp.einsum('bhqd,bhkd->bhqk', q, k) / jnp.sqrt(jnp.float32(h))
        if CAUSAL:
            causal_mask = jnp.tril(jnp.ones((T, T), dtype=bool))
            scores = jnp.where(causal_mask, scores, -jnp.inf)
        p = jax.nn.softmax(scores, axis=-1)
        o = jnp.einsum('bhqk,bhkd->bhqd', p, v)
        o = o.transpose(0, 2, 1, 3).reshape(B, T, D)
        return o @ W_O.T

    def _L0_ffn_ref(hidden_states, gate_w, gate_bias, fc1_w, fc2_w, w1, w2, shared_up_w, shared_down_w):
        import jax, jax.numpy as jnp
        import numpy as np
        H, LAT, INTER, E, G, TOPK_G, TOP_K = (256, 128, 128, 32, 4, 2, 8)
        SHARED_INTER = 512
        ROUTED_SCALE = 2.5
        B, S = (2, 128)

        def relu2(x):
            return jnp.square(jax.nn.relu(x))
        orig_shape = hidden_states.shape
        x = hidden_states.reshape(-1, H)
        T = x.shape[0]
        logits = jnp.einsum('th,eh->te', x.astype(jnp.float32), gate_w)
        scores = jax.nn.sigmoid(logits)
        sb = scores + gate_bias
        grp = sb.reshape(T, G, E // G)
        group_scores = jax.lax.top_k(grp, 2)[0].sum(-1)
        _, gidx = jax.lax.top_k(group_scores, TOPK_G)
        gmask = jax.nn.one_hot(gidx, G, dtype=sb.dtype).sum(1)
        masked = jnp.where(gmask[:, :, None] > 0, grp, -jnp.inf).reshape(T, E)
        _, topi = jax.lax.top_k(masked, TOP_K)
        wsel = jnp.take_along_axis(scores, topi, axis=1)
        wsel = wsel / wsel.sum(-1, keepdims=True) * ROUTED_SCALE
        cw = jnp.zeros((T, E), jnp.float32).at[jnp.arange(T)[:, None], topi].add(wsel)
        x_lat = x @ fc1_w.T
        h = relu2(jnp.einsum('tl,eil->eti', x_lat, w1))
        h = h * cw.T[:, :, None]
        y_lat = jnp.einsum('eti,eli->tl', h, w2)
        routed = y_lat @ fc2_w.T
        shared = relu2(x @ shared_up_w.T) @ shared_down_w.T
        return (shared + routed).reshape(orig_shape)

    def _L1_attn_ref(hidden_states, slope_rate, w_qkv, w_gate, w_out, rms_weight):
        import jax, jax.numpy as jnp
        import numpy as np
        B, N, HID, H, D = (2, 1024, 256, 16, 128)
        BLOCK = 32
        EPS = 1e-06

        def _alibi_slopes(h):
            start = 2.0 ** (-2.0 ** (-(np.log2(h) - 3)))
            return np.array([start * start ** i for i in range(h)], dtype=np.float32)

        def _lightning_attention(q, k, v, slope_rate):
            b, h, n, d = q.shape
            nb = n // BLOCK
            s = slope_rate.reshape(1, h, 1, 1).astype(q.dtype)
            arr = jnp.arange(1, BLOCK + 1, dtype=q.dtype)
            q_decay = jnp.exp(-s * arr[None, None, :, None])
            k_decay = jnp.exp(-s * (BLOCK - arr)[None, None, :, None])
            idx = arr[:, None] - arr[None, :]
            diag_decay = jnp.where(idx[None, None] >= 0, jnp.exp(-s * idx[None, None]), 0.0)
            block_decay = jnp.exp(-s * BLOCK)

            def to_blocks(x):
                return x.reshape(b, h, nb, BLOCK, d).transpose(2, 0, 1, 3, 4)
            qb, kb, vb = (to_blocks(q), to_blocks(k), to_blocks(v))

            def step(kv, blk):
                qi, ki, vi = blk
                inter = jnp.einsum('bhld,bhde->bhle', qi * q_decay, kv)
                qk = jnp.einsum('bhld,bhmd->bhlm', qi, ki) * diag_decay
                intra = jnp.einsum('bhlm,bhme->bhle', qk, vi)
                kv = block_decay * kv + jnp.einsum('bhld,bhle->bhde', ki * k_decay, vi)
                return (kv, inter + intra)
            kv0 = jnp.zeros((b, h, d, d), q.dtype)
            _, out = jax.lax.scan(step, kv0, (qb, kb, vb))
            return out.transpose(1, 2, 0, 3, 4).reshape(b, h, n, d)
        b, n, _ = hidden_states.shape
        qkv = jax.nn.silu(hidden_states @ w_qkv)
        q, k, v = jnp.split(qkv, 3, axis=-1)

        def shp(x):
            return x.reshape(b, n, H, D).transpose(0, 2, 1, 3)
        o = _lightning_attention(shp(q), shp(k), shp(v), slope_rate)
        o = o.transpose(0, 2, 1, 3).reshape(b, n, H * D)
        var = jnp.mean(jnp.square(o), axis=-1, keepdims=True)
        o = o * jax.lax.rsqrt(var + EPS) * rms_weight
        o = jax.nn.sigmoid(hidden_states @ w_gate) * o
        return o @ w_out

    def _L1_ffn_ref(hidden_states, gate_weight, gate_up_proj, down_proj, old_to_new):
        import jax, jax.numpy as jnp
        import numpy as np
        NUM_EXPERTS = 128
        NUM_KEPT = 48
        TOP_K = 8
        HIDDEN = 256
        INTER = 96
        CAP = 96
        BATCH, SEQ = (2, 128)
        B, S, H = hidden_states.shape
        x = hidden_states.reshape(-1, H)
        T = x.shape[0]
        logits = x @ gate_weight.T
        logits = jnp.where(old_to_new[None, :] == -1, -jnp.inf, logits)
        probs = jax.nn.softmax(logits.astype(jnp.float32), axis=-1).astype(logits.dtype)
        top_v, top_i = jax.lax.top_k(probs, TOP_K)
        top_v = top_v / jnp.sum(top_v, axis=-1, keepdims=True)
        sel_new = old_to_new[top_i]
        E = gate_up_proj.shape[0]
        flat_e = sel_new.reshape(-1)
        flat_w = top_v.reshape(-1)
        tok = jnp.repeat(jnp.arange(T), TOP_K)
        oh = (flat_e[:, None] == jnp.arange(E)[None, :]).astype(jnp.int32)
        pos = jnp.sum(jnp.cumsum(oh, axis=0) * oh, axis=-1) - 1
        valid = pos < CAP
        pos_c = jnp.where(valid, pos, CAP)
        xb = jnp.zeros((E, CAP + 1, H), x.dtype).at[flat_e, pos_c].set(x[tok])
        xb = xb[:, :CAP]
        gu = jnp.einsum('ech,eoh->eco', xb, gate_up_proj)
        g, u = jnp.split(gu, 2, axis=-1)
        h = jax.nn.silu(g) * u
        out = jnp.einsum('eci,ehi->ech', h, down_proj)
        y = out[flat_e, jnp.minimum(pos_c, CAP - 1)]
        w = flat_w * valid.astype(flat_w.dtype)
        final = jnp.zeros_like(x).at[tok].add(y * w[:, None])
        return final.reshape(B, S, H)
    x = L0_attn_x
    x = x + _L0_attn_ref(_layernorm(x, axis=-1), L0_attn_W_Q, L0_attn_W_K, L0_attn_W_V, L0_attn_W_O)
    x = x + _L0_ffn_ref(_layernorm(x, axis=-1), L0_ffn_gate_w, L0_ffn_gate_bias, L0_ffn_fc1_w, L0_ffn_fc2_w, L0_ffn_w1, L0_ffn_w2, L0_ffn_shared_up_w, L0_ffn_shared_down_w)
    x = x + _L1_attn_ref(_layernorm(x, axis=-1), L1_attn_slope_rate, L1_attn_w_qkv, L1_attn_w_gate, L1_attn_w_out, L1_attn_rms_weight)
    x = x + _L1_ffn_ref(_layernorm(x, axis=-1), L1_ffn_gate_weight, L1_ffn_gate_up_proj, L1_ffn_down_proj, L1_ffn_old_to_new)
    return x

_drawn_inputs = setup_inputs


def setup_inputs(seed=0):
    import zlib

    import numpy as np

    out = dict(_drawn_inputs(seed))
    spreads = {'L1_attn_rms_weight': (1.0, 0.6)}
    factors = {'L0_ffn_gate_w': 8.0,
     'L0_ffn_gate_bias': 8.0,
     'L0_ffn_fc1_w': 8.0,
     'L0_ffn_fc2_w': 8.0,
     'L0_ffn_w1': 8.0,
     'L0_ffn_w2': 8.0,
     'L1_ffn_gate_weight': 25.812,
     'L1_ffn_gate_up_proj': 25.784,
     'L1_ffn_down_proj': 25.719,
     'L0_ffn_shared_up_w': 8.0,
     'L0_ffn_shared_down_w': 8.0,
     'L1_attn_slope_rate': 8.0,
     'L1_attn_w_qkv': 8.0,
     'L1_attn_w_gate': 8.0,
     'L1_attn_w_out': 8.0}
    for name, (base, spread) in spreads.items():
        noise = np.random.default_rng([zlib.crc32(name.encode()), seed]).standard_normal(out[name].shape)
        drawn = base * np.exp(spread * noise) if base else spread * noise
        out[name] = jnp.asarray(drawn.astype(out[name].dtype))
    for name, factor in factors.items():
        out[name] = (out[name] * factor).astype(out[name].dtype)
    return out
```

```python
from contextlib import ExitStack

import concourse.bass as bass
from concourse import mybir

F32 = mybir.dt.float32
F32R = mybir.dt.float32r
BF16 = mybir.dt.bfloat16
U32 = mybir.dt.uint32
I32 = mybir.dt.int32
ALU = mybir.AluOpType
ACT = mybir.ActivationFunctionType
AX = mybir.AxisListType

P = 128
D = 256
KD = D // P
BATCH, SEQ = 4, 1024
T = BATCH * SEQ
TILES = T // P
CHUNK = 512
CHUNKS = T // CHUNK
TPC = CHUNK // P
NEG = -1.0e30

CREDIT = 2


def done(step):
    return step + 1 + CREDIT


class Phase:

    def __init__(self, nc, name):
        self.nc, self.name, self.ctx = nc, name, ExitStack()
        self.owned = []

    def __enter__(self):
        return self

    def __exit__(self, *exc):
        self.ctx.close()
        self.nc.clear_and_free_semaphores(self.owned)
        self.nc.all_engine_barrier()

    def sb(self, name, shape, dt=F32):
        return self.ctx.enter_context(self.nc.sbuf_tensor(f"{self.name}_{name}", shape, dt))

    def ps(self, name, shape, dt=F32):
        return self.ctx.enter_context(self.nc.psum_tensor(f"{self.name}_{name}", shape, dt))

    def sem(self, name):
        self.owned.append(self.nc.alloc_semaphore(f"{self.name}_{name}"))
        return self.owned[-1]

    def sems(self, names):
        return [self.sem(n) for n in names.split()]

    def block(self):
        return self.ctx.enter_context(self.nc.Block())


def give_credit(eng, *sems):
    for s in sems:
        eng.sem_inc(s, CREDIT)


def constants_phase(nc, x, X, ident, identb, mask_q, mask_k):
    with Phase(nc, "const") as ph:
        x_in, pool_set, pool_sel, f_ready = ph.sems("x_in pool_set pool_sel ident_ready")
        block = ph.block()

        @block.sync
        def _(sp):
            src = x.rearrange("(t p) n -> p t n", p=P)
            for g in range(4):
                sp.dma_start(X[:, 8 * g:8 * g + 8, :], src[:, 8 * g:8 * g + 8, :]).then_inc(x_in, 16)
            sp.wait_ge(x_in, 64)

        @block.gpsimd
        def _(pool):
            nc.gpsimd.memset(ident[:], 0.0).then_inc(pool_set, 1)
            nc.gpsimd.memset(mask_q[:], 0.0).then_inc(pool_set, 1)
            nc.gpsimd.memset(mask_k[:], 0.0).then_inc(pool_set, 1)
            pool.wait_ge(pool_set, 3)
            nc.gpsimd.affine_select(out=ident[:], in_=ident[:], compare_op=ALU.not_equal, fill=1.0, base=0,
                                    pattern=[[-1, P]], channel_multiplier=1).then_inc(f_ready, 1)
            nc.gpsimd.affine_select(out=mask_q[:], in_=mask_q[:], compare_op=ALU.is_ge, fill=NEG, base=0,
                                    pattern=[[-1, P]], channel_multiplier=1).then_inc(pool_sel, 1)
            nc.gpsimd.affine_select(out=mask_k[:], in_=mask_k[:], compare_op=ALU.is_ge, fill=NEG, base=0,
                                    pattern=[[1, P]], channel_multiplier=-1).then_inc(pool_sel, 1)

        @block.vector
        def _(dve):
            dve.wait_ge(f_ready, 1)
            nc.vector.tensor_copy(identb[:], ident[:])


def transpose_phase(nc, name, SRC, XH, XL, ident, norm, normed=None):
    with Phase(nc, name) as ph:
        stats = ph.sb("stats", [P, TILES, 6])
        mv = ph.sb("mv", [P, TILES, 2])
        std = ph.sb("std", [P, TILES])
        rstd = ph.sb("rstd", [P, TILES])
        rows = ph.sb("rows", [P, 2, TPC, D])
        tr = ph.ps("tr", [P, 2, KD, CHUNK])
        (stats_ready, mv_ready, var_ready, std_ready, rstd_ready, rows_ready, transposed, high_ready,
         low_ready, stored0, stored1) = ph.sems("stats_ready mv_ready var_ready std_ready rstd_ready rows_ready "
                                                "transposed high_ready low_ready stored0 stored1")
        block = ph.block()

        @block.vector
        def _(dve):
            if norm:
                for t in range(TILES):
                    nc.vector.bn_stats(stats[:, t, :], SRC[:, t, :]).then_inc(stats_ready, 1)
                dve.wait_ge(stats_ready, TILES)
                for t in range(TILES):
                    nc.vector.bn_aggr(mv[:, t, :], stats[:, t, :]).then_inc(mv_ready, 1)
                dve.wait_ge(mv_ready, TILES)
                nc.vector.tensor_scalar(std[:], mv[:, :, 1], 1.0e-5, None, ALU.add).then_inc(var_ready, 1)
                dve.wait_ge(std_ready, 1)
                nc.vector.reciprocal(rstd[:], std[:]).then_inc(rstd_ready, 1)
                dve.wait_ge(rstd_ready, 1)
            give_credit(dve, rows_ready, low_ready)

            def make_rows(i, u):
                g = i * 2 + u
                dve.wait_ge(transposed, done(g - 2))
                if normed is not None:
                    dve.wait_ge((stored0, stored1)[u], (i + 1) * 16)
                for j in range(TPC):
                    if norm:
                        t = g * TPC + j
                        ins = nc.vector.tensor_scalar(rows[:, u, j, :], SRC[:, bass.ds(t, 1), :],
                                                      mv[:, bass.ds(t, 1), 0], rstd[:, bass.ds(t, 1)],
                                                      ALU.subtract, ALU.mult)
                    else:
                        ins = nc.vector.tensor_scalar(rows[:, u, j, :], SRC[:, bass.ds(g * TPC + j, 1), :],
                                                      1.0, None, ALU.mult)
                ins.then_inc(rows_ready, 1)

            def make_low(g, u):
                dve.wait_ge(high_ready, done(g))
                nc.vector.tensor_tensor(XL[:, :, bass.ds(g * CHUNK, CHUNK)], tr[:, u],
                                        XH[:, :, bass.ds(g * CHUNK, CHUNK)].bitcast(F32),
                                        ALU.subtract).then_inc(low_ready, 1)

            with dve.Fori(0, CHUNKS // 2) as i:
                for u in range(2):
                    make_rows(i, u)
                for u in range(2):
                    make_low(i * 2 + u, u)

        @block.tensor
        def _(pe):
            give_credit(pe, transposed)
            with pe.Fori(0, CHUNKS // 2) as i:
                for u in range(2):
                    g = i * 2 + u
                    pe.wait_ge(rows_ready, done(g))
                    pe.wait_ge(low_ready, done(g - 2))
                    for k in range(KD):
                        for j in range(TPC):
                            ins = nc.tensor.transpose(tr[:, u, k, j * P:(j + 1) * P],
                                                      rows[:, u, j, k * P:(k + 1) * P], ident[:])
                    ins.then_inc(transposed, 1)

        @block.scalar
        def _(act):
            if norm:
                act.wait_ge(var_ready, 1)
                nc.scalar.activation(std[:], std[:], ACT.Sqrt).then_inc(std_ready, 1)
            give_credit(act, high_ready)
            with act.Fori(0, CHUNKS // 2) as i:
                for u in range(2):
                    g = i * 2 + u
                    act.wait_ge(transposed, done(g))
                    act.wait_ge(high_ready, CREDIT)
                    nc.scalar.activation(XH[:, :, bass.ds(g * CHUNK, CHUNK)], tr[:, u], ACT.Copy)\
                        .then_inc(high_ready, 1)

        @block.sync
        def _(sp):
            if normed is None:
                return
            sp.sem_inc(stored0, 16)
            sp.sem_inc(stored1, 16)
            with sp.Fori(0, CHUNKS // 2) as i:
                for u in range(2):
                    g = i * 2 + u
                    sp.wait_ge(rows_ready, done(g))
                    sp.dma_start(normed[bass.ds(g * CHUNK, CHUNK), 0:D].rearrange("(t p) n -> p t n", p=P),
                                 rows[:, u]).then_inc((stored0, stored1)[u], 16)
            sp.wait_ge(stored0, 16 * (CHUNKS // 2 + 1))
            sp.wait_ge(stored1, 16 * (CHUNKS // 2 + 1))
AH, AD = 16, 16
HG = 4
UNITS = BATCH * AH // HG
TERMS = 3
QK_TERMS = ((0, 0), (0, 1), (1, 0), (1, 1), (0, 2), (2, 0))
ROWS_QK = len(QK_TERMS) * AD
ROWS_ALL = ROWS_QK + TERMS
VW = 32


def qkv_phase(nc, a, XH, XL, q_parts, k_parts, v_rows):
    with Phase(nc, "qkv") as ph:
        names = ("Q", "K", "V")
        raw = ph.sb("raw", [P, KD, 3, D])
        WH = ph.sb("WH", [P, KD, 3, D], F32R)
        WL = ph.sb("WL", [P, KD, 3, D], F32R)
        parts = ph.sb("parts", [P, 2, TERMS, CHUNK], BF16)
        rest = ph.sb("rest", [P, 2, CHUNK])
        vt = ph.sb("vt", [P, 2, AH, VW])
        PQ = ph.ps("PQ", [P, 2, CHUNK])
        PV = ph.ps("PV", [P, 2, 512])
        (w_in, wh_ready, wl_ready, projected, high, rest1, mid, low, stored, v_set, v_proj, v_copied,
         v_stored0, v_stored1, stored1) = ph.sems("w_in wh_ready wl_ready projected high rest1 mid low stored "
                                                  "v_set v_proj v_copied v_stored0 v_stored1 stored1")
        stored = (stored, stored1)
        v_stored = (v_stored0, v_stored1)
        block = ph.block()
        RUNS = [(w, m) for w in range(2) for m in range(2)]

        @block.sync
        def _(sp):
            for n, w in enumerate(names):
                sp.dma_start(raw[:, :, n, :], a[f"L0_attn_W_{w}"].rearrange("(k p) n -> p k n", p=P)).then_inc(w_in, 16)
            for s in stored:
                sp.sem_inc(s, 16)
            for r, (w, m) in enumerate(RUNS):
                dst = (q_parts, k_parts)[w]
                with sp.Fori(0, CHUNKS // 2) as i:
                    for u in range(2):
                        g = i * 2 + u
                        sp.wait_ge(low, done(g + r * CHUNKS))
                        sp.dma_start(dst[:, m * P:(m + 1) * P, bass.ds(g * CHUNK, CHUNK)]
                                     .rearrange("t p n -> p t n"), parts[:, u]).then_inc(stored[u], 16)
            for t in range(TILES):
                u = t % 2
                sp.wait_ge(v_copied, t + 1)
                sp.dma_start(v_rows[:, t * P:(t + 1) * P, :].rearrange("g p n -> p g n"),
                             vt[:, u].rearrange("p (g h) d -> p g (h d)", g=AH // HG)).then_inc(v_stored[u], 16)
            for u in range(2):
                sp.wait_ge(stored[u], 16 * (1 + len(RUNS) * CHUNKS // 2))
                sp.wait_ge(v_stored[u], 16 * TILES // 2)

        @block.scalar
        def _(act):
            act.wait_ge(w_in, 48)
            nc.scalar.activation(WH[:], raw[:], ACT.Copy).then_inc(wh_ready, 1)
            give_credit(act, high, mid)
            for r in range(len(RUNS)):
                with act.Fori(0, CHUNKS // 2) as i:
                    for u in range(2):
                        n = i * 2 + u + r * CHUNKS
                        act.wait_ge(stored[u], (i + r * CHUNKS // 2 + 1) * 16)
                        act.wait_ge(projected, done(n))
                        nc.scalar.activation(parts[:, u, 0], PQ[:, u], ACT.Copy).then_inc(high, 1)
                        act.wait_ge(rest1, done(n))
                        nc.scalar.activation(parts[:, u, 1], rest[:, u], ACT.Copy).then_inc(mid, 1)
            act.wait_ge(v_set, 2)
            for t in range(TILES):
                u = t % 2
                act.wait_ge(v_proj, t + 1)
                if t >= 2:
                    act.wait_ge(v_stored[u], 16 * (t // 2))
                nc.scalar.activation(vt[:, u, :, 0:AD], PV[:, u, 0:D].rearrange("p (h d) -> p h d", d=AD), ACT.Copy)\
                    .then_inc(v_copied, 1)

        @block.vector
        def _(dve):
            dve.wait_ge(wh_ready, 1)
            nc.vector.tensor_tensor(WL[:], raw[:], WH[:].bitcast(F32), ALU.subtract).then_inc(wl_ready, 1)
            nc.vector.memset(vt[:], 0.0).then_inc(v_set, 1)
            dve.wait_ge(v_set, 1)
            nc.vector.memset(vt[:, :, :, AD:AD + 1], 1.0).then_inc(v_set, 1)
            give_credit(dve, rest1, low)
            for r in range(len(RUNS)):
                with dve.Fori(0, CHUNKS // 2) as i:
                    for u in range(2):
                        n = i * 2 + u + r * CHUNKS
                        dve.wait_ge(high, done(n))
                        nc.vector.tensor_tensor(rest[:, u], PQ[:, u], parts[:, u, 0], ALU.subtract).then_inc(rest1, 1)
                        dve.wait_ge(mid, done(n))
                        nc.vector.tensor_tensor(parts[:, u, 2], rest[:, u], parts[:, u, 1], ALU.subtract)\
                            .then_inc(low, 1)

        @block.tensor
        def _(pe):
            pe.wait_ge(wl_ready, 1)
            give_credit(pe, projected)
            for r, (w, m) in enumerate(RUNS):
                with pe.Fori(0, CHUNKS // 2) as i:
                    for u in range(2):
                        g = i * 2 + u
                        pe.wait_ge(low, done(g + r * CHUNKS - 2))
                        s = 0
                        for W, x in ((WH, XH), (WH, XL), (WL, XH)):
                            for k in range(KD):
                                ins = nc.tensor.matmul(PQ[:, u], W[:, k, w, m * P:(m + 1) * P],
                                                       x[:, k, bass.ds(g * CHUNK, CHUNK)],
                                                       start=(s == 0), stop=(s == 3 * KD - 1))
                                s += 1
                        ins.then_inc(projected, 1)
            for t in range(TILES):
                u = t % 2
                if t >= 2:
                    pe.wait_ge(v_copied, t - 1)
                s = 0
                for x, W in ((XH, WH), (XL, WH), (XH, WL)):
                    for k in range(KD):
                        ins = nc.tensor.matmul(PV[:, u, 0:D], x[:, k, t * P:(t + 1) * P], W[:, k, 2, :],
                                               start=(s == 0), stop=(s == 3 * KD - 1))
                        s += 1
                ins.then_inc(v_proj, 1)


def score_phase(nc, q_parts, k_parts, v_rows, max_rows, AO, ident, identb, mask_q, mask_k):
    QT = SEQ // P
    SCALE = 1.0 / float(AD) ** 0.5
    PIECES = [(t, k0, min(CHUNK, (t + 1) * P - k0)) for t in range(QT) for k0 in range(0, (t + 1) * P, CHUNK)]
    GROUPS = ([[0], [1, 3], [2]], [[0, 1], [2, 3], [4, 5, 7], [6]])

    def span(half, kt):
        q0 = max(0, kt * P - half * CHUNK)
        return q0, CHUNK - q0

    def layout(half, group):
        at, out = 0, []
        for kt in group:
            q0, n = span(half, kt)
            if at % CHUNK and at % CHUNK + n > CHUNK:
                at = (at // CHUNK + 1) * CHUNK
            out.append((kt, q0, n, at))
            at += n
        return out, at

    STEPS = [(half, g) for half in range(2) for g in range(len(GROUPS[half]))]
    NS = len(STEPS) * HG
    NP = len(PIECES) * HG
    PER = -(-NP // NS)
    OUT_AT = PER * HG * (len(GROUPS[0]) + 2) - 1
    with Phase(nc, "score") as ph:
        QR = ph.sb("QR", [P, 2, HG, SEQ], BF16)
        KR = ph.sb("KR", [P, 2, HG, SEQ], BF16)
        V = ph.sb("V", [P, 2, QT, HG, VW])
        pm = ph.sb("pm", [P, HG, QT, 2])
        mx = ph.sb("mx", [P, QT, HG])
        mrest = ph.sb("mrest", [P, QT, HG])
        mparts = ph.sb("mparts", [P, QT, TERMS, HG], BF16)
        mrow = ph.sb("mrow", [TERMS * HG, SEQ], BF16)
        PR = ph.sb("PR", [P, 2, HG, 2 * CHUNK])
        OS = ph.sb("OS", [P, CHUNK])
        rc = ph.sb("rc", [P, TPC, HG, 1])
        SM = ph.ps("SM", [P, 2, CHUNK])
        SE = ph.ps("SE", [P, 2, 2 * CHUNK])
        PV = ph.ps("PV", [P, CHUNK])
        TR = ph.ps("TR", [P, CHUNK])
        TRB = TR[:].bitcast(BF16)
        (in0, in1, ones_set, pe_m, dve_m, pm_done, mx_done, mh, mr1, mm, ml, m_tr, m_row, m_out, m_in0, m_in1,
         pe_s, act_p, pe_pv, act_o, pe_ot, dve_rc, dve_o) = ph.sems(
            "in0 in1 ones_set pe_m dve_m pm_done mx_done mh mr1 mm ml m_tr m_row m_out m_in0 m_in1 "
            "pe_s act_p pe_pv act_o pe_ot dve_rc dve_o")
        loaded = (in0, in1)
        m_in = (m_in0, m_in1)
        NLOAD = 2 * len(QK_TERMS) + 1
        block = ph.block()

        @block.sync
        def _(sp):
            sp.sem_inc(in0, 16)
            sp.sem_inc(in1, 16)
            sp.sem_inc(m_out, 16)

            def load(n, u):
                b, hg = n // (AH // HG), n % (AH // HG)
                for j, (tq, tk) in enumerate(QK_TERMS):
                    for parts, t, dst in ((q_parts, tq, QR), (k_parts, tk, KR)):
                        src = parts[t, bass.ds(hg * HG * AD, HG * AD), bass.ds(b * SEQ, SEQ)]
                        sp.dma_start(dst[j * AD:(j + 1) * AD, u], src.rearrange("(h d) n -> d h n", d=AD))\
                            .then_inc(loaded[u], 16)
                sp.dma_start(V[:, u].rearrange("p t h d -> p t (h d)"),
                             v_rows[bass.ds(hg, 1), bass.ds(b * SEQ, SEQ), :].rearrange("o (t p) n -> p (o t) n", p=P))\
                    .then_inc(loaded[u], 16)

            def maxima(n, u):
                sp.wait_ge(m_row, done(n))
                sp.dma_start(max_rows, mrow[:]).then_inc(m_out, 16)
                sp.wait_ge(m_out, (n + 2) * 16)
                sp.dma_start(QR[ROWS_QK:ROWS_ALL, u], max_rows.rearrange("(t h) n -> t h n", t=TERMS))\
                    .then_inc(m_in[u], 16)

            load(0, 0)
            maxima(0, 0)
            with sp.Fori(0, UNITS // 2) as i:
                for u in range(2):
                    n = i * 2 + u
                    sp.wait_ge(pe_pv, done(n * len(STEPS) - 1))
                    load((n + 1) % UNITS, 1 - u)
                    maxima(n + 1, 1 - u)
            sp.wait_ge(m_in0, 16 * (UNITS // 2 + 1))

        @block.gpsimd
        def _(pool):
            nc.gpsimd.memset(KR[ROWS_QK:P], 1.0).then_inc(ones_set, 1)

        def score_columns(pe_out, lhs, rhs, rows, diagonal, mask):
            ins = nc.tensor.matmul(pe_out, lhs, rhs, start=True, stop=diagonal is None)
            if diagonal is not None:
                ins = nc.tensor.matmul(diagonal, identb[:], mask[:], start=False, stop=True)
            return ins

        @block.tensor
        def _(pe):
            give_credit(pe, pe_m, m_tr, pe_s, pe_pv, pe_ot)
            from_rows = ROWS_QK

            def max_piece(n, u, p):
                h, (t, k0, nk) = p // len(PIECES), PIECES[p % len(PIECES)]
                bank = p % 2
                pe.wait_ge(dve_m, done(n * NP + p - 2))
                diag = SM[:, bank, nk - P:nk] if k0 + nk == (t + 1) * P else None
                score_columns(SM[:, bank, 0:nk], QR[0:from_rows, u, h, t * P:(t + 1) * P],
                              KR[0:from_rows, u, h, k0:k0 + nk], from_rows, diag, mask_q).then_inc(pe_m, 1)

            def max_rows_out(n):
                pe.wait_ge(ml, done(n))
                pe.wait_ge(dve_o, done(2 * n - 3))
                for t in range(QT):
                    ins = nc.tensor.transpose(TRB[0:TERMS * HG, t * P:(t + 1) * P],
                                              mparts[:, t].rearrange("p a h -> p (a h)"), identb[:])
                ins.then_inc(m_tr, 1)

            def scores(n, u, s, h):
                half, g = STEPS[s]
                e = s * HG + h
                pe.wait_ge(act_p, done(n * NS + e - 2))
                items, _ = layout(half, GROUPS[half][g])
                for kt, q0, nq, at in items:
                    q = half * CHUNK + q0
                    cols = SE[:, e % 2, at:at + nq]
                    diag = SE[:, e % 2, at:at + P] if q == kt * P else None
                    ins = score_columns(cols, KR[0:ROWS_ALL, u, h, kt * P:(kt + 1) * P],
                                        QR[0:ROWS_ALL, u, h, q:q + nq], ROWS_ALL, diag, mask_k)
                ins.then_inc(pe_s, 1)

            def values(n, u, s):
                half, g = STEPS[s]
                if g == 0:
                    pe.wait_ge(act_o, done(2 * n + half - 1))
                pe.wait_ge(act_p, done(n * NS + (s + 1) * HG - 1))
                items, _ = layout(half, GROUPS[half][g])
                last = g == len(GROUPS[half]) - 1
                for j, (kt, q0, nq, at) in enumerate(items):
                    for h in range(HG):
                        ins = nc.tensor.matmul(PV[VW * h:VW * (h + 1), q0:q0 + nq], V[:, u, kt, h, :],
                                               PR[:, s % 2, h, at:at + nq], start=(g == 0 and j == 0),
                                               stop=(last and j == len(items) - 1), skip_group_check=True)
                ins.then_inc(pe_pv, 1)

            def outputs(n, half):
                pe.wait_ge(act_o, done(2 * n + half))
                pe.wait_ge(dve_o, done(2 * n + half - 1))
                if half == 0:
                    pe.wait_ge(m_row, done(n))
                for t in range(TPC):
                    ins = nc.tensor.transpose(TR[:, t * P:(t + 1) * P], OS[:, t * P:(t + 1) * P], ident[:])
                ins.then_inc(pe_ot, 1)

            pe.wait_ge(in0, 16 * (NLOAD + 1))
            pe.wait_ge(ones_set, 1)
            for p in range(NP):
                h, (t, k0, nk) = p // len(PIECES), PIECES[p % len(PIECES)]
                max_piece(0, 0, p)
            pe.wait_ge(ml, done(0))
            for t in range(QT):
                ins = nc.tensor.transpose(TRB[0:TERMS * HG, t * P:(t + 1) * P],
                                          mparts[:, t].rearrange("p a h -> p (a h)"), identb[:])
            ins.then_inc(m_tr, 1)
            with pe.Fori(0, UNITS // 2) as i:
                for u in range(2):
                    n = i * 2 + u
                    pe.wait_ge(loaded[1 - u], (i + 1 + u) * (16 * NLOAD) + 16)
                    pe.wait_ge(m_in[u], (i + 1) * 16)
                    p = 0
                    for s in range(len(STEPS)):
                        for h in range(HG):
                            scores(n, u, s, h)
                            for _ in range(PER):
                                if p < NP:
                                    max_piece(n + 1, 1 - u, p)
                                    p += 1
                        if s >= 1:
                            values(n, u, s - 1)
                        if s == len(GROUPS[0]) + 1:
                            outputs(n, 0)
                    values(n, u, len(STEPS) - 1)
                    pe.wait_ge(ml, done(n + 1))
                    pe.wait_ge(dve_o, done(2 * n))
                    for t in range(QT):
                        ins = nc.tensor.transpose(TRB[0:TERMS * HG, t * P:(t + 1) * P],
                                                  mparts[:, t].rearrange("p a h -> p (a h)"), identb[:])
                    ins.then_inc(m_tr, 1)
                    pe.wait_ge(m_row, done(n + 1))
                    pe.wait_ge(act_o, done(2 * n + 1))
                    for t in range(TPC):
                        ins = nc.tensor.transpose(TR[:, t * P:(t + 1) * P], OS[:, t * P:(t + 1) * P], ident[:])
                    ins.then_inc(pe_ot, 1)

        @block.scalar
        def _(act):
            act.preload_act_table(ACT.Exp)
            give_credit(act, act_p, act_o, mh, mm, m_row)

            def exps(n, s, h):
                half, g = STEPS[s]
                e = s * HG + h
                items, width = layout(half, GROUPS[half][g])
                act.wait_ge(pe_pv, done(n * len(STEPS) + s - 2))
                act.wait_ge(pe_s, done(n * NS + e))
                nc.scalar.activation(PR[:, s % 2, h, 0:width], SE[:, e % 2, 0:width], ACT.Exp, scale=SCALE)\
                    .then_inc(act_p, 1)

            def copy_out(n, half):
                act.wait_ge(pe_ot, done(2 * n + half - 1))
                act.wait_ge(pe_pv, done(n * len(STEPS) + (len(GROUPS[0]) if half == 0 else len(STEPS)) - 1))
                nc.scalar.activation(OS[:], PV[:], ACT.Copy).then_inc(act_o, 1)

            def max_parts(n):
                act.wait_ge(mx_done, done(n))
                nc.scalar.activation(mparts[:, :, 0, :], mx[:], ACT.Copy).then_inc(mh, 1)
                act.wait_ge(mr1, done(n))
                nc.scalar.activation(mparts[:, :, 1, :], mrest[:], ACT.Copy).then_inc(mm, 1)

            def max_row(n):
                act.wait_ge(m_tr, done(n))
                act.wait_ge(m_out, (n + 1) * 16)
                nc.scalar.activation(mrow[:], TRB[0:TERMS * HG, :], ACT.Copy).then_inc(m_row, 1)

            max_parts(0)
            max_row(0)
            with act.Fori(0, UNITS // 2) as i:
                for u in range(2):
                    n = i * 2 + u
                    for s in range(len(STEPS)):
                        for h in range(HG):
                            exps(n, s, h)
                        if s == len(GROUPS[0]):
                            copy_out(n, 0)
                    max_parts(n + 1)
                    copy_out(n, 1)
                    max_row(n + 1)

        @block.vector
        def _(dve):
            give_credit(dve, dve_m, mx_done, mr1, ml, dve_rc, dve_o, pm_done)

            def max_piece(n, p):
                h, (t, k0, nk) = p // len(PIECES), PIECES[p % len(PIECES)]
                dve.wait_ge(pe_m, done(n * NP + p))
                nc.vector.tensor_reduce(pm[:, h, t, k0 // CHUNK:k0 // CHUNK + 1], SM[:, p % 2, 0:nk], AX.X, ALU.max)\
                    .then_inc(dve_m, 1)

            def finish_max(n):
                dve.wait_ge(dve_m, done((n + 1) * NP - 1))
                nc.vector.tensor_tensor(pm[:, :, QT // 2:QT, 0], pm[:, :, QT // 2:QT, 0], pm[:, :, QT // 2:QT, 1],
                                        ALU.max).then_inc(pm_done, 1)
                dve.wait_ge(pm_done, done(n))
                nc.vector.tensor_scalar(mx[:], pm[:, :, :, 0].rearrange("p h t -> p t h"), -1.0, None, ALU.mult)\
                    .then_inc(mx_done, 1)
                dve.wait_ge(mh, done(n))
                nc.vector.tensor_tensor(mrest[:], mx[:], mparts[:, :, 0, :], ALU.subtract).then_inc(mr1, 1)
                dve.wait_ge(mm, done(n))
                nc.vector.tensor_tensor(mparts[:, :, 2, :], mrest[:], mparts[:, :, 1, :], ALU.subtract)\
                    .then_inc(ml, 1)

            def normalise(n, half):
                tr = TR[:].rearrange("p (t h d) -> p t h d", t=TPC, h=HG)
                dve.wait_ge(pe_ot, done(2 * n + half))
                nc.vector.reciprocal(rc[:], tr[:, :, :, AD:AD + 1]).then_inc(dve_rc, 1)
                dve.wait_ge(dve_rc, done(2 * n + half))
                for t in range(TPC):
                    b, hg = n // (AH // HG), n % (AH // HG)
                    dst = AO[:, bass.ds(b * QT + half * TPC + t, 1), bass.ds(hg * HG * AD, HG * AD)]
                    ins = nc.vector.tensor_tensor(dst.rearrange("p o (h d) -> p (o h) d", d=AD), tr[:, t, :, 0:AD],
                                                  rc[:, t].to_broadcast([P, HG, AD]), ALU.mult)
                ins.then_inc(dve_o, 1)

            for p in range(NP):
                max_piece(0, p)
            finish_max(0)
            with dve.Fori(0, UNITS // 2) as i:
                for u in range(2):
                    n = i * 2 + u
                    for p in range(NP):
                        max_piece(n + 1, p)
                        if p == OUT_AT:
                            normalise(n, 0)
                    finish_max(n + 1)
                    normalise(n, 1)


def output_phase(nc, w_o, X, XH, XL):
    with Phase(nc, "proj") as ph:
        raw = ph.sb("raw", [P, KD, D])
        WH = ph.sb("WH", [P, KD, D], F32R)
        WL = ph.sb("WL", [P, KD, D], F32R)
        Y = ph.ps("Y", [P, 2, 512])
        w_in, wh_ready, wl_ready, made, added = ph.sems("w_in wh_ready wl_ready made added")
        block = ph.block()

        @block.sync
        def _(sp):
            sp.dma_start(raw[:], w_o.rearrange("(k p) n -> p k n", p=P)).then_inc(w_in, 16)

        @block.scalar
        def _(act):
            act.wait_ge(w_in, 16)
            nc.scalar.activation(WH[:], raw[:], ACT.Copy).then_inc(wh_ready, 1)

        @block.tensor
        def _(pe):
            pe.wait_ge(wl_ready, 1)
            for t in range(TILES):
                if t >= 2:
                    pe.wait_ge(added, t - 1)
                s = 0
                for x, W in ((XH, WH), (XL, WH), (XH, WL)):
                    for k in range(KD):
                        ins = nc.tensor.matmul(Y[:, t % 2, 0:D], x[:, k, t * P:(t + 1) * P], W[:, k, :],
                                               start=(s == 0), stop=(s == 3 * KD - 1))
                        s += 1
                ins.then_inc(made, 1)

        @block.vector
        def _(dve):
            dve.wait_ge(wh_ready, 1)
            nc.vector.tensor_tensor(WL[:], raw[:], WH[:].bitcast(F32), ALU.subtract).then_inc(wl_ready, 1)
            for t in range(TILES):
                dve.wait_ge(made, t + 1)
                nc.vector.tensor_tensor(X[:, t, :], Y[:, t % 2, 0:D], X[:, t, :], ALU.add).then_inc(added, 1)


def attention_layer(nc, a, X, ident, identb, mask_q, mask_k):
    q_parts = nc.dram_tensor("q_parts", (TERMS, D, T), BF16, kind="Internal").ap()
    k_parts = nc.dram_tensor("k_parts", (TERMS, D, T), BF16, kind="Internal").ap()
    v_rows = nc.dram_tensor("v_rows", (AH // HG, T, HG * VW), F32, kind="Internal").ap()
    max_rows = nc.dram_tensor("max_rows", (TERMS * HG, SEQ), BF16, kind="Internal").ap()
    with ExitStack() as c:
        XH = c.enter_context(nc.sbuf_tensor("A_XH", [P, KD, T], F32R))
        XL = c.enter_context(nc.sbuf_tensor("A_XL", [P, KD, T], F32R))
        transpose_phase(nc, "lnA", X, XH, XL, ident, True)
        qkv_phase(nc, a, XH, XL, q_parts, k_parts, v_rows)
    with ExitStack() as c:
        AO = c.enter_context(nc.sbuf_tensor("AO", [P, TILES, D], F32))
        score_phase(nc, q_parts, k_parts, v_rows, max_rows, AO, ident, identb, mask_q, mask_k)
        XH = c.enter_context(nc.sbuf_tensor("A2_XH", [P, KD, T], F32R))
        XL = c.enter_context(nc.sbuf_tensor("A2_XL", [P, KD, T], F32R))
        transpose_phase(nc, "trA", AO, XH, XL, ident, False)
        output_phase(nc, a["L0_attn_W_O"], X, XH, XL)
EXPERTS, LAT, INTER, SHARED = 32, 128, 128, 512
GROUPS_E, PER_GROUP, TOP_GROUPS, TOP_K = 4, 8, 2, 8
ROUTED_SCALE = 2.5
SB = SHARED // P
CWR = TERMS * EXPERTS


def shared_phase(nc, a, X, XH, XL, LH, LL, scores):
    NW = LAT + SHARED
    with Phase(nc, "shared") as ph:
        raw = ph.sb("raw", [P, KD, NW])
        WH = ph.sb("WH", [P, KD, NW], F32R)
        WL = ph.sb("WL", [P, KD, NW], F32R)
        graw = ph.sb("graw", [P, KD, EXPERTS])
        GH = ph.sb("GH", [P, KD, EXPERTS], F32R)
        GL = ph.sb("GL", [P, KD, EXPERTS], F32R)
        down = ph.sb("down", [P, SB, D])
        r = ph.sb("r", [P, 2, CHUNK])
        su = ph.sb("su", [P, SB, CHUNK])
        HP = ph.ps("HP", [P, 3, CHUNK])
        OP = ph.ps("OP", [P, 2, 512])
        LG = ph.ps("LG", [P, TILES, EXPERTS])
        (w_in, wh_ready, wl_ready, pe_l, pe_h, act_lh, dve_ll, act_r, act_su, pe_o, dve_x, pe_lg,
         act_lg) = ph.sems("w_in wh_ready wl_ready pe_l pe_h act_lh dve_ll act_r act_su pe_o dve_x pe_lg act_lg")
        block = ph.block()

        @block.sync
        def _(sp):
            sp.dma_start(raw[:, :, 0:LAT], a["L0_ffn_fc1_w"].rearrange("(k p) n -> p k n", p=P)).then_inc(w_in, 16)
            sp.dma_start(raw[:, :, LAT:NW], a["L0_ffn_shared_up_w"].rearrange("(k p) n -> p k n", p=P))\
                .then_inc(w_in, 16)
            sp.dma_start(graw[:], a["L0_ffn_gate_w"].rearrange("(k p) n -> p k n", p=P)).then_inc(w_in, 16)
            sp.dma_start(down[:], a["L0_ffn_shared_down_w"].rearrange("(s p) n -> p s n", p=P)).then_inc(w_in, 16)

        @block.scalar
        def _(act):
            act.wait_ge(w_in, 64)
            nc.scalar.activation(WH[:], raw[:], ACT.Copy).then_inc(wh_ready, 1)
            nc.scalar.activation(GH[:], graw[:], ACT.Copy).then_inc(wh_ready, 1)
            give_credit(act, act_lh, act_r, act_su)
            with act.Fori(0, CHUNKS) as g:
                act.wait_ge(pe_l, done(g))
                act.wait_ge(act_lh, CREDIT)
                nc.scalar.activation(LH[:, bass.ds(g * CHUNK, CHUNK)], HP[:, 2], ACT.Copy).then_inc(act_lh, 1)
                for s in range(SB):
                    n = g * SB + s
                    act.wait_ge(pe_h, done(n))
                    nc.scalar.activation(r[:, s % 2], HP[:, s % 2], ACT.Relu).then_inc(act_r, 1)
                    act.wait_ge(pe_o, done((g - 1) * TPC + TPC - 1))
                    act.wait_ge(act_r, done(n))
                    nc.scalar.activation(su[:, s], r[:, s % 2], ACT.Square).then_inc(act_su, 1)
            act.wait_ge(pe_lg, 1)
            nc.scalar.activation(scores[:], LG[:], ACT.Sigmoid).then_inc(act_lg, 1)

        @block.tensor
        def _(pe):
            pe.wait_ge(wl_ready, 2)
            give_credit(pe, pe_l, pe_h, pe_o)

            def first_product(bank, c0, g):
                n = 0
                for W, x in ((WH, XH), (WH, XL), (WL, XH)):
                    for k in range(KD):
                        ins = nc.tensor.matmul(HP[:, bank], W[:, k, c0:c0 + P], x[:, k, bass.ds(g * CHUNK, CHUNK)],
                                               start=(n == 0), stop=(n == 3 * KD - 1))
                        n += 1
                return ins

            with pe.Fori(0, CHUNKS) as g:
                pe.wait_ge(dve_ll, done(g - 1))
                first_product(2, 0, g).then_inc(pe_l, 1)
                for s in range(SB):
                    pe.wait_ge(act_r, done(g * SB + s - 2))
                    first_product(s % 2, LAT + s * P, g).then_inc(pe_h, 1)
                pe.wait_ge(act_su, done(g * SB + SB - 1))
                for t in range(TPC):
                    pe.wait_ge(dve_x, done(g * TPC + t - 2))
                    for s in range(SB):
                        ins = nc.tensor.matmul(OP[:, t % 2, 0:D], su[:, s, t * P:(t + 1) * P], down[:, s, :],
                                               start=(s == 0), stop=(s == SB - 1))
                    ins.then_inc(pe_o, 1)
            for t in range(TILES):
                n = 0
                for x, W in ((XH, GH), (XL, GH), (XH, GL)):
                    for k in range(KD):
                        ins = nc.tensor.matmul(LG[:, t, :], x[:, k, t * P:(t + 1) * P], W[:, k, :],
                                               start=(n == 0), stop=(n == 3 * KD - 1))
                        n += 1
            ins.then_inc(pe_lg, 1)

        @block.vector
        def _(dve):
            dve.wait_ge(wh_ready, 2)
            nc.vector.tensor_tensor(WL[:], raw[:], WH[:].bitcast(F32), ALU.subtract).then_inc(wl_ready, 1)
            nc.vector.tensor_tensor(GL[:], graw[:], GH[:].bitcast(F32), ALU.subtract).then_inc(wl_ready, 1)
            give_credit(dve, dve_ll, dve_x)
            with dve.Fori(0, CHUNKS) as g:
                cols = bass.ds(g * CHUNK, CHUNK)
                dve.wait_ge(act_lh, done(g))
                nc.vector.tensor_tensor(LL[:, cols], HP[:, 2], LH[:, cols].bitcast(F32), ALU.subtract)\
                    .then_inc(dve_ll, 1)
                for t in range(TPC):
                    dve.wait_ge(pe_o, done(g * TPC + t))
                    xt = X[:, bass.ds(g * TPC + t, 1), :]
                    nc.vector.tensor_tensor(xt, OP[:, t % 2:t % 2 + 1, 0:D], xt, ALU.add).then_inc(dve_x, 1)


def group_routing_phase(nc, bias, scores, CWT, identb):
    E, G, N = EXPERTS, GROUPS_E, PER_GROUP
    TAKEN = -3.0e38
    with Phase(nc, "route") as ph:
        bias_b = ph.sb("bias", [P, 1, E])
        sb_ = ph.sb("biased", [P, TILES, E])
        hi1 = ph.sb("hi1", [P, TILES * G, 4])
        lo1 = ph.sb("lo1", [P, TILES * G, 4])
        hi2 = ph.sb("hi2", [P, TILES * G, 2])
        lo2 = ph.sb("lo2", [P, TILES * G, 2])
        t2 = ph.sb("t2", [P, TILES * G, 2])
        u2 = ph.sb("u2", [P, TILES * G, 2])
        hi3 = ph.sb("hi3", [P, TILES * G, 1])
        lo3 = ph.sb("lo3", [P, TILES * G, 1])
        gs = ph.sb("gs", [P, TILES, G])
        beats = ph.sb("beats", [P, TILES, G, G - 1])
        rank = ph.sb("rank", [P, TILES, G])
        gm = ph.sb("gm", [P, TILES * G, 1])
        pen = ph.sb("pen", [P, TILES * G, 1])
        masked = ph.sb("masked", [P, TILES, E])
        top = ph.sb("top", [P, TILES, 8])
        left = ph.sb("left", [P, TILES, E])
        w = ph.sb("w", [P, TILES, E])
        total = ph.sb("total", [P, TILES, 1])
        rest = ph.sb("rest", [P, TILES, E])
        parts = ph.sb("parts", [P, TILES, TERMS, E], BF16)
        TB = ph.ps("TB", [CWR, 4, 1024], BF16)
        b_in, chain, parts_ready, transposed, copied = ph.sems("b_in chain parts_ready transposed copied")
        block = ph.block()

        @block.sync
        def _(sp):
            sp.dma_start(bias_b[:, 0, :], bias.rearrange("(o e) -> o e", o=1).to_broadcast([P, E])).then_inc(b_in, 16)

        @block.vector
        def _(dve):
            n = [0]

            def step(ins):
                n[0] += 1
                ins.then_inc(chain, 1)
                dve.wait_ge(chain, n[0])

            tt = nc.vector.tensor_tensor
            dve.wait_ge(b_in, 16)
            step(tt(sb_[:], scores[:], bias_b[:].to_broadcast([P, TILES, E]), ALU.add))
            v = sb_[:].rearrange("p t (g n) -> p (t g) n", g=G)
            step(tt(hi1[:], v[:, :, 0:4], v[:, :, 4:8], ALU.max))
            step(tt(lo1[:], v[:, :, 0:4], v[:, :, 4:8], ALU.min))
            for hi, lo, hi_n, lo_n, m in ((hi1, lo1, hi2, lo2, 2), (hi2, lo2, hi3, lo3, 1)):
                step(tt(hi_n[:], hi[:, :, 0:m], hi[:, :, m:2 * m], ALU.max))
                step(tt(t2[:, :, 0:m], hi[:, :, 0:m], hi[:, :, m:2 * m], ALU.min))
                step(tt(u2[:, :, 0:m], lo[:, :, 0:m], lo[:, :, m:2 * m], ALU.max))
                step(tt(lo_n[:], t2[:, :, 0:m], u2[:, :, 0:m], ALU.max))
            step(tt(gs[:].rearrange("p t g -> p (t g)"), hi3[:, :, 0], lo3[:, :, 0], ALU.add))
            for g in range(G):
                own = gs[:, :, g:g + 1]
                if g:
                    step(tt(beats[:, :, g, 0:g], gs[:, :, 0:g], own.to_broadcast([P, TILES, g]), ALU.is_ge))
                if g < G - 1:
                    step(tt(beats[:, :, g, g:G - 1], gs[:, :, g + 1:G], own.to_broadcast([P, TILES, G - 1 - g]),
                            ALU.is_gt))
            step(nc.vector.tensor_reduce(rank[:], beats[:], AX.X, ALU.add))
            r2 = rank[:].rearrange("p t (g o) -> p (t g) o", o=1)
            step(nc.vector.tensor_scalar(gm[:], r2, float(TOP_GROUPS), None, ALU.is_lt))
            step(nc.vector.tensor_scalar(pen[:], gm[:], 1.0, -NEG, ALU.subtract, ALU.mult))
            mv = masked[:].rearrange("p t (g n) -> p (t g) n", g=G)
            step(tt(mv, v, gm[:].to_broadcast([P, TILES * G, N]), ALU.mult))
            step(tt(mv, mv, pen[:].to_broadcast([P, TILES * G, N]), ALU.add))
            for t in range(TILES):
                ins = nc.vector.max(top[:, t, :], masked[:, t, :])
            step(ins)
            for t in range(TILES):
                ins = nc.vector.match_replace(left[:, t, :], top[:, t, :], masked[:, t, :], TAKEN)
            step(ins)
            step(nc.vector.tensor_scalar(left[:], left[:], TAKEN, None, ALU.is_equal))
            step(tt(w[:], scores[:], left[:], ALU.mult))
            step(nc.vector.tensor_reduce(total[:, :, 0], w[:], AX.X, ALU.add))
            step(nc.vector.reciprocal(total[:], total[:]))
            step(nc.vector.tensor_scalar(total[:], total[:], ROUTED_SCALE, None, ALU.mult))
            step(tt(w[:], w[:], total[:].to_broadcast([P, TILES, E]), ALU.mult))
            step(nc.vector.tensor_copy(parts[:, :, 0, :], w[:]))
            step(tt(rest[:], w[:], parts[:, :, 0, :], ALU.subtract))
            step(nc.vector.tensor_copy(parts[:, :, 1, :], rest[:]))
            tt(parts[:, :, 2, :], rest[:], parts[:, :, 1, :], ALU.subtract).then_inc(parts_ready, 1)

        @block.tensor
        def _(pe):
            pe.wait_ge(parts_ready, 1)
            for t in range(TILES):
                ins = nc.tensor.transpose(TB[:, t // 8, (t % 8) * P:(t % 8 + 1) * P],
                                          parts[:, t].rearrange("p s e -> p (s e)"), identb[:])
                if t % 8 == 7:
                    ins.then_inc(transposed, 1)

        @block.scalar
        def _(act):
            for j in range(4):
                act.wait_ge(transposed, j + 1)
                nc.scalar.activation(CWT[:, j * 1024:(j + 1) * 1024], TB[:, j], ACT.Copy).then_inc(copied, 1)


def experts_phase(nc, a, X, LH, LL, CWT):
    E = EXPERTS
    with Phase(nc, "experts") as ph:
        W1H = ph.sb("W1H", [P, E, INTER], F32R)
        W1L = ph.sb("W1L", [P, E, INTER], F32R)
        W2 = ph.sb("W2", [P, E, LAT])
        fc2 = ph.sb("fc2", [P, D])
        pick = ph.sb("pick", [CWR, E, P], BF16)
        raw = ph.sb("raw", [P, E, INTER])
        r = ph.sb("r", [P, 2, CHUNK])
        sq = ph.sb("sq", [P, 2, CHUNK])
        h = ph.sb("h", [P, 2, CHUNK])
        y = ph.sb("y", [P, CHUNK])
        HP = ph.ps("HP", [P, 2, CHUNK])
        CW = ph.ps("CW", [P, 2, CHUNK])
        Y = ph.ps("Y", [P, CHUNK])
        OP = ph.ps("OP", [P, 2, 512])
        (w_in, wh_ready, wl_ready, zero, picked, pe_h, pe_cw, act_r, act_sq, dve_h, pe_y, act_y, pe_o,
         dve_x) = ph.sems("w_in wh_ready wl_ready zero picked pe_h pe_cw act_r act_sq dve_h pe_y act_y pe_o dve_x")
        block = ph.block()

        @block.sync
        def _(sp):
            sp.dma_start(raw[:], a["L0_ffn_w1"].rearrange("e l i -> l e i")).then_inc(w_in, 16)
            sp.dma_start(W2[:], a["L0_ffn_w2"].rearrange("e i l -> i e l")).then_inc(w_in, 16)
            sp.dma_start(fc2[:], a["L0_ffn_fc2_w"]).then_inc(w_in, 16)

        @block.gpsimd
        def _(pool):
            nc.gpsimd.memset(pick[:], 0.0).then_inc(zero, 1)
            pool.wait_ge(zero, 1)
            for j in range(TERMS):
                rows = pick[j * E:(j + 1) * E]
                nc.gpsimd.affine_select(out=rows, in_=rows, compare_op=ALU.not_equal, fill=1.0, base=0,
                                        pattern=[[-1, E], [0, P]], channel_multiplier=1).then_inc(picked, 1)

        @block.scalar
        def _(act):
            act.wait_ge(w_in, 48)
            nc.scalar.activation(W1H[:], raw[:], ACT.Copy).then_inc(wh_ready, 1)
            give_credit(act, act_r, act_sq, act_y)
            with act.Fori(0, CHUNKS) as g:
                for e in range(E):
                    n = g * E + e
                    act.wait_ge(act_sq, done(n - 2))
                    act.wait_ge(pe_h, done(n))
                    nc.scalar.activation(r[:, e % 2], HP[:, e % 2], ACT.Relu).then_inc(act_r, 1)
                    act.wait_ge(dve_h, done(n - 2))
                    act.wait_ge(act_r, done(n))
                    nc.scalar.activation(sq[:, e % 2], r[:, e % 2], ACT.Square).then_inc(act_sq, 1)
                act.wait_ge(pe_o, done(g * TPC - 1))
                act.wait_ge(pe_y, done(g * E + E - 1))
                nc.scalar.activation(y[:], Y[:], ACT.Copy).then_inc(act_y, 1)

        @block.tensor
        def _(pe):
            pe.wait_ge(wl_ready, 1)
            pe.wait_ge(picked, TERMS)
            give_credit(pe, pe_h, pe_cw, pe_y, pe_o)
            with pe.Fori(0, CHUNKS) as g:
                cols = bass.ds(g * CHUNK, CHUNK)

                def up(e):
                    n = g * E + e
                    pe.wait_ge(act_r, done(n - 2))
                    nc.tensor.matmul(HP[:, e % 2], W1H[:, e, :], LH[:, cols], start=True, stop=False)
                    nc.tensor.matmul(HP[:, e % 2], W1H[:, e, :], LL[:, cols], start=False, stop=False)
                    nc.tensor.matmul(HP[:, e % 2], W1L[:, e, :], LH[:, cols], start=False, stop=True).then_inc(pe_h, 1)
                    pe.wait_ge(dve_h, done(n - 2))
                    nc.tensor.matmul(CW[:, e % 2], pick[:, e, :], CWT[:, cols], start=True, stop=True)\
                        .then_inc(pe_cw, 1)

                up(0)
                up(1)
                for e in range(E):
                    if e == 0:
                        pe.wait_ge(act_y, done(g - 1))
                    pe.wait_ge(dve_h, done(g * E + e))
                    nc.tensor.matmul(Y[:], W2[:, e, :], h[:, e % 2], start=(e == 0), stop=(e == E - 1))\
                        .then_inc(pe_y, 1)
                    if e + 2 < E:
                        up(e + 2)
                pe.wait_ge(act_y, done(g))
                for t in range(TPC):
                    pe.wait_ge(dve_x, done(g * TPC + t - 2))
                    nc.tensor.matmul(OP[:, t % 2, 0:D], y[:, t * P:(t + 1) * P], fc2[:], start=True, stop=True)\
                        .then_inc(pe_o, 1)

        @block.vector
        def _(dve):
            dve.wait_ge(wh_ready, 1)
            nc.vector.tensor_tensor(W1L[:], raw[:], W1H[:].bitcast(F32), ALU.subtract).then_inc(wl_ready, 1)
            give_credit(dve, dve_h, dve_x)
            with dve.Fori(0, CHUNKS) as g:
                for e in range(E):
                    n = g * E + e
                    dve.wait_ge(pe_y, done(n - 2))
                    dve.wait_ge(pe_cw, done(n))
                    dve.wait_ge(act_sq, done(n))
                    nc.vector.tensor_tensor(h[:, e % 2], sq[:, e % 2], CW[:, e % 2], ALU.mult).then_inc(dve_h, 1)
                for t in range(TPC):
                    dve.wait_ge(pe_o, done(g * TPC + t))
                    xt = X[:, bass.ds(g * TPC + t, 1), :]
                    nc.vector.tensor_tensor(xt, OP[:, t % 2:t % 2 + 1, 0:D], xt, ALU.add).then_inc(dve_x, 1)


def latent_moe_layer(nc, a, X, ident, identb):
    with ExitStack() as c:
        LH = c.enter_context(nc.sbuf_tensor("B_LH", [P, T], F32R))
        LL = c.enter_context(nc.sbuf_tensor("B_LL", [P, T], F32R))
        CWT = c.enter_context(nc.sbuf_tensor("B_CWT", [CWR, T], BF16))
        scores = c.enter_context(nc.sbuf_tensor("B_scores", [P, TILES, EXPERTS], F32))
        with ExitStack() as c2:
            XH = c2.enter_context(nc.sbuf_tensor("B_XH", [P, KD, T], F32R))
            XL = c2.enter_context(nc.sbuf_tensor("B_XL", [P, KD, T], F32R))
            transpose_phase(nc, "lnB", X, XH, XL, ident, True)
            shared_phase(nc, a, X, XH, XL, LH, LL, scores)
        group_routing_phase(nc, a["L0_ffn_gate_bias"], scores, CWT, identb)
        experts_phase(nc, a, X, LH, LL, CWT)
def linear_attention_phase(nc, X, XH, XL, ident, w_qkv, w_gate, w_out, rms_w, slope):
    H, DH, BLK = 16, 128, 128
    NBLK = SEQ // BLK
    HD = H * DH
    B4 = BATCH
    with Phase(nc, "lin") as ph:
        raw = ph.sb("raw", [P, KD, 4, DH])
        WH = ph.sb("WH", [P, KD, 4, DH], F32R)
        WL = ph.sb("WL", [P, KD, 4, DH], F32R)
        wo_raw = ph.sb("wo_raw", [P, D])
        WO = ph.sb("WO", [P, D])
        rms = ph.sb("rms", [P, H])
        slopes = ph.sb("slopes", [P, H])
        nslopes = ph.sb("nslopes", [P, H])
        pos_i = ph.sb("pos_i", [P, 3, BLK], I32)
        pos = ph.sb("pos", [P, 3, BLK])
        qdec = ph.sb("qdec", [P, H, BLK])
        qdec_h = ph.sb("qdec_h", [P, BLK])
        ddec = ph.sb("ddec", [P, H, BLK])
        kdec = ph.sb("kdec", [P, H])
        bdec = ph.sb("bdec", [P, H])
        ones = ph.sb("ones", [P, 2])
        acc = ph.sb("acc", [P, TILES, D])
        ssq = ph.sb("ssq", [P, BATCH, NBLK])
        rs = ph.sb("rs", [P, TILES])
        qT = ph.sb("qT", [P, 2, B4, BLK])
        kT = ph.sb("kT", [P, 2, B4, BLK])
        v = ph.sb("v", [P, 2, B4, DH])
        gT = ph.sb("gT", [P, 2, B4, BLK])
        qd = ph.sb("qd", [P, 2, B4, BLK])
        sd = ph.sb("sd", [P, B4, BLK])
        kd = ph.sb("kd", [P, B4, DH])
        kv = ph.sb("kv", [P, B4, DH])
        o2 = ph.sb("o2", [P, 2, B4, BLK])
        go = ph.sb("go", [P, 2, B4, BLK])
        PJ = ph.ps("PJ", [P, 2, B4, P])
        S = ph.ps("S", [P, B4, P])
        KT = ph.ps("KT", [P, B4, P])
        O = ph.ps("O", [P, B4, P])
        OUT = ph.ps("OUT", [P, 2, 2, D])
        SQ = ph.ps("SQ", [P, 512])
        (w_in, wo_in, c_in, iota_ready, pos_ready, tab_exp, tab_ready, neg_ready,
         wh_ready, wl_ready, wo_ready, memsets,
         pe_q, pe_k, pe_v, pe_g, pe_s, pe_kt, pe_o, pe_kv, pe_out0, pe_out1, pe_sq,
         act_q, act_k, act_v, act_g, act_sq, pool_qd,
         dve_sd, dve_kd, dve_kv, dve_go, dve_acc0, dve_acc1, dve_ssq, dve_qdh, fin, fin2, fin3) = ph.sems(
            "w_in wo_in c_in iota_ready pos_ready tab_exp tab_ready neg_ready wh_ready wl_ready wo_ready memsets "
            "pe_q pe_k pe_v pe_g pe_s pe_kt pe_o pe_kv pe_out0 pe_out1 pe_sq act_q act_k act_v act_g act_sq "
            "pool_qd dve_sd dve_kd dve_kv dve_go dve_acc0 dve_acc1 dve_ssq dve_qdh fin fin2 fin3")
        pe_out = (pe_out0, pe_out1)
        dve_acc = (dve_acc0, dve_acc1)
        xh = XH[:].rearrange("p k (b c l) -> p k b c l", b=B4, c=NBLK)
        xl = XL[:].rearrange("p k (b c l) -> p k b c l", b=B4, c=NBLK)
        acc_v = acc[:].rearrange("p (b c) n -> p b c n", b=B4)
        wqkv_v = w_qkv.rearrange("(k p) n -> p k n", p=P)
        wg_v = w_gate.rearrange("(k p) n -> p k n", p=P)
        Q, K, V, G = range(4)
        block = ph.block()

        @block.sync
        def _(sp):
            sp.dma_start(rms[:], rms_w.rearrange("(h p) -> p h", p=P), allow_slow_non_contiguous=True).then_inc(c_in, 16)
            sp.dma_start(slopes[:], slope.rearrange("(o h) -> o h", o=1).to_broadcast([P, H])).then_inc(c_in, 16)

            def load_head(h):
                for w in range(3):
                    sp.dma_start(raw[:, :, w, :], wqkv_v[:, :, bass.ds(h * DH + w * HD, DH)]).then_inc(w_in, 16)
                sp.dma_start(raw[:, :, G, :], wg_v[:, :, bass.ds(h * DH, DH)]).then_inc(w_in, 16)
                sp.dma_start(wo_raw[:], w_out[bass.ds(h * DH, DH), :]).then_inc(wo_in, 16)

            load_head(0)
            with sp.Fori(0, H - 1) as h:
                sp.wait_ge(wl_ready, h + 1)
                sp.wait_ge(wo_ready, h + 1)
                load_head(h + 1)
            sp.wait_ge(wl_ready, H)
            sp.wait_ge(wo_ready, H)
            load_head(0)
            sp.wait_ge(w_in, 64 * (H + 1))
            sp.wait_ge(wo_in, 16 * (H + 1))

        @block.gpsimd
        def _(pool):
            nc.gpsimd.iota(pos_i[:, 0, :], [[1, BLK]], base=1, channel_multiplier=0).then_inc(iota_ready, 1)
            nc.gpsimd.iota(pos_i[:, 1, :], [[1, BLK]], base=0, channel_multiplier=-1).then_inc(iota_ready, 1)
            nc.gpsimd.iota(pos_i[:, 2, :], [[0, BLK]], base=BLK - 1, channel_multiplier=-1).then_inc(iota_ready, 1)
            for h in range(H):
                pool.wait_ge(tab_exp, 4 * h + 4)
                nc.gpsimd.affine_select(out=ddec[:, h, :], in_=ddec[:, h, :], compare_op=ALU.is_ge, fill=0.0, base=0,
                                        pattern=[[1, BLK]], channel_multiplier=-1).then_inc(tab_ready, 1)
            give_credit(pool, pool_qd)
            with pool.Fori(0, H) as h:
                for c in range(NBLK):
                    i, u = h * NBLK + c, c % 2
                    pool.wait_ge(act_q, done(i))
                    pool.wait_ge(pe_o, done(i - 2))
                    if c == 0:
                        pool.wait_ge(dve_qdh, h + 1)
                    nc.gpsimd.tensor_tensor(qd[:, u], qT[:, u],
                                            qdec_h[:].rearrange("p (o l) -> p o l", o=1).to_broadcast([P, B4, BLK]),
                                            ALU.mult).then_inc(pool_qd, 1)

        @block.scalar
        def _(act):
            act.wait_ge(neg_ready, 1)
            for h in range(H):
                sc = nslopes[:, h:h + 1]
                nc.scalar.activation(qdec[:, h, :], pos[:, 0, :], ACT.Exp, scale=sc).then_inc(tab_exp, 1)
                nc.scalar.activation(ddec[:, h, :], pos[:, 1, :], ACT.Exp, scale=sc).then_inc(tab_exp, 1)
                nc.scalar.activation(kdec[:, h:h + 1], pos[:, 2, 0:1], ACT.Exp, scale=sc).then_inc(tab_exp, 1)
                nc.scalar.activation(bdec[:, h:h + 1], pos[:, 0, BLK - 1:BLK], ACT.Exp, scale=sc).then_inc(tab_exp, 1)
            act.preload_act_table(ACT.Silu)
            give_credit(act, act_q, act_k, act_v, act_g, act_sq)

            def weights_high(load):
                act.wait_ge(w_in, (load + 1) * 64)
                act.wait_ge(pe_g, done(load * NBLK - 1))
                nc.scalar.activation(WH[:], raw[:], ACT.Copy).then_inc(wh_ready, 1)

            def qk(n, u):
                act.wait_ge(pe_out1, done(n - 2))
                act.wait_ge(pool_qd, done(n - 2))
                act.wait_ge(pe_q, done(n))
                nc.scalar.activation(qT[:, u], PJ[:, 0], ACT.Silu).then_inc(act_q, 1)
                act.wait_ge(pe_k, done(n))
                nc.scalar.activation(kT[:, u], PJ[:, 1], ACT.Silu).then_inc(act_k, 1)

            def vg(n, u):
                act.wait_ge(pe_v, done(n))
                nc.scalar.activation(v[:, u], PJ[:, 0], ACT.Silu).then_inc(act_v, 1)
                act.wait_ge(dve_go, done(n - 2))
                act.wait_ge(pe_g, done(n))
                nc.scalar.activation(gT[:, u], PJ[:, 1], ACT.Tanh, scale=0.5).then_inc(act_g, 1)

            weights_high(0)
            qk(0, 0)
            vg(0, 0)
            with act.Fori(0, H) as h:
                for c in range(NBLK):
                    i, u = h * NBLK + c, c % 2
                    if c == NBLK - 1:
                        weights_high(h + 1)
                    qk(i + 1, 1 - u)
                    act.wait_ge(pe_o, done(i))
                    act.wait_ge(pe_sq, done(i - 2))
                    nc.scalar.activation(o2[:, u], O[:], ACT.Square).then_inc(act_sq, 1)
                    vg(i + 1, 1 - u)
            act.wait_ge(fin, 1)
            nc.scalar.activation(rs[:], rs[:], ACT.Sqrt).then_inc(fin2, 1)

        @block.tensor
        def _(pe):
            give_credit(pe, pe_q, pe_k, pe_v, pe_g, pe_s, pe_kt, pe_o, pe_kv, pe_out0, pe_out1, pe_sq)

            def project_t(bank, w, c, sem):
                n = 0
                for a, x in ((WH, xh), (WH, xl), (WL, xh)):
                    for k in range(KD):
                        ins = nc.tensor.matmul(PJ[:, bank], a[:, k, w, :], x[:, k, :, c, :],
                                               start=(n == 0), stop=(n == 3 * KD - 1))
                        n += 1
                ins.then_inc(sem, 1)

            def project_qk(n, c, load):
                if c == 0:
                    pe.wait_ge(wl_ready, load + 1)
                pe.wait_ge(act_v, done(n - 1))
                project_t(0, Q, c, pe_q)
                pe.wait_ge(act_g, done(n - 1))
                project_t(1, K, c, pe_k)

            def project_vg(n, c):
                pe.wait_ge(act_q, done(n))
                for b in range(B4):
                    m = 0
                    for x, w in ((xh, WH), (xl, WH), (xh, WL)):
                        for k in range(KD):
                            ins = nc.tensor.matmul(PJ[:, 0, b, :], x[:, k, b, c, :], w[:, k, V, :],
                                                   start=(m == 0), stop=(m == 3 * KD - 1))
                            m += 1
                ins.then_inc(pe_v, 1)
                pe.wait_ge(act_k, done(n))
                project_t(1, G, c, pe_g)

            project_qk(0, 0, 0)
            project_vg(0, 0)
            pe.wait_ge(memsets, 1)
            with pe.Fori(0, H) as h:
                for c in range(NBLK):
                    i, u = h * NBLK + c, c % 2
                    nc_ = (c + 1) % NBLK
                    pe.wait_ge(act_k, done(i))
                    pe.wait_ge(dve_sd, done(i - 1))
                    for b in range(B4):
                        ins = nc.tensor.matmul(S[:, b, :], kT[:, u, b, :], qT[:, u, b, :], start=True, stop=True)
                    ins.then_inc(pe_s, 1)
                    if c == 0:
                        pe.wait_ge(dve_kd, done(i - 1))
                    else:
                        pe.wait_ge(dve_kv, h * (NBLK - 1) + c)
                    for b in range(B4):
                        ins = nc.tensor.transpose(KT[:, b, :], kT[:, u, b, :], ident[:])
                    ins.then_inc(pe_kt, 1)
                    project_qk(i + 1, nc_, h + 1)
                    pe.wait_ge(act_v, done(i))
                    pe.wait_ge(dve_sd, done(i))
                    pe.wait_ge(pool_qd, done(i))
                    pe.wait_ge(dve_go, done(i - 1))
                    for b in range(B4):
                        ins = nc.tensor.matmul(O[:, b, :], v[:, u, b, :], sd[:, b, :], start=True, stop=(c == 0))
                        if c:
                            ins = nc.tensor.matmul(O[:, b, :], kv[:, b, :], qd[:, u, b, :], start=False, stop=True)
                    ins.then_inc(pe_o, 1)
                    pe.wait_ge(dve_kd, done(i))
                    if c < NBLK - 1:
                        for b in range(B4):
                            ins = nc.tensor.matmul(KT[:, b, :], kd[:, b, :], v[:, u, b, :], start=True, stop=True)
                        ins.then_inc(pe_kv, 1)
                    project_vg(i + 1, nc_)
                    pe.wait_ge(dve_go, done(i))
                    pe.wait_ge(wo_ready, h + 1)
                    for half in range(2):
                        pe.wait_ge(dve_acc[half], done(i - 1))
                        for b in range(2):
                            ins = nc.tensor.matmul(OUT[:, half, b, :], go[:, u, 2 * half + b, :], WO[:],
                                                   start=True, stop=True)
                        ins.then_inc(pe_out[half], 1)
                    pe.wait_ge(act_sq, done(i))
                    pe.wait_ge(dve_ssq, done(i - 1))
                    for b in range(B4):
                        ins = nc.tensor.matmul(SQ[:, b:b + 1], o2[:, u, b, :], ones[:, 0:1], start=True, stop=True)
                    ins.then_inc(pe_sq, 1)

        @block.vector
        def _(dve):
            nc.vector.memset(acc[:], 0.0).then_inc(memsets, 1)
            nc.vector.memset(ssq[:], 0.0).then_inc(memsets, 1)
            nc.vector.memset(ones[:], 1.0).then_inc(memsets, 1)
            dve.wait_ge(iota_ready, 3)
            nc.vector.tensor_scalar(pos[:], pos_i[:], 0.0, None, ALU.max).then_inc(pos_ready, 1)
            dve.wait_ge(c_in, 32)
            nc.vector.tensor_scalar(nslopes[:], slopes[:], -1.0, None, ALU.mult).then_inc(pos_ready, 1)
            dve.wait_ge(pos_ready, 2)
            dve.wait_ge(memsets, 3)
            dve.sem_inc(neg_ready, 1)
            give_credit(dve, dve_sd, dve_kd, dve_go, dve_acc0, dve_acc1, dve_ssq)

            def weights_low(load):
                dve.wait_ge(wh_ready, load + 1)
                nc.vector.tensor_tensor(WL[:], raw[:], WH[:].bitcast(F32), ALU.subtract).then_inc(wl_ready, 1)

            def weights_out(load, rms_col):
                dve.wait_ge(wo_in, (load + 1) * 16)
                nc.vector.tensor_scalar(WO[:], wo_raw[:], rms_col, 0.5, ALU.mult, ALU.mult).then_inc(wo_ready, 1)

            weights_low(0)
            weights_out(0, rms[:, 0:1])
            dve.wait_ge(tab_ready, H)
            with dve.Fori(0, H) as h:
                for c in range(NBLK):
                    i, u = h * NBLK + c, c % 2
                    if c == 0:
                        dve.wait_ge(pool_qd, done(i - 1))
                        nc.vector.tensor_scalar(qdec_h[:], qdec[:, bass.ds(h, 1), :], 1.0, None, ALU.mult)\
                            .then_inc(dve_qdh, 1)
                    if c == NBLK - 1:
                        weights_low(h + 1)
                    dve.wait_ge(pe_s, done(i))
                    dve.wait_ge(pe_o, done(i - 1))
                    nc.vector.tensor_tensor(sd[:], S[:], ddec[:, bass.ds(h, 1), :].to_broadcast([P, B4, BLK]),
                                            ALU.mult).then_inc(dve_sd, 1)
                    dve.wait_ge(pe_kt, done(i))
                    if c > 0:
                        dve.wait_ge(pe_kv, done(h * (NBLK - 1) + c - 1))
                    nc.vector.tensor_scalar(kd[:], KT[:], kdec[:, bass.ds(h, 1)], None, ALU.mult)\
                        .then_inc(dve_kd, 1)
                    if c < NBLK - 1:
                        dve.wait_ge(pe_kv, done(h * (NBLK - 1) + c))
                        if c == 0:
                            nc.vector.tensor_copy(kv[:], KT[:]).then_inc(dve_kv, 1)
                        else:
                            dve.wait_ge(dve_kv, h * (NBLK - 1) + c)
                            nc.vector.scalar_tensor_tensor(kv[:], kv[:], bdec[:, bass.ds(h, 1)], KT[:],
                                                           ALU.mult, ALU.add).then_inc(dve_kv, 1)
                    dve.wait_ge(act_sq, done(i))
                    dve.wait_ge(act_g, done(i))
                    dve.wait_ge(pe_out1, done(i - 2))
                    nc.vector.scalar_tensor_tensor(go[:, u], gT[:, u], 1.0, O[:], ALU.add, ALU.mult)\
                        .then_inc(dve_go, 1)
                    for half in range(2):
                        dve.wait_ge(pe_out[half], done(i))
                        dve.wait_ge(dve_acc[half], done(i - 1))
                        dst = acc_v[:, 2 * half:2 * half + 2, c, :]
                        nc.vector.tensor_tensor(dst, OUT[:, half], dst, ALU.add).then_inc(dve_acc[half], 1)
                    dve.wait_ge(pe_sq, done(i))
                    dve.wait_ge(dve_ssq, done(i - 1))
                    nc.vector.tensor_tensor(ssq[:, :, c], SQ[:, 0:B4], ssq[:, :, c], ALU.add).then_inc(dve_ssq, 1)
                    if c == NBLK - 1:
                        weights_out(h + 1, rms[:, bass.ds((h + 1) % H, 1)])
            dve.wait_ge(dve_ssq, done(H * NBLK - 1))
            nc.vector.tensor_scalar(rs[:], ssq[:].rearrange("p b c -> p (b c)"), 1.0 / HD, 1.0e-6, ALU.mult, ALU.add)\
                .then_inc(fin, 1)
            dve.wait_ge(fin2, 1)
            nc.vector.reciprocal(rs[:], rs[:]).then_inc(fin3, 1)
            dve.wait_ge(fin3, 1)
            for t in range(TILES):
                nc.vector.scalar_tensor_tensor(X[:, t, :], acc[:, t, :], rs[:, t:t + 1], X[:, t, :],
                                               ALU.mult, ALU.add)


def linear_attention_layer(nc, a, X, ident):
    with ExitStack() as c:
        XH = c.enter_context(nc.sbuf_tensor("C_XH", [P, KD, T], F32R))
        XL = c.enter_context(nc.sbuf_tensor("C_XL", [P, KD, T], F32R))
        transpose_phase(nc, "lnC", X, XH, XL, ident, True)
        linear_attention_phase(nc, X, XH, XL, ident, a["L1_attn_w_qkv"], a["L1_attn_w_gate"],
                               a["L1_attn_w_out"], a["L1_attn_rms_weight"], a["L1_attn_slope_rate"])
KEPT, OLD, WIDTH, CAP, TOP_D = 48, 128, 96, 96, 8
ROW = D + KEPT
SLOTS = 4


def logits_phase(nc, a, XH, XL, ident, lg, known):
    with Phase(nc, "logit") as ph:
        raw = ph.sb("raw", [P, KD, OLD])
        GH = ph.sb("GH", [P, KD, OLD], F32R)
        GL = ph.sb("GL", [P, KD, OLD], F32R)
        o2n = ph.sb("o2n", [P, 1], I32)
        spread = ph.sb("spread", [P, P])
        pen = ph.sb("pen", [P, 1, OLD])
        LG = ph.ps("LG", [P, 4, TPC, OLD])
        PN = ph.ps("PN", [P, OLD])
        (g_in, known_ready, spread_ready, pen_part, pen_ready, pe_pn, gh_ready, gl_ready, pe_lg, masked) = ph.sems(
            "g_in known_ready spread_ready pen_part pen_ready pe_pn gh_ready gl_ready pe_lg masked")
        block = ph.block()

        @block.sync
        def _(sp):
            sp.dma_start(o2n[:], a["L1_ffn_old_to_new"].rearrange("(p o) -> p o", o=1)).then_inc(g_in, 16)
            sp.dma_start(raw[:], a["L1_ffn_gate_weight"].rearrange("(k p) n -> p k n", p=P)).then_inc(g_in, 16)

        @block.scalar
        def _(act):
            act.wait_ge(g_in, 32)
            nc.scalar.activation(GH[:], raw[:], ACT.Copy).then_inc(gh_ready, 1)

        @block.tensor
        def _(pe):
            pe.wait_ge(spread_ready, 1)
            nc.tensor.transpose(PN[:], spread[:], ident[:]).then_inc(pe_pn, 1)
            pe.wait_ge(gl_ready, 1)
            for g in range(CHUNKS):
                if g >= 4:
                    pe.wait_ge(masked, g - 3)
                for t in range(TPC):
                    tok = (g * TPC + t) * P
                    n = 0
                    for x, W in ((XH, GH), (XL, GH), (XH, GL)):
                        for k in range(KD):
                            ins = nc.tensor.matmul(LG[:, g % 4, t, :], x[:, k, tok:tok + P], W[:, k, :],
                                                   start=(n == 0), stop=(n == 3 * KD - 1))
                            n += 1
                ins.then_inc(pe_lg, 1)

        @block.vector
        def _(dve):
            dve.wait_ge(g_in, 32)
            nc.vector.tensor_copy(known[:], o2n[:]).then_inc(known_ready, 1)
            dve.wait_ge(known_ready, 1)
            nc.vector.tensor_scalar(pen[:, 0, 0:1], known[:], -1.0, NEG, ALU.is_equal, ALU.mult).then_inc(pen_part, 1)
            dve.wait_ge(pen_part, 1)
            nc.vector.tensor_copy(spread[:], pen[:, 0, 0:1].to_broadcast([P, P])).then_inc(spread_ready, 1)
            dve.wait_ge(gh_ready, 1)
            nc.vector.tensor_tensor(GL[:], raw[:], GH[:].bitcast(F32), ALU.subtract).then_inc(gl_ready, 1)
            dve.wait_ge(pe_pn, 1)
            nc.vector.tensor_copy(pen[:, 0, :], PN[:]).then_inc(pen_ready, 1)
            dve.wait_ge(pen_ready, 1)
            for g in range(CHUNKS):
                dve.wait_ge(pe_lg, g + 1)
                nc.vector.tensor_tensor(lg[:, g * TPC:(g + 1) * TPC, :], LG[:, g % 4],
                                        pen[:].to_broadcast([P, TPC, OLD]), ALU.add).then_inc(masked, 1)


def kept_router_phase(nc, a, X, lg, known, ident, identb, rows, out, idx):
    with Phase(nc, "keep") as ph:
        cols_i = ph.sb("cols_i", [P, KEPT], I32)
        cols = ph.sb("cols", [P, KEPT])
        perm = ph.sb("perm", [P, KEPT])
        permb = ph.sb("permb", [P, KEPT], BF16)
        stat = ph.sb("stat", [P, TILES, 1])
        top = ph.sb("top", [P, TILES, 8])
        left = ph.sb("left", [P, TILES, OLD])
        sel = ph.sb("sel", [P, TILES, OLD], BF16)
        wT = ph.sb("wT", [P, 2, CHUNK])
        sT = ph.sb("sT", [P, 2, CHUNK], BF16)
        w = ph.sb("w", [P, TILES, KEPT])
        down_i = ph.sb("down_i", [KEPT, T], I32)
        val = ph.sb("val", [KEPT, 2, T])
        first = ph.sb("first", [KEPT, CAP])
        slot_i = ph.sb("slot_i", [CAP, 1], I32)
        slot = ph.sb("slot", [CAP, 1])
        unused = ph.sb("unused", [CAP, KEPT])
        tok = ph.sb("tok", [CAP, KEPT])
        zero = ph.sb("zero", [SPARE, ROW])
        WT = ph.ps("WT", [P, 2, CHUNK])
        ST = ph.ps("ST", [P, 2, 2 * CHUNK], BF16)
        WN = ph.ps("WN", [P, TPC, OLD])
        SN = ph.ps("SN", [KEPT, 2, CHUNK])
        LT = ph.ps("LT", [CAP, KEPT])
        (iotas, chain, e_ready, act_e, w_ready, pe_t, act_w, act_s, pe_wn, pe_sn, dve_wn, dve_sn, list_ready, pe_lt,
         stored, zeroed) = ph.sems(
            "iotas chain e_ready act_e w_ready pe_t act_w act_s pe_wn pe_sn dve_wn dve_sn list_ready pe_lt "
            "stored zeroed")
        block = ph.block()

        @block.sync
        def _(sp):
            sp.dma_start(out[0:T, :].rearrange("(t p) n -> p t n", p=P), X[:]).then_inc(stored, 16)
            sp.wait_ge(zeroed, 1)
            sp.dma_start(out[T:T + SPARE, :], zero[:, 0:D]).then_inc(stored, 16)
            sp.dma_start(rows[T:T + SPARE, :], zero[:]).then_inc(stored, 16)
            sp.wait_ge(dve_wn, CHUNKS)
            sp.dma_start(rows[0:T, D:ROW].rearrange("(t p) n -> p t n", p=P), w[:]).then_inc(stored, 16)
            sp.wait_ge(stored, 64)

        @block.gpsimd
        def _(pool):
            nc.gpsimd.iota(cols_i[:], [[1, KEPT]], base=0, channel_multiplier=0).then_inc(iotas, 1)
            nc.gpsimd.iota(slot_i[:], [[0, 1]], base=0, channel_multiplier=1).then_inc(iotas, 1)
            nc.gpsimd.memset(zero[:], 0.0).then_inc(zeroed, 1)
            nc.gpsimd.iota(down_i[:], [[-1, T]], base=T, channel_multiplier=0).then_inc(iotas, 1)

        @block.tensor
        def _(pe):
            pe.wait_ge(w_ready, 1)
            for g in range(CHUNKS + 1):
                if g < CHUNKS:
                    b = g % 2
                    if g >= 2:
                        pe.wait_ge(act_s, g - 1)
                    for t in range(TPC):
                        nc.tensor.transpose(WT[:, b, t * P:(t + 1) * P], left[:, g * TPC + t, :], ident[:])
                        ins = nc.tensor.transpose(ST[:, b, t * P:(t + 1) * P], sel[:, g * TPC + t, :], identb[:])
                    ins.then_inc(pe_t, 1)
                if g >= 1:
                    q, b = g - 1, (g - 1) % 2
                    pe.wait_ge(act_s, q + 1)
                    if q >= 1:
                        pe.wait_ge(dve_wn, q)
                    for t in range(TPC):
                        ins = nc.tensor.matmul(WN[:, t, 0:KEPT], wT[:, b, t * P:(t + 1) * P], perm[:],
                                               start=True, stop=True)
                    ins.then_inc(pe_wn, 1)
                    if q >= 2:
                        pe.wait_ge(dve_sn, q - 1)
                    nc.tensor.matmul(SN[:, b, :], permb[:], sT[:, b, :], start=True, stop=True).then_inc(pe_sn, 1)
            pe.wait_ge(list_ready, 1)
            nc.tensor.transpose(LT[:], first[:], ident[0:KEPT, 0:KEPT]).then_inc(pe_lt, 1)

        @block.scalar
        def _(act):
            act.wait_ge(e_ready, 1)
            nc.scalar.activation(lg[:], lg[:], ACT.Exp).then_inc(act_e, 1)
            for g in range(CHUNKS):
                act.wait_ge(pe_t, g + 1)
                if g >= 2:
                    act.wait_ge(pe_sn, g - 1)
                nc.scalar.activation(wT[:, g % 2], WT[:, g % 2], ACT.Copy).then_inc(act_w, 1)
                nc.scalar.activation(sT[:, g % 2], ST[:, g % 2, 0:CHUNK], ACT.Copy).then_inc(act_s, 1)

        @block.vector
        def _(dve):
            n = [0]

            def step(ins):
                n[0] += 1
                ins.then_inc(chain, 1)
                dve.wait_ge(chain, n[0])

            tt, ts = nc.vector.tensor_tensor, nc.vector.tensor_scalar
            wide = [P, TILES, OLD]
            step(nc.vector.tensor_reduce(stat[:, :, 0], lg[:], AX.X, ALU.max))
            tt(lg[:], lg[:], stat[:].to_broadcast(wide), ALU.subtract).then_inc(e_ready, 1)
            dve.wait_ge(iotas, 3)
            step(nc.vector.tensor_copy(cols[:], cols_i[:]))
            step(nc.vector.tensor_copy(slot[:], slot_i[:]))
            step(ts(perm[:], cols[:], known[:, 0:1], None, ALU.is_equal))
            step(nc.vector.tensor_copy(permb[:], perm[:]))
            dve.wait_ge(act_e, 1)
            step(nc.vector.tensor_reduce(stat[:, :, 0], lg[:], AX.X, ALU.add))
            step(nc.vector.reciprocal(stat[:], stat[:]))
            step(tt(lg[:], lg[:], stat[:].to_broadcast(wide), ALU.mult))
            for t in range(TILES):
                ins = nc.vector.max(top[:, t, :], lg[:, t, :])
            step(ins)
            for t in range(TILES):
                ins = nc.vector.match_replace(left[:, t, :], top[:, t, :], lg[:, t, :], -1.0)
            step(ins)
            step(nc.vector.tensor_reduce(stat[:, :, 0], top[:], AX.X, ALU.add))
            step(nc.vector.reciprocal(stat[:], stat[:]))
            step(ts(sel[:], left[:], 0.0, None, ALU.is_lt))
            step(tt(left[:], lg[:], sel[:], ALU.mult))
            tt(left[:], left[:], stat[:].to_broadcast(wide), ALU.mult).then_inc(w_ready, 1)
            for g in range(CHUNKS):
                dve.wait_ge(pe_wn, g + 1)
                nc.vector.tensor_copy(w[:, g * TPC:(g + 1) * TPC, :], WN[:, :, 0:KEPT]).then_inc(dve_wn, 1)
                dve.wait_ge(pe_sn, g + 1)
                tt(val[:, 0, g * CHUNK:(g + 1) * CHUNK], SN[:, g % 2], down_i[:, g * CHUNK:(g + 1) * CHUNK], ALU.mult)\
                    .then_inc(dve_sn, 1)
            dve.wait_ge(dve_sn, CHUNKS)
            for r in range(CAP // 8):
                step(nc.vector.max(first[:, 8 * r:8 * r + 8], val[:, r % 2]))
                if r < CAP // 8 - 1:
                    step(nc.vector.match_replace(val[:, 1 - r % 2], first[:, 8 * r:8 * r + 8], val[:, r % 2], 0.0))
            dve.sem_inc(list_ready, 1)
            dve.wait_ge(pe_lt, 1)
            step(ts(unused[:], LT[:], 0.0, slot[:, 0:1], ALU.is_equal, ALU.mult))
            step(ts(tok[:], LT[:], -1.0, float(T), ALU.mult, ALU.add))
            tt(idx[:], tok[:], unused[:], ALU.add)


def kept_experts_phase(nc, a, rows, out, idx, ident):
    gu = a["L1_ffn_gate_up_proj"]
    dn = a["L1_ffn_down_proj"]
    S = SLOTS
    with Phase(nc, "kept") as ph:
        GU = ph.sb("GU", [P, S, KD, 2 * WIDTH])
        DN = ph.sb("DN", [WIDTH, S, D])
        ix = ph.sb("ix", [CAP, S, 1], U32)
        xg = ph.sb("xg", [CAP, S, ROW])
        xT = ph.sb("xT", [P, 2, KD, CAP])
        sg = ph.sb("sg", [WIDTH, 2, CAP])
        h = ph.sb("h", [WIDTH, 2, CAP])
        ys = ph.sb("ys", [CAP, S, D])
        XT = ph.ps("XT", [P, 2, 512])
        GP = ph.ps("GP", [WIDTH, 2, 512])
        YP = ph.ps("YP", [CAP, 2, 512])
        w_in = [ph.sem(f"w_in{u}") for u in range(S)]
        g_in = [ph.sem(f"g_in{u}") for u in range(S)]
        (ix_ready, pe_x, act_x, pe_gu, act_g, dve_h, pe_y, dve_y, added, pool_turns, slot_free) = ph.sems(
            "ix_ready pe_x act_x pe_gu act_g dve_h pe_y dve_y added pool_turns slot_free")
        block = ph.block()

        @block.sync
        def _(sp):
            def load(e, u):
                sp.dma_start(GU[:, u], gu[bass.ds(e, 1)].rearrange("e (k p) n -> p (e k) n", p=P)).then_inc(w_in[u], 16)
                sp.dma_start(DN[:, u], dn[bass.ds(e, 1)].rearrange("e i n -> i (e n)")).then_inc(w_in[u], 16)

            for u in range(S):
                load(u, u)
            with sp.Fori(0, KEPT // S - 1) as i:
                for u in range(S):
                    sp.wait_ge(pe_y, done(i * S + u))
                    load((i + 1) * S + u, u)

        @block.gpsimd
        def _(pool):
            def gather(e, u):
                pool.wait_ge(ix_ready, done(e))
                pool.sem_inc(pool_turns, 1)
                nc.gpsimd.indirect_dma_start(out=xg[:, u], out_offset=None, in_=rows,
                                             in_offset=bass.IndirectOffsetOnAxis(ap=ix[:, u], axis=0))\
                    .then_inc(g_in[u], 16)

            def scatter(e, u):
                pool.wait_ge(dve_y, done(e))
                pool.sem_inc(pool_turns, 1)
                nc.gpsimd.indirect_dma_start(out=out, out_offset=bass.IndirectOffsetOnAxis(ap=ix[:, u], axis=0),
                                             in_=ys[:, u], in_offset=None, compute_op=ALU.add).then_inc(added, 16)
                pool.wait_ge(added, (e + 1) * 16)
                pool.sem_inc(slot_free, 1)

            give_credit(pool, slot_free)
            gather(0, 0)
            gather(1, 1)
            with pool.Fori(0, KEPT // S) as i:
                for u in range(S):
                    e = i * S + u
                    gather(e + 2, (u + 2) % S)
                    scatter(e, u)
            pool.wait_ge(added, 16 * KEPT)
            pool.wait_ge(g_in[0], 16 * (KEPT // S + 1))
            pool.wait_ge(g_in[1], 16 * (KEPT // S + 1))

        @block.tensor
        def _(pe):
            give_credit(pe, pe_x, pe_gu, pe_y)

            def turn(e, u):
                b = u % 2
                pe.wait_ge(act_x, done(e - 2))
                for k in range(KD):
                    ins = nc.tensor.transpose(XT[:, b, k * CAP:(k + 1) * CAP], xg[:, u, k * P:(k + 1) * P],
                                              ident[0:CAP, 0:CAP])
                ins.then_inc(pe_x, 1)

            def products(e, u):
                b = u % 2
                pe.wait_ge(act_x, done(e))
                pe.wait_ge(dve_h, done(e - 2))
                for m in range(2):
                    for k in range(KD):
                        ins = nc.tensor.matmul(GP[:, b, m * CAP:(m + 1) * CAP],
                                               GU[:, u, k, m * WIDTH:(m + 1) * WIDTH], xT[:, b, k, :],
                                               start=(k == 0), stop=(k == KD - 1))
                ins.then_inc(pe_gu, 1)

            def outputs(e, u):
                b = u % 2
                pe.wait_ge(dve_h, done(e))
                pe.wait_ge(dve_y, done(e - 2))
                nc.tensor.matmul(YP[:, b, 0:D], h[:, b], DN[:, u], start=True, stop=True).then_inc(pe_y, 1)

            with pe.Fori(0, KEPT // S) as i:
                for u in range(S):
                    e = i * S + u
                    pe.wait_ge(g_in[u], (i + 1) * 16)
                    turn(e, u)
                    pe.wait_ge(w_in[u], (i + 1) * 32)
                    products(e, u)
                    outputs(e, u)

        @block.scalar
        def _(act):
            act.preload_act_table(ACT.Silu)
            give_credit(act, act_x, act_g)
            with act.Fori(0, KEPT // S) as i:
                for u in range(S):
                    e, b = i * S + u, u % 2
                    act.wait_ge(pe_gu, done(e - 2))
                    act.wait_ge(pe_x, done(e))
                    nc.scalar.activation(xT[:, b], XT[:, b, 0:KD * CAP].rearrange("p (k c) -> p k c", k=KD), ACT.Copy)\
                        .then_inc(act_x, 1)
                    act.wait_ge(dve_h, done(e - 2))
                    act.wait_ge(pe_gu, done(e))
                    nc.scalar.activation(sg[:, b], GP[:, b, 0:CAP], ACT.Silu).then_inc(act_g, 1)

        @block.vector
        def _(dve):
            give_credit(dve, ix_ready, dve_h, dve_y)

            def indices(e, u):
                nc.vector.tensor_scalar(ix[:, u], idx[:, bass.ds(e, 1)], 0.0, None, ALU.add).then_inc(ix_ready, 1)

            indices(0, 0)
            indices(1, 1)
            with dve.Fori(0, KEPT // S) as i:
                for u in range(S):
                    e, b = i * S + u, u % 2
                    dve.wait_ge(slot_free, done(e - 2))
                    indices((e + 2) % KEPT, (u + 2) % S)
                    dve.wait_ge(pe_y, done(e - 2))
                    dve.wait_ge(act_g, done(e))
                    nc.vector.tensor_tensor(h[:, b], sg[:, b], GP[:, b, CAP:2 * CAP], ALU.mult).then_inc(dve_h, 1)
                    dve.wait_ge(pe_y, done(e))
                    nc.vector.tensor_scalar(ys[:, u], YP[:, b, 0:D], xg[:, u, bass.ds(e + D, 1)], None, ALU.mult)\
                        .then_inc(dve_y, 1)


def capacity_moe_layer(nc, a, X, ident, identb, out):
    rows = nc.dram_tensor("token_rows", (T + SPARE, ROW), F32, kind="Internal").ap()
    with ExitStack() as c:
        idx = c.enter_context(nc.sbuf_tensor("D_idx", [CAP, KEPT], U32))
        lg = c.enter_context(nc.sbuf_tensor("D_lg", [P, TILES, OLD], F32))
        known = c.enter_context(nc.sbuf_tensor("D_known", [P, 1], F32))
        with ExitStack() as c2:
            XH = c2.enter_context(nc.sbuf_tensor("D_XH", [P, KD, T], F32R))
            XL = c2.enter_context(nc.sbuf_tensor("D_XL", [P, KD, T], F32R))
            transpose_phase(nc, "lnD", X, XH, XL, ident, True, normed=rows)
            logits_phase(nc, a, XH, XL, ident, lg, known)
        kept_router_phase(nc, a, X, lg, known, ident, identb, rows, out, idx)
        kept_experts_phase(nc, a, rows, out, idx, ident)
def build_program(nc, a, out):
    x = a["L0_attn_x"].rearrange("b s d -> (b s) d")
    with ExitStack() as ctx:
        def keep(name, shape, dt=F32):
            return ctx.enter_context(nc.sbuf_tensor(name, shape, dt))

        X = keep("X", [P, TILES, D])
        ident = keep("ident", [P, P])
        identb = keep("identb", [P, P], BF16)
        mask_q = keep("mask_q", [P, P], BF16)
        mask_k = keep("mask_k", [P, P], BF16)
        constants_phase(nc, x, X, ident, identb, mask_q, mask_k)
        attention_layer(nc, a, X, ident, identb, mask_q, mask_k)
        latent_moe_layer(nc, a, X, ident, identb)
        linear_attention_layer(nc, a, X, ident)
        capacity_moe_layer(nc, a, X, ident, identb, out)


TRANSPOSED = ("L0_attn_W_Q", "L0_attn_W_K", "L0_attn_W_V", "L0_attn_W_O", "L0_ffn_gate_w", "L0_ffn_fc1_w",
              "L0_ffn_fc2_w", "L0_ffn_w1", "L0_ffn_w2", "L0_ffn_shared_up_w", "L0_ffn_shared_down_w",
              "L1_ffn_gate_weight", "L1_ffn_gate_up_proj", "L1_ffn_down_proj")
SPARE = 96


def kernel(**inputs):
    import numpy as np
    import concourse.bacc as bacc
    from concourse.bass_utils import run_bass_kernel_spmd

    nc = bacc.Bacc("TRN2", target_bir_lowering=False, num_devices=1)
    arrays, aps = {}, {}
    for name, value in inputs.items():
        v = np.asarray(value)
        if name in TRANSPOSED:
            v = np.swapaxes(v, -1, -2)
        if name == "L1_attn_slope_rate":
            v = v.reshape(-1)
        v = np.ascontiguousarray(v)
        arrays[name] = v
        aps[name] = nc.dram_tensor(name, v.shape, mybir.dt.from_np(v.dtype), kind="ExternalInput").ap()
    out = nc.dram_tensor("out", (T + SPARE, D), F32, kind="ExternalOutput").ap()
    build_program(nc, aps, out)
    r = run_bass_kernel_spmd(nc, [arrays], core_ids=[0])
    return np.asarray(r.results[0]["out"])[:T].reshape(BATCH, SEQ, D)
```

```python
from contextlib import ExitStack

import concourse.bass as bass
from concourse import mybir

F32 = mybir.dt.float32
F32R = mybir.dt.float32r
BF16 = mybir.dt.bfloat16
U32 = mybir.dt.uint32
I32 = mybir.dt.int32
ALU = mybir.AluOpType
ACT = mybir.ActivationFunctionType
AX = mybir.AxisListType

P = 128
D = 256
KD = D // P
BATCH, SEQ = 4, 1024
T = BATCH * SEQ
TILES = T // P
CHUNK = 512
CHUNKS = T // CHUNK
TPC = CHUNK // P
NEG = -1.0e30

CREDIT = 2


def done(step):
    return step + 1 + CREDIT


class Phase:

    def __init__(self, nc, name):
        self.nc, self.name, self.ctx = nc, name, ExitStack()
        self.owned = []

    def __enter__(self):
        return self

    def __exit__(self, *exc):
        self.ctx.close()
        self.nc.clear_and_free_semaphores(self.owned)
        self.nc.all_engine_barrier()

    def sb(self, name, shape, dt=F32):
        return self.ctx.enter_context(self.nc.sbuf_tensor(f"{self.name}_{name}", shape, dt))

    def ps(self, name, shape, dt=F32):
        return self.ctx.enter_context(self.nc.psum_tensor(f"{self.name}_{name}", shape, dt))

    def sem(self, name):
        self.owned.append(self.nc.alloc_semaphore(f"{self.name}_{name}"))
        return self.owned[-1]

    def sems(self, names):
        return [self.sem(n) for n in names.split()]

    def block(self):
        return self.ctx.enter_context(self.nc.Block())


def give_credit(eng, *sems):
    for s in sems:
        eng.sem_inc(s, CREDIT)


LH, LBLK = 16, 128


def constants_phase(nc, x, slope, X, ident, identb, mask_q, mask_k, decays, kdec, bdec):
    with Phase(nc, "const") as ph:
        slopes = ph.sb("slopes", [P, LH])
        nslopes = ph.sb("nslopes", [P, LH])
        pos_i = ph.sb("pos_i", [P, 3, LBLK], I32)
        pos = ph.sb("pos", [P, 3, LBLK])
        tab = ph.sb("tab", [P, LH, 2, LBLK])
        (x_in, pool_set, pool_sel, f_ready, slope_in, iota_ready, pos_ready, tab_exp, tab_ready, tab_stored) = ph.sems(
            "x_in pool_set pool_sel ident_ready slope_in iota_ready pos_ready tab_exp tab_ready tab_stored")
        block = ph.block()

        @block.sync
        def _(sp):
            sp.dma_start(slopes[:], slope.rearrange("(o h) -> o h", o=1).to_broadcast([P, LH])).then_inc(slope_in, 16)
            src = x.rearrange("(t p) n -> p t n", p=P)
            for g in range(4):
                sp.dma_start(X[:, 8 * g:8 * g + 8, :], src[:, 8 * g:8 * g + 8, :]).then_inc(x_in, 16)
            sp.wait_ge(tab_ready, LH)
            sp.dma_start(decays.rearrange("h p w l -> p h w l"), tab[:]).then_inc(tab_stored, 16)
            sp.wait_ge(x_in, 64)
            sp.wait_ge(tab_stored, 16)

        @block.scalar
        def _(act):
            act.wait_ge(pos_ready, 2)
            for h in range(LH):
                nc.scalar.activation(tab[:, h, :, :], pos[:, 0:2, :], ACT.Exp, scale=nslopes[:, h:h + 1])\
                    .then_inc(tab_exp, 1)
            nc.scalar.activation(kdec[:], nslopes[:], ACT.Exp, scale=pos[:, 2, 0:1])
            nc.scalar.activation(bdec[:], nslopes[:], ACT.Exp, scale=float(LBLK))

        @block.gpsimd
        def _(pool):
            nc.gpsimd.iota(pos_i[:, 0, :], [[1, LBLK]], base=1, channel_multiplier=0).then_inc(iota_ready, 1)
            nc.gpsimd.iota(pos_i[:, 1, :], [[1, LBLK]], base=0, channel_multiplier=-1).then_inc(iota_ready, 1)
            nc.gpsimd.iota(pos_i[:, 2, :], [[0, LBLK]], base=LBLK - 1, channel_multiplier=-1).then_inc(iota_ready, 1)
            nc.gpsimd.memset(ident[:], 0.0).then_inc(pool_set, 1)
            nc.gpsimd.memset(mask_q[:], 0.0).then_inc(pool_set, 1)
            nc.gpsimd.memset(mask_k[:], 0.0).then_inc(pool_set, 1)
            pool.wait_ge(pool_set, 3)
            nc.gpsimd.affine_select(out=ident[:], in_=ident[:], compare_op=ALU.not_equal, fill=1.0, base=0,
                                    pattern=[[-1, P]], channel_multiplier=1).then_inc(f_ready, 1)
            nc.gpsimd.affine_select(out=mask_q[:], in_=mask_q[:], compare_op=ALU.is_ge, fill=NEG, base=0,
                                    pattern=[[-1, P]], channel_multiplier=1).then_inc(pool_sel, 1)
            nc.gpsimd.affine_select(out=mask_k[:], in_=mask_k[:], compare_op=ALU.is_ge, fill=NEG, base=0,
                                    pattern=[[1, P]], channel_multiplier=-1).then_inc(pool_sel, 1)
            for h in range(LH):
                pool.wait_ge(tab_exp, h + 1)
                nc.gpsimd.affine_select(out=tab[:, h, 1, :], in_=tab[:, h, 1, :], compare_op=ALU.is_ge, fill=0.0,
                                        base=0, pattern=[[1, LBLK]], channel_multiplier=-1).then_inc(tab_ready, 1)

        @block.vector
        def _(dve):
            dve.wait_ge(iota_ready, 3)
            nc.vector.tensor_scalar(pos[:], pos_i[:], 0.0, None, ALU.max).then_inc(pos_ready, 1)
            dve.wait_ge(slope_in, 16)
            nc.vector.tensor_scalar(nslopes[:], slopes[:], -1.0, None, ALU.mult).then_inc(pos_ready, 1)
            dve.wait_ge(f_ready, 1)
            nc.vector.tensor_copy(identb[:], ident[:])


def transpose_phase(nc, name, SRC, XH, XL, ident, norm, normed=None):
    with Phase(nc, name) as ph:
        stats = ph.sb("stats", [P, TILES, 6])
        mv = ph.sb("mv", [P, TILES, 2])
        std = ph.sb("std", [P, TILES])
        rstd = ph.sb("rstd", [P, TILES])
        rows = ph.sb("rows", [P, 2, TPC, D])
        tr = ph.ps("tr", [P, 2, KD, CHUNK])
        (stats_ready, mv_ready, var_ready, std_ready, rstd_ready, rows_ready, transposed, high_ready,
         low_ready, stored0, stored1) = ph.sems("stats_ready mv_ready var_ready std_ready rstd_ready rows_ready "
                                                "transposed high_ready low_ready stored0 stored1")
        block = ph.block()

        @block.vector
        def _(dve):
            if norm:
                for t in range(TILES):
                    nc.vector.bn_stats(stats[:, t, :], SRC[:, t, :]).then_inc(stats_ready, 1)
                dve.wait_ge(stats_ready, TILES)
                for t in range(TILES):
                    nc.vector.bn_aggr(mv[:, t, :], stats[:, t, :]).then_inc(mv_ready, 1)
                dve.wait_ge(mv_ready, TILES)
                nc.vector.tensor_scalar(std[:], mv[:, :, 1], 1.0e-5, None, ALU.add).then_inc(var_ready, 1)
                dve.wait_ge(std_ready, 1)
                nc.vector.reciprocal(rstd[:], std[:]).then_inc(rstd_ready, 1)
                dve.wait_ge(rstd_ready, 1)
            give_credit(dve, rows_ready, low_ready)

            def make_rows(i, u):
                g = i * 2 + u
                dve.wait_ge(transposed, done(g - 2))
                if normed is not None:
                    dve.wait_ge((stored0, stored1)[u], (i + 1) * 16)
                for j in range(TPC):
                    if norm:
                        t = g * TPC + j
                        ins = nc.vector.tensor_scalar(rows[:, u, j, :], SRC[:, bass.ds(t, 1), :],
                                                      mv[:, bass.ds(t, 1), 0], rstd[:, bass.ds(t, 1)],
                                                      ALU.subtract, ALU.mult)
                    else:
                        ins = nc.vector.tensor_scalar(rows[:, u, j, :], SRC[:, bass.ds(g * TPC + j, 1), :],
                                                      1.0, None, ALU.mult)
                ins.then_inc(rows_ready, 1)

            def make_low(g, u):
                dve.wait_ge(high_ready, done(g))
                nc.vector.tensor_tensor(XL[:, :, bass.ds(g * CHUNK, CHUNK)], tr[:, u],
                                        XH[:, :, bass.ds(g * CHUNK, CHUNK)].bitcast(F32),
                                        ALU.subtract).then_inc(low_ready, 1)

            with dve.Fori(0, CHUNKS // 2) as i:
                for u in range(2):
                    make_rows(i, u)
                for u in range(2):
                    make_low(i * 2 + u, u)

        @block.tensor
        def _(pe):
            give_credit(pe, transposed)
            with pe.Fori(0, CHUNKS // 2) as i:
                for u in range(2):
                    g = i * 2 + u
                    pe.wait_ge(rows_ready, done(g))
                    pe.wait_ge(low_ready, done(g - 2))
                    for k in range(KD):
                        for j in range(TPC):
                            ins = nc.tensor.transpose(tr[:, u, k, j * P:(j + 1) * P],
                                                      rows[:, u, j, k * P:(k + 1) * P], ident[:])
                    ins.then_inc(transposed, 1)

        @block.scalar
        def _(act):
            if norm:
                act.wait_ge(var_ready, 1)
                nc.scalar.activation(std[:], std[:], ACT.Sqrt).then_inc(std_ready, 1)
            give_credit(act, high_ready)
            with act.Fori(0, CHUNKS // 2) as i:
                for u in range(2):
                    g = i * 2 + u
                    act.wait_ge(transposed, done(g))
                    act.wait_ge(high_ready, CREDIT)
                    nc.scalar.activation(XH[:, :, bass.ds(g * CHUNK, CHUNK)], tr[:, u], ACT.Copy)\
                        .then_inc(high_ready, 1)

        @block.sync
        def _(sp):
            if normed is None:
                return
            sp.sem_inc(stored0, 16)
            sp.sem_inc(stored1, 16)
            with sp.Fori(0, CHUNKS // 2) as i:
                for u in range(2):
                    g = i * 2 + u
                    sp.wait_ge(rows_ready, done(g))
                    sp.dma_start(normed[bass.ds(g * CHUNK, CHUNK), 0:D].rearrange("(t p) n -> p t n", p=P),
                                 rows[:, u]).then_inc((stored0, stored1)[u], 16)
            sp.wait_ge(stored0, 16 * (CHUNKS // 2 + 1))
            sp.wait_ge(stored1, 16 * (CHUNKS // 2 + 1))
AH, AD = 16, 16
HG = 4
UNITS = BATCH * AH // HG
TERMS = 3
QK_TERMS = ((0, 0), (0, 1), (1, 0), (1, 1), (0, 2), (2, 0))
ROWS_QK = len(QK_TERMS) * AD
ROWS_ALL = ROWS_QK + TERMS
VW = 32


def qkv_phase(nc, a, XH, XL, q_parts, k_parts, v_rows):
    with Phase(nc, "qkv") as ph:
        names = ("Q", "K", "V")
        raw = ph.sb("raw", [P, KD, 3, D])
        WH = ph.sb("WH", [P, KD, 3, D], F32R)
        WL = ph.sb("WL", [P, KD, 3, D], F32R)
        parts = ph.sb("parts", [P, 2, TERMS, CHUNK], BF16)
        rest = ph.sb("rest", [P, 2, CHUNK])
        vt = ph.sb("vt", [P, 2, AH, VW])
        PQ = ph.ps("PQ", [P, 2, CHUNK])
        PV = ph.ps("PV", [P, 2, 512])
        (w_in, wh_ready, wl_ready, projected, high, rest1, mid, low, stored, v_set, v_proj, v_copied,
         v_stored0, v_stored1, stored1) = ph.sems("w_in wh_ready wl_ready projected high rest1 mid low stored "
                                                  "v_set v_proj v_copied v_stored0 v_stored1 stored1")
        stored = (stored, stored1)
        v_stored = (v_stored0, v_stored1)
        block = ph.block()
        RUNS = [(w, m) for w in range(2) for m in range(2)]

        @block.sync
        def _(sp):
            for n, w in enumerate(names):
                sp.dma_start(raw[:, :, n, :], a[f"L0_attn_W_{w}"].rearrange("(k p) n -> p k n", p=P)).then_inc(w_in, 16)
            for s in stored:
                sp.sem_inc(s, 16)
            for r, (w, m) in enumerate(RUNS):
                dst = (q_parts, k_parts)[w]
                with sp.Fori(0, CHUNKS // 2) as i:
                    for u in range(2):
                        g = i * 2 + u
                        sp.wait_ge(low, done(g + r * CHUNKS))
                        sp.dma_start(dst[:, m * P:(m + 1) * P, bass.ds(g * CHUNK, CHUNK)]
                                     .rearrange("t p n -> p t n"), parts[:, u]).then_inc(stored[u], 16)
            for t in range(TILES):
                u = t % 2
                sp.wait_ge(v_copied, t + 1)
                sp.dma_start(v_rows[:, t * P:(t + 1) * P, :].rearrange("g p n -> p g n"),
                             vt[:, u].rearrange("p (g h) d -> p g (h d)", g=AH // HG)).then_inc(v_stored[u], 16)
            for u in range(2):
                sp.wait_ge(stored[u], 16 * (1 + len(RUNS) * CHUNKS // 2))
                sp.wait_ge(v_stored[u], 16 * TILES // 2)

        @block.scalar
        def _(act):
            act.wait_ge(w_in, 48)
            nc.scalar.activation(WH[:], raw[:], ACT.Copy).then_inc(wh_ready, 1)
            give_credit(act, high, mid)
            for r in range(len(RUNS)):
                with act.Fori(0, CHUNKS // 2) as i:
                    for u in range(2):
                        n = i * 2 + u + r * CHUNKS
                        act.wait_ge(stored[u], (i + r * CHUNKS // 2 + 1) * 16)
                        act.wait_ge(projected, done(n))
                        nc.scalar.activation(parts[:, u, 0], PQ[:, u], ACT.Copy).then_inc(high, 1)
                        act.wait_ge(rest1, done(n))
                        nc.scalar.activation(parts[:, u, 1], rest[:, u], ACT.Copy).then_inc(mid, 1)
            act.wait_ge(v_set, 2)
            for t in range(TILES):
                u = t % 2
                act.wait_ge(v_proj, t + 1)
                if t >= 2:
                    act.wait_ge(v_stored[u], 16 * (t // 2))
                nc.scalar.activation(vt[:, u, :, 0:AD], PV[:, u, 0:D].rearrange("p (h d) -> p h d", d=AD), ACT.Copy)\
                    .then_inc(v_copied, 1)

        @block.vector
        def _(dve):
            dve.wait_ge(wh_ready, 1)
            nc.vector.tensor_tensor(WL[:], raw[:], WH[:].bitcast(F32), ALU.subtract).then_inc(wl_ready, 1)
            nc.vector.memset(vt[:], 0.0).then_inc(v_set, 1)
            dve.wait_ge(v_set, 1)
            nc.vector.memset(vt[:, :, :, AD:AD + 1], 1.0).then_inc(v_set, 1)
            give_credit(dve, rest1, low)
            for r in range(len(RUNS)):
                with dve.Fori(0, CHUNKS // 2) as i:
                    for u in range(2):
                        n = i * 2 + u + r * CHUNKS
                        dve.wait_ge(high, done(n))
                        nc.vector.tensor_tensor(rest[:, u], PQ[:, u], parts[:, u, 0], ALU.subtract).then_inc(rest1, 1)
                        dve.wait_ge(mid, done(n))
                        nc.vector.tensor_tensor(parts[:, u, 2], rest[:, u], parts[:, u, 1], ALU.subtract)\
                            .then_inc(low, 1)

        @block.tensor
        def _(pe):
            pe.wait_ge(wl_ready, 1)
            give_credit(pe, projected)
            for r, (w, m) in enumerate(RUNS):
                with pe.Fori(0, CHUNKS // 2) as i:
                    for u in range(2):
                        g = i * 2 + u
                        pe.wait_ge(low, done(g + r * CHUNKS - 2))
                        s = 0
                        for W, x in ((WH, XH), (WH, XL), (WL, XH)):
                            for k in range(KD):
                                ins = nc.tensor.matmul(PQ[:, u], W[:, k, w, m * P:(m + 1) * P],
                                                       x[:, k, bass.ds(g * CHUNK, CHUNK)],
                                                       start=(s == 0), stop=(s == 3 * KD - 1))
                                s += 1
                        ins.then_inc(projected, 1)
            for t in range(TILES):
                u = t % 2
                if t >= 2:
                    pe.wait_ge(v_copied, t - 1)
                s = 0
                for x, W in ((XH, WH), (XL, WH), (XH, WL)):
                    for k in range(KD):
                        ins = nc.tensor.matmul(PV[:, u, 0:D], x[:, k, t * P:(t + 1) * P], W[:, k, 2, :],
                                               start=(s == 0), stop=(s == 3 * KD - 1))
                        s += 1
                ins.then_inc(v_proj, 1)


def score_phase(nc, q_parts, k_parts, v_rows, max_rows, AO, ident, identb, mask_q, mask_k):
    QT = SEQ // P
    SCALE = 1.0 / float(AD) ** 0.5
    PIECES = []
    for t in range(QT):
        for k0 in range(0, (t + 1) * P, CHUNK):
            nk = min(CHUNK, (t + 1) * P - k0)
            nh = {1: 4, 2: 2}.get(nk // P, 1)
            PIECES += [(t, k0, nk, h0, nh) for h0 in range(0, HG, nh)]
    GROUPS = ([[0], [1, 3], [2]], [[0, 1], [2, 3], [4, 5, 7], [6]])

    def span(half, kt):
        q0 = max(0, kt * P - half * CHUNK)
        return q0, CHUNK - q0

    def layout(half, group):
        at, out = 0, []
        for kt in group:
            q0, n = span(half, kt)
            if at % CHUNK and at % CHUNK + n > CHUNK:
                at = (at // CHUNK + 1) * CHUNK
            out.append((kt, q0, n, at))
            at += n
        return out, at

    STEPS = [(half, g) for half in range(2) for g in range(len(GROUPS[half]))]
    NS = len(STEPS) * HG
    NP = len(PIECES)
    assert NP % 2 == 0
    SHIFT = 25
    SLOTS = 4
    LAST = len(STEPS) - 1
    HALF0 = len(GROUPS[0])
    TURN = []
    NSTEPS = len(STEPS)
    for st in range(1, NSTEPS):
        TURN += [("scores", st, h) for h in range(HG)]
        TURN += [("values", st - 1, j) for j in range(len(GROUPS[STEPS[st - 1][0]][STEPS[st - 1][1]]))]
    TURN += [("scores", NSTEPS, 0), ("scores", NSTEPS, 1)]
    TURN += [("values", LAST, j) for j in range(len(GROUPS[1][-1]))]
    TURN += [("scores", NSTEPS, 2), ("scores", NSTEPS, 3)]

    def columns(kind, st, j):
        half, g = STEPS[st % NSTEPS]
        items, width = layout(half, GROUPS[half][g])
        return width if kind == "scores" else 4 * items[j][2]

    total = sum(columns(*part) for part in TURN)
    OUT = [NP * sum(columns(*part) for part in TURN[:i + 1]) // total for i in range(len(TURN))]
    ROWS_AT = TURN.index(("scores", HALF0 + 1, 2))
    HALF_AT = TURN.index(("values", HALF0 + 1, len(GROUPS[1][1]) - 1))
    assert OUT[ROWS_AT] > NP - SHIFT
    with Phase(nc, "score") as ph:
        QR = ph.sb("QR", [P, SLOTS, HG, SEQ], BF16)
        KR = ph.sb("KR", [P, SLOTS, HG, SEQ], BF16)
        V = ph.sb("V", [P, SLOTS, QT, HG, VW])
        pm = ph.sb("pm", [P, 2, HG, QT, 2])
        mx = ph.sb("mx", [P, QT, HG])
        mrest = ph.sb("mrest", [P, QT, HG])
        mparts = ph.sb("mparts", [P, QT, TERMS, HG], BF16)
        mrow = ph.sb("mrow", [TERMS * HG, SEQ], BF16)
        PR = ph.sb("PR", [P, 2, HG, 2 * CHUNK])
        OS = ph.sb("OS", [P, CHUNK])
        rc = ph.sb("rc", [P, TPC, HG, 1])
        minus_one = ph.sb("minus_one", [P, HG])
        SM = ph.ps("SM", [P, 2, CHUNK])
        SE = ph.ps("SE", [P, 2, 2 * CHUNK])
        PV = ph.ps("PV", [P, CHUNK])
        TR = ph.ps("TR", [P, CHUNK])
        TRB = TR[:].bitcast(BF16)
        loaded = [ph.sem(f"loaded{u}") for u in range(SLOTS)]
        m_in = [ph.sem(f"m_in{u}") for u in range(SLOTS)]
        (ones_set, rows_set, pe_m, dve_m, pm_done, mx_done, mh, mr1, mm, ml, m_tr, m_row, m_out,
         pe_s, act_p, pe_pv, act_o, pe_ot, dve_rc, dve_o) = ph.sems(
            "ones_set rows_set pe_m dve_m pm_done mx_done mh mr1 mm ml m_tr m_row m_out "
            "pe_s act_p pe_pv act_o pe_ot dve_rc dve_o")
        NLOAD = 2 * len(QK_TERMS) + 1
        block = ph.block()

        def turn_piece(u, k):
            ahead, p = divmod(NP + SHIFT + k, NP)
            return ahead, (u + ahead) % SLOTS, p

        @block.sync
        def _(sp):
            sp.sem_inc(m_out, 16)

            def load(n, u):
                b, hg = n // (AH // HG), n % (AH // HG)
                for j, (tq, tk) in enumerate(QK_TERMS):
                    for parts, t, dst in ((q_parts, tq, QR), (k_parts, tk, KR)):
                        src = parts[t, bass.ds(hg * HG * AD, HG * AD), bass.ds(b * SEQ, SEQ)]
                        sp.dma_start(dst[j * AD:(j + 1) * AD, u], src.rearrange("(h d) n -> d h n", d=AD))\
                            .then_inc(loaded[u], 16)
                sp.dma_start(V[:, u].rearrange("p t h d -> p t (h d)"),
                             v_rows[bass.ds(hg, 1), bass.ds(b * SEQ, SEQ), :].rearrange("o (t p) n -> p (o t) n", p=P))\
                    .then_inc(loaded[u], 16)

            def maxima(n, u):
                sp.wait_ge(m_row, done(n))
                sp.dma_start(max_rows, mrow[:]).then_inc(m_out, 16)
                sp.wait_ge(m_out, (n + 2) * 16)
                sp.dma_start(QR[ROWS_QK:ROWS_ALL, u], max_rows.rearrange("(t h) n -> t h n", t=TERMS))\
                    .then_inc(m_in[u], 16)

            for n in range(3):
                load(n, n)
            maxima(0, 0)
            with sp.Fori(0, UNITS // SLOTS) as i:
                for u in range(SLOTS):
                    n = i * SLOTS + u
                    sp.wait_ge(pe_pv, done(n * len(STEPS) - 1))
                    load((n + 3) % UNITS, (u + 3) % SLOTS)
                    maxima(n + 1, (u + 1) % SLOTS)
            for u in range(SLOTS):
                sp.wait_ge(loaded[u], 16 * NLOAD * (UNITS // SLOTS + (u < 3)))
                sp.wait_ge(m_in[u], 16 * (UNITS // SLOTS + (u < 1)))

        @block.gpsimd
        def _(pool):
            nc.gpsimd.memset(minus_one[:], -1.0).then_inc(ones_set, 1)
            pool.wait_ge(ones_set, 1)
            give_credit(pool, mx_done, mh, mr1, mm, ml)

            def max_parts(n, w):
                pool.wait_ge(pm_done, done(n))
                top = pm[:, w, :, :, 0].rearrange("p h t -> p t h")
                minus = minus_one[:].rearrange("p (o l) -> p o l", o=1).to_broadcast([P, QT, HG])
                nc.gpsimd.tensor_tensor(mx[:], top, minus, ALU.mult).then_inc(mx_done, 1)
                pool.wait_ge(m_tr, done(n - 1))
                nc.gpsimd.tensor_tensor(mparts[:, :, 0, :], top, minus, ALU.mult).then_inc(mh, 1)
                pool.wait_ge(mx_done, done(n))
                pool.wait_ge(mh, done(n))
                nc.gpsimd.tensor_tensor(mrest[:], mx[:], mparts[:, :, 0, :], ALU.subtract).then_inc(mr1, 1)
                nc.gpsimd.tensor_tensor(mparts[:, :, 1, :], mx[:], mparts[:, :, 0, :], ALU.subtract).then_inc(mm, 1)
                pool.wait_ge(mr1, done(n))
                pool.wait_ge(mm, done(n))
                nc.gpsimd.tensor_tensor(mparts[:, :, 2, :], mrest[:], mparts[:, :, 1, :], ALU.subtract)\
                    .then_inc(ml, 1)

            max_parts(0, 0)
            with pool.Fori(0, UNITS // SLOTS) as i:
                for u in range(SLOTS):
                    max_parts(i * SLOTS + u + 1, (u + 1) % 2)

        def score_columns(pe_out, lhs, rhs, diagonal, mask):
            ins = nc.tensor.matmul(pe_out, lhs, rhs, start=True, stop=diagonal is None)
            if diagonal is not None:
                ins = nc.tensor.matmul(diagonal, identb[:], mask[:], start=False, stop=True)
            return ins

        @block.tensor
        def _(pe):
            give_credit(pe, pe_m, m_tr, pe_s, pe_pv, pe_ot)

            def max_piece(count, u, p):
                t, k0, nk, h0, nh = PIECES[p]
                bank = p % 2
                pe.wait_ge(dve_m, done(count - 2))
                for j in range(nh):
                    end = (j + 1) * nk
                    diag = SM[:, bank, end - P:end] if k0 + nk == (t + 1) * P else None
                    ins = score_columns(SM[:, bank, end - nk:end], QR[0:ROWS_QK, u, h0 + j, t * P:(t + 1) * P],
                                        KR[0:ROWS_QK, u, h0 + j, k0:k0 + nk], diag, mask_q)
                ins.then_inc(pe_m, 1)

            def max_rows_out(n):
                pe.wait_ge(ml, done(n))
                for t in range(QT):
                    ins = nc.tensor.transpose(TRB[0:TERMS * HG, t * P:(t + 1) * P],
                                              mparts[:, t].rearrange("p a h -> p (a h)"), identb[:])
                ins.then_inc(m_tr, 1)

            def scores(n, u, s, h):
                half, g = STEPS[s]
                e = s * HG + h
                pe.wait_ge(act_p, done(n * NS + e - 2))
                items, _ = layout(half, GROUPS[half][g])
                for kt, q0, nq, at in items:
                    q = half * CHUNK + q0
                    cols = SE[:, e % 2, at:at + nq]
                    diag = SE[:, e % 2, at:at + P] if q == kt * P else None
                    ins = score_columns(cols, KR[0:ROWS_ALL, u, h, kt * P:(kt + 1) * P],
                                        QR[0:ROWS_ALL, u, h, q:q + nq], diag, mask_k)
                ins.then_inc(pe_s, 1)

            def values(n, u, s, j):
                half, g = STEPS[s]
                if j == 0:
                    if g == 0:
                        pe.wait_ge(act_o, done(2 * n + half - 1))
                    pe.wait_ge(act_p, done(n * NS + (s + 1) * HG - 1))
                items, _ = layout(half, GROUPS[half][g])
                last = g == len(GROUPS[half]) - 1
                kt, q0, nq, at = items[j]
                for h in range(HG):
                    ins = nc.tensor.matmul(PV[VW * h:VW * (h + 1), q0:q0 + nq], V[:, u, kt, h, :],
                                           PR[:, (u + s) % 2, h, at:at + nq], start=(g == 0 and j == 0),
                                           stop=(last and j == len(items) - 1), skip_group_check=True)
                if j == len(items) - 1:
                    ins.then_inc(pe_pv, 1)

            def outputs(n, half):
                pe.wait_ge(act_o, done(2 * n + half))
                pe.wait_ge(dve_o, done(2 * n + half - 1))
                if half == 0:
                    pe.wait_ge(m_row, done(n + 1))
                for t in range(TPC):
                    ins = nc.tensor.transpose(TR[:, t * P:(t + 1) * P], OS[:, t * P:(t + 1) * P], ident[:])
                ins.then_inc(pe_ot, 1)

            pe.wait_ge(loaded[0], 16 * NLOAD)
            pe.wait_ge(rows_set, 1)
            for g in range(NP + SHIFT):
                if g == NP:
                    pe.wait_ge(loaded[1], 16 * NLOAD)
                max_piece(g, g // NP, g % NP)
                if g == NP + SHIFT // 3:
                    max_rows_out(0)
            pe.wait_ge(m_in[0], 16)
            for h in range(HG):
                scores(0, 0, 0, h)
            with pe.Fori(0, UNITS // SLOTS) as i:
                for u in range(SLOTS):
                    n = i * SLOTS + u
                    k = 0
                    for at, (kind, s, j) in enumerate(TURN):
                        if kind == "values":
                            values(n, u, s, j)
                        elif s < NSTEPS:
                            scores(n, u, s, j)
                        else:
                            if j == 0:
                                pe.wait_ge(m_in[(u + 1) % SLOTS], (i + 1 + (u + 1) // SLOTS) * 16)
                            scores(n + 1, (u + 1) % SLOTS, 0, j)
                        while k < OUT[at]:
                            ahead, slot, p = turn_piece(u, k)
                            if ahead == 2 and p == 0:
                                pe.wait_ge(loaded[slot], (i + 1 + (u + 2) // SLOTS) * (16 * NLOAD))
                            max_piece((n + 1) * NP + SHIFT + k, slot, p)
                            k += 1
                        if at == ROWS_AT:
                            pe.wait_ge(dve_o, done(2 * n - 1))
                            max_rows_out(n + 1)
                        if at == HALF_AT:
                            outputs(n, 0)
                    outputs(n, 1)

        @block.scalar
        def _(act):
            act.preload_act_table(ACT.Exp)
            give_credit(act, act_p, act_o, m_row)

            def exps(n, u, s, h):
                half, g = STEPS[s]
                e = s * HG + h
                items, width = layout(half, GROUPS[half][g])
                act.wait_ge(pe_pv, done(n * len(STEPS) + s - 2))
                act.wait_ge(pe_s, done(n * NS + e))
                nc.scalar.activation(PR[:, (u + s) % 2, h, 0:width], SE[:, e % 2, 0:width], ACT.Exp, scale=SCALE)\
                    .then_inc(act_p, 1)

            def copy_out(n, half):
                act.wait_ge(pe_ot, done(2 * n + half - 1))
                act.wait_ge(pe_pv, done(n * len(STEPS) + (HALF0 if half == 0 else len(STEPS)) - 1))
                nc.scalar.activation(OS[:], PV[:], ACT.Copy).then_inc(act_o, 1)

            def max_row(n):
                act.wait_ge(m_tr, done(n))
                act.wait_ge(m_out, (n + 1) * 16)
                nc.scalar.activation(mrow[:], TRB[0:TERMS * HG, :], ACT.Copy).then_inc(m_row, 1)

            max_row(0)
            for h in range(HG):
                exps(0, 0, 0, h)
            with act.Fori(0, UNITS // SLOTS) as i:
                for u in range(SLOTS):
                    n = i * SLOTS + u
                    for s in range(1, len(STEPS)):
                        if s == HALF0 + 1:
                            copy_out(n, 0)
                        for h in range(HG):
                            exps(n, u, s, h)
                        if s == HALF0 + 1:
                            max_row(n + 1)
                    for h in range(HG):
                        exps(n + 1, u + 1, 0, h)
                        if h == 0:
                            copy_out(n, 1)

        @block.vector
        def _(dve):
            give_credit(dve, dve_m, pm_done, dve_rc, dve_o)

            def max_piece(count, w, p):
                t, k0, nk, h0, nh = PIECES[p]
                dve.wait_ge(pe_m, done(count))
                nc.vector.tensor_reduce(pm[:, w, h0:h0 + nh, t, k0 // CHUNK],
                                        SM[:, p % 2, 0:nh * nk].rearrange("p (h k) -> p h k", h=nh), AX.X,
                                        ALU.max).then_inc(dve_m, 1)

            def join_pieces(n, w):
                dve.wait_ge(dve_m, done((n + 1) * NP - 1))
                nc.vector.tensor_tensor(pm[:, w, :, QT // 2:QT, 0], pm[:, w, :, QT // 2:QT, 0],
                                        pm[:, w, :, QT // 2:QT, 1], ALU.max).then_inc(pm_done, 1)

            def normalise(n, half):
                tr = TR[:].rearrange("p (t h d) -> p t h d", t=TPC, h=HG)
                dve.wait_ge(pe_ot, done(2 * n + half))
                nc.vector.reciprocal(rc[:], tr[:, :, :, AD:AD + 1]).then_inc(dve_rc, 1)
                dve.wait_ge(dve_rc, done(2 * n + half))
                for t in range(TPC):
                    b, hg = n // (AH // HG), n % (AH // HG)
                    dst = AO[:, bass.ds(b * QT + half * TPC + t, 1), bass.ds(hg * HG * AD, HG * AD)]
                    ins = nc.vector.tensor_tensor(dst.rearrange("p o (h d) -> p (o h) d", d=AD), tr[:, t, :, 0:AD],
                                                  rc[:, t].to_broadcast([P, HG, AD]), ALU.mult)
                ins.then_inc(dve_o, 1)

            nc.vector.memset(KR[ROWS_QK:P], 1.0).then_inc(rows_set, 1)
            for g in range(NP + SHIFT):
                max_piece(g, g // NP % 2, g % NP)
                if g == NP - 1:
                    join_pieces(0, 0)
            with dve.Fori(0, UNITS // SLOTS) as i:
                for u in range(SLOTS):
                    n = i * SLOTS + u
                    for k in range(NP):
                        ahead, slot, p = turn_piece(u, k)
                        if ahead == 2 and p == 0:
                            dve.wait_ge(ml, done(n))
                        max_piece((n + 1) * NP + SHIFT + k, slot % 2, p)
                        if p == NP - 1:
                            join_pieces(n + 1, slot % 2)
                        if k == OUT[HALF_AT] - 1:
                            normalise(n, 0)
                    normalise(n, 1)


def output_phase(nc, w_o, X, XH, XL):
    with Phase(nc, "proj") as ph:
        raw = ph.sb("raw", [P, KD, D])
        WH = ph.sb("WH", [P, KD, D], F32R)
        WL = ph.sb("WL", [P, KD, D], F32R)
        Y = ph.ps("Y", [P, 2, 512])
        w_in, wh_ready, wl_ready, made, added = ph.sems("w_in wh_ready wl_ready made added")
        block = ph.block()

        @block.sync
        def _(sp):
            sp.dma_start(raw[:], w_o.rearrange("(k p) n -> p k n", p=P)).then_inc(w_in, 16)

        @block.scalar
        def _(act):
            act.wait_ge(w_in, 16)
            nc.scalar.activation(WH[:], raw[:], ACT.Copy).then_inc(wh_ready, 1)

        @block.tensor
        def _(pe):
            pe.wait_ge(wl_ready, 1)
            for t in range(TILES):
                if t >= 2:
                    pe.wait_ge(added, t - 1)
                s = 0
                for x, W in ((XH, WH), (XL, WH), (XH, WL)):
                    for k in range(KD):
                        ins = nc.tensor.matmul(Y[:, t % 2, 0:D], x[:, k, t * P:(t + 1) * P], W[:, k, :],
                                               start=(s == 0), stop=(s == 3 * KD - 1))
                        s += 1
                ins.then_inc(made, 1)

        @block.vector
        def _(dve):
            dve.wait_ge(wh_ready, 1)
            nc.vector.tensor_tensor(WL[:], raw[:], WH[:].bitcast(F32), ALU.subtract).then_inc(wl_ready, 1)
            for t in range(TILES):
                dve.wait_ge(made, t + 1)
                nc.vector.tensor_tensor(X[:, t, :], Y[:, t % 2, 0:D], X[:, t, :], ALU.add).then_inc(added, 1)


def attention_layer(nc, a, X, ident, identb, mask_q, mask_k):
    q_parts = nc.dram_tensor("q_parts", (TERMS, D, T), BF16, kind="Internal").ap()
    k_parts = nc.dram_tensor("k_parts", (TERMS, D, T), BF16, kind="Internal").ap()
    v_rows = nc.dram_tensor("v_rows", (AH // HG, T, HG * VW), F32, kind="Internal").ap()
    max_rows = nc.dram_tensor("max_rows", (TERMS * HG, SEQ), BF16, kind="Internal").ap()
    with ExitStack() as c:
        XH = c.enter_context(nc.sbuf_tensor("A_XH", [P, KD, T], F32R))
        XL = c.enter_context(nc.sbuf_tensor("A_XL", [P, KD, T], F32R))
        transpose_phase(nc, "lnA", X, XH, XL, ident, True)
        qkv_phase(nc, a, XH, XL, q_parts, k_parts, v_rows)
    with ExitStack() as c:
        AO = c.enter_context(nc.sbuf_tensor("AO", [P, TILES, D], F32))
        score_phase(nc, q_parts, k_parts, v_rows, max_rows, AO, ident, identb, mask_q, mask_k)
        XH = c.enter_context(nc.sbuf_tensor("A2_XH", [P, KD, T], F32R))
        XL = c.enter_context(nc.sbuf_tensor("A2_XL", [P, KD, T], F32R))
        transpose_phase(nc, "trA", AO, XH, XL, ident, False)
        output_phase(nc, a["L0_attn_W_O"], X, XH, XL)
EXPERTS, LAT, INTER, SHARED = 32, 128, 128, 512
GROUPS_E, PER_GROUP, TOP_GROUPS, TOP_K = 4, 8, 2, 8
ROUTED_SCALE = 2.5
SB = SHARED // P
CWR = TERMS * EXPERTS


def shared_phase(nc, a, X, XH, XL, LH, LL, scores):
    NW = LAT + SHARED
    with Phase(nc, "shared") as ph:
        raw = ph.sb("raw", [P, KD, NW])
        WH = ph.sb("WH", [P, KD, NW], F32R)
        WL = ph.sb("WL", [P, KD, NW], F32R)
        graw = ph.sb("graw", [P, KD, EXPERTS])
        GH = ph.sb("GH", [P, KD, EXPERTS], F32R)
        GL = ph.sb("GL", [P, KD, EXPERTS], F32R)
        down = ph.sb("down", [P, SB, D])
        r = ph.sb("r", [P, 2, CHUNK])
        su = ph.sb("su", [P, 2, SB, CHUNK])
        HP = ph.ps("HP", [P, 3, CHUNK])
        OP = ph.ps("OP", [P, 2, 512])
        LG = ph.ps("LG", [P, TILES, EXPERTS])
        (w_in, wh_ready, wl_ready, pe_l, pe_h, act_lh, dve_ll, act_r, act_su, pe_o, dve_x, pe_lg,
         act_lg) = ph.sems("w_in wh_ready wl_ready pe_l pe_h act_lh dve_ll act_r act_su pe_o dve_x pe_lg act_lg")
        block = ph.block()

        @block.sync
        def _(sp):
            sp.dma_start(raw[:, :, 0:LAT], a["L0_ffn_fc1_w"].rearrange("(k p) n -> p k n", p=P)).then_inc(w_in, 16)
            sp.dma_start(raw[:, :, LAT:NW], a["L0_ffn_shared_up_w"].rearrange("(k p) n -> p k n", p=P))\
                .then_inc(w_in, 16)
            sp.dma_start(graw[:], a["L0_ffn_gate_w"].rearrange("(k p) n -> p k n", p=P)).then_inc(w_in, 16)
            sp.dma_start(down[:], a["L0_ffn_shared_down_w"].rearrange("(s p) n -> p s n", p=P)).then_inc(w_in, 16)

        @block.scalar
        def _(act):
            act.wait_ge(w_in, 64)
            nc.scalar.activation(WH[:], raw[:], ACT.Copy).then_inc(wh_ready, 1)
            nc.scalar.activation(GH[:], graw[:], ACT.Copy).then_inc(wh_ready, 1)
            give_credit(act, act_lh, act_r, act_su)

            def first(g, u, slot_used):
                act.wait_ge(pe_l, done(g))
                act.wait_ge(act_lh, CREDIT)
                nc.scalar.activation(LH[:, bass.ds(g * CHUNK, CHUNK)], HP[:, 2], ACT.Copy).then_inc(act_lh, 1)
                for s in range(SB):
                    n = g * SB + s
                    act.wait_ge(pe_h, done(n))
                    nc.scalar.activation(r[:, s % 2], HP[:, s % 2], ACT.Relu).then_inc(act_r, 1)
                    if slot_used:
                        act.wait_ge(pe_o, done((g - 1) * TPC - 1))
                    act.wait_ge(act_r, done(n))
                    nc.scalar.activation(su[:, u, s], r[:, s % 2], ACT.Square).then_inc(act_su, 1)

            first(0, 0, False)
            first(1, 1, False)
            with act.Fori(1, CHUNKS // 2) as i:
                for u in range(2):
                    first(i * 2 + u, u, True)
            act.wait_ge(pe_lg, 1)
            nc.scalar.activation(scores[:], LG[:], ACT.Sigmoid).then_inc(act_lg, 1)

        @block.tensor
        def _(pe):
            pe.wait_ge(wl_ready, 2)
            give_credit(pe, pe_l, pe_h, pe_o)

            def first_product(bank, c0, g):
                n = 0
                for W, x in ((WH, XH), (WH, XL), (WL, XH)):
                    for k in range(KD):
                        ins = nc.tensor.matmul(HP[:, bank], W[:, k, c0:c0 + P], x[:, k, bass.ds(g * CHUNK, CHUNK)],
                                               start=(n == 0), stop=(n == 3 * KD - 1))
                        n += 1
                return ins

            def first(g):
                pe.wait_ge(dve_ll, done(g - 1))
                first_product(2, 0, g).then_inc(pe_l, 1)
                for s in range(SB):
                    pe.wait_ge(act_r, done(g * SB + s - 2))
                    first_product(s % 2, LAT + s * P, g).then_inc(pe_h, 1)

            def second(g, u):
                pe.wait_ge(act_su, done(g * SB + SB - 1))
                for t in range(TPC):
                    pe.wait_ge(dve_x, done(g * TPC + t - 2))
                    for s in range(SB):
                        ins = nc.tensor.matmul(OP[:, t % 2, 0:D], su[:, u, s, t * P:(t + 1) * P], down[:, s, :],
                                               start=(s == 0), stop=(s == SB - 1))
                    ins.then_inc(pe_o, 1)

            first(0)
            with pe.Fori(0, CHUNKS // 2 - 1) as i:
                for u in range(2):
                    first(i * 2 + u + 1)
                    second(i * 2 + u, u)
            first(CHUNKS - 1)
            second(CHUNKS - 2, 0)
            second(CHUNKS - 1, 1)
            for t in range(TILES):
                n = 0
                for x, W in ((XH, GH), (XL, GH), (XH, GL)):
                    for k in range(KD):
                        ins = nc.tensor.matmul(LG[:, t, :], x[:, k, t * P:(t + 1) * P], W[:, k, :],
                                               start=(n == 0), stop=(n == 3 * KD - 1))
                        n += 1
            ins.then_inc(pe_lg, 1)

        @block.vector
        def _(dve):
            dve.wait_ge(wh_ready, 2)
            nc.vector.tensor_tensor(WL[:], raw[:], WH[:].bitcast(F32), ALU.subtract).then_inc(wl_ready, 1)
            nc.vector.tensor_tensor(GL[:], graw[:], GH[:].bitcast(F32), ALU.subtract).then_inc(wl_ready, 1)
            give_credit(dve, dve_ll, dve_x)

            def latent_low(g):
                cols = bass.ds(g * CHUNK, CHUNK)
                dve.wait_ge(act_lh, done(g))
                nc.vector.tensor_tensor(LL[:, cols], HP[:, 2], LH[:, cols].bitcast(F32), ALU.subtract)\
                    .then_inc(dve_ll, 1)

            def add(g):
                for t in range(TPC):
                    dve.wait_ge(pe_o, done(g * TPC + t))
                    xt = X[:, bass.ds(g * TPC + t, 1), :]
                    nc.vector.tensor_tensor(xt, OP[:, t % 2:t % 2 + 1, 0:D], xt, ALU.add).then_inc(dve_x, 1)

            latent_low(0)
            with dve.Fori(0, CHUNKS - 1) as g:
                latent_low(g + 1)
                add(g)
            add(CHUNKS - 1)


def group_routing_phase(nc, a, scores, CWT, identb, W1H, W1L, W2H, W2L, pick):
    E, G, N = EXPERTS, GROUPS_E, PER_GROUP
    QE = 8
    LOADS = [(w, e) for w in range(2) for e in range(0, E, QE)]
    bias = a["L0_ffn_gate_bias"]
    TAKEN = -3.0e38
    with Phase(nc, "route") as ph:
        bias_b = ph.sb("bias", [P, 1, E])
        sb_ = ph.sb("biased", [P, TILES, E])
        hi1 = ph.sb("hi1", [P, TILES * G, 4])
        lo1 = ph.sb("lo1", [P, TILES * G, 4])
        hi2 = ph.sb("hi2", [P, TILES * G, 2])
        lo2 = ph.sb("lo2", [P, TILES * G, 2])
        t2 = ph.sb("t2", [P, TILES * G, 2])
        u2 = ph.sb("u2", [P, TILES * G, 2])
        hi3 = ph.sb("hi3", [P, TILES * G, 1])
        lo3 = ph.sb("lo3", [P, TILES * G, 1])
        gs = ph.sb("gs", [P, TILES, G])
        beats = ph.sb("beats", [P, TILES, G, G - 1])
        rank = ph.sb("rank", [P, TILES, G])
        gm = ph.sb("gm", [P, TILES * G, 1])
        pen = ph.sb("pen", [P, TILES * G, 1])
        masked = ph.sb("masked", [P, TILES, E])
        top = ph.sb("top", [P, TILES, 8])
        left = ph.sb("left", [P, TILES, E])
        w = ph.sb("w", [P, TILES, E])
        total = ph.sb("total", [P, TILES, 1])
        rest = ph.sb("rest", [P, TILES, E])
        parts = ph.sb("parts", [P, TILES, TERMS, E], BF16)
        raw = ph.sb("raw", [P, 2, QE, P])
        TB = ph.ps("TB", [CWR, 4, 1024], BF16)
        (b_in, chain, parts_ready, transposed, copied, w_in0, w_in1, w_high, w_low, zero, picked) = ph.sems(
            "b_in chain parts_ready transposed copied w_in0 w_in1 w_high w_low zero picked")
        w_in = (w_in0, w_in1)
        block = ph.block()

        @block.sync
        def _(sp):
            sp.dma_start(bias_b[:, 0, :], bias.rearrange("(o e) -> o e", o=1).to_broadcast([P, E])).then_inc(b_in, 16)
            views = (a["L0_ffn_w1"].rearrange("e l i -> l e i"), a["L0_ffn_w2"].rearrange("e i l -> i e l"))
            for n, (w, e) in enumerate(LOADS):
                if n >= 2:
                    sp.wait_ge(w_low, n - 1)
                sp.dma_start(raw[:, n % 2], views[w][:, e:e + QE, :]).then_inc(w_in[n % 2], 16)

        @block.gpsimd
        def _(pool):
            nc.gpsimd.memset(pick[:], 0.0).then_inc(zero, 1)
            pool.wait_ge(zero, 1)
            for j in range(TERMS):
                rows = pick[j * E:(j + 1) * E]
                nc.gpsimd.affine_select(out=rows, in_=rows, compare_op=ALU.not_equal, fill=1.0, base=0,
                                        pattern=[[-1, E], [0, P]], channel_multiplier=1).then_inc(picked, 1)
            pool.wait_ge(picked, TERMS)
            for n, (w, e) in enumerate(LOADS):
                high, low = ((W1H, W1L), (W2H, W2L))[w]
                pool.wait_ge(w_high, n + 1)
                nc.gpsimd.tensor_tensor(low[:, e:e + QE, :], raw[:, n % 2], high[:, e:e + QE, :].bitcast(F32),
                                        ALU.subtract).then_inc(w_low, 1)

        @block.vector
        def _(dve):
            n = [0]

            def step(ins):
                n[0] += 1
                ins.then_inc(chain, 1)
                dve.wait_ge(chain, n[0])

            tt = nc.vector.tensor_tensor
            dve.wait_ge(b_in, 16)
            step(tt(sb_[:], scores[:], bias_b[:].to_broadcast([P, TILES, E]), ALU.add))
            v = sb_[:].rearrange("p t (g n) -> p (t g) n", g=G)
            step(tt(hi1[:], v[:, :, 0:4], v[:, :, 4:8], ALU.max))
            step(tt(lo1[:], v[:, :, 0:4], v[:, :, 4:8], ALU.min))
            for hi, lo, hi_n, lo_n, m in ((hi1, lo1, hi2, lo2, 2), (hi2, lo2, hi3, lo3, 1)):
                step(tt(hi_n[:], hi[:, :, 0:m], hi[:, :, m:2 * m], ALU.max))
                step(tt(t2[:, :, 0:m], hi[:, :, 0:m], hi[:, :, m:2 * m], ALU.min))
                step(tt(u2[:, :, 0:m], lo[:, :, 0:m], lo[:, :, m:2 * m], ALU.max))
                step(tt(lo_n[:], t2[:, :, 0:m], u2[:, :, 0:m], ALU.max))
            step(tt(gs[:].rearrange("p t g -> p (t g)"), hi3[:, :, 0], lo3[:, :, 0], ALU.add))
            for g in range(G):
                own = gs[:, :, g:g + 1]
                if g:
                    step(tt(beats[:, :, g, 0:g], gs[:, :, 0:g], own.to_broadcast([P, TILES, g]), ALU.is_ge))
                if g < G - 1:
                    step(tt(beats[:, :, g, g:G - 1], gs[:, :, g + 1:G], own.to_broadcast([P, TILES, G - 1 - g]),
                            ALU.is_gt))
            step(nc.vector.tensor_reduce(rank[:], beats[:], AX.X, ALU.add))
            r2 = rank[:].rearrange("p t (g o) -> p (t g) o", o=1)
            step(nc.vector.tensor_scalar(gm[:], r2, float(TOP_GROUPS), None, ALU.is_lt))
            step(nc.vector.tensor_scalar(pen[:], gm[:], 1.0, -NEG, ALU.subtract, ALU.mult))
            mv = masked[:].rearrange("p t (g n) -> p (t g) n", g=G)
            step(tt(mv, v, gm[:].to_broadcast([P, TILES * G, N]), ALU.mult))
            step(tt(mv, mv, pen[:].to_broadcast([P, TILES * G, N]), ALU.add))
            for t in range(TILES):
                ins = nc.vector.max(top[:, t, :], masked[:, t, :])
            step(ins)
            for t in range(TILES):
                ins = nc.vector.match_replace(left[:, t, :], top[:, t, :], masked[:, t, :], TAKEN)
            step(ins)
            step(nc.vector.tensor_scalar(left[:], left[:], TAKEN, None, ALU.is_equal))
            step(tt(w[:], scores[:], left[:], ALU.mult))
            step(nc.vector.tensor_reduce(total[:, :, 0], w[:], AX.X, ALU.add))
            step(nc.vector.reciprocal(total[:], total[:]))
            step(nc.vector.tensor_scalar(total[:], total[:], ROUTED_SCALE, None, ALU.mult))
            step(tt(w[:], w[:], total[:].to_broadcast([P, TILES, E]), ALU.mult))
            step(nc.vector.tensor_copy(parts[:, :, 0, :], w[:]))
            step(tt(rest[:], w[:], parts[:, :, 0, :], ALU.subtract))
            step(nc.vector.tensor_copy(parts[:, :, 1, :], rest[:]))
            tt(parts[:, :, 2, :], rest[:], parts[:, :, 1, :], ALU.subtract).then_inc(parts_ready, 1)

        @block.tensor
        def _(pe):
            pe.wait_ge(parts_ready, 1)
            for t in range(TILES):
                ins = nc.tensor.transpose(TB[:, t // 8, (t % 8) * P:(t % 8 + 1) * P],
                                          parts[:, t].rearrange("p s e -> p (s e)"), identb[:])
                if t % 8 == 7:
                    ins.then_inc(transposed, 1)

        @block.scalar
        def _(act):
            for n, (w, e) in enumerate(LOADS):
                act.wait_ge(w_in[n % 2], 16 * (n // 2 + 1))
                nc.scalar.activation((W1H, W2H)[w][:, e:e + QE, :], raw[:, n % 2], ACT.Copy).then_inc(w_high, 1)
            for j in range(4):
                act.wait_ge(transposed, j + 1)
                nc.scalar.activation(CWT[:, j * 1024:(j + 1) * 1024], TB[:, j], ACT.Copy).then_inc(copied, 1)


def experts_phase(nc, a, X, LH, LL, CWT, W1H, W1L, W2H, W2L, pick):
    E = EXPERTS
    AHEAD = 4
    SLOTS = 3

    def before(n, e):
        return n - (2 if e < 2 else SLOTS)

    with Phase(nc, "experts") as ph:
        fc2 = ph.sb("fc2", [P, D])
        r = ph.sb("r", [P, 2, CHUNK])
        sq = ph.sb("sq", [P, 2, CHUNK])
        h = ph.sb("h", [P, 2, CHUNK])
        hh = ph.sb("hh", [P, SLOTS, CHUNK], F32R)
        hl = ph.sb("hl", [P, SLOTS, CHUNK], F32R)
        y = ph.sb("y", [P, CHUNK])
        HP = ph.ps("HP", [P, SLOTS, CHUNK])
        CW = ph.ps("CW", [P, SLOTS, CHUNK])
        Y = ph.ps("Y", [P, CHUNK])
        OP = ph.ps("OP", [P, 2, D])
        (w_in, y_set, pe_h, pe_cw, act_r, act_sq, dve_h, act_hh, dve_hl, pe_y, act_y, pe_o, dve_x) = ph.sems(
            "w_in y_set pe_h pe_cw act_r act_sq dve_h act_hh dve_hl pe_y act_y pe_o dve_x")
        block = ph.block()
        COPY_AT, OUT_AFTER = AHEAD - 2, (1, 4)

        @block.sync
        def _(sp):
            sp.dma_start(fc2[:], a["L0_ffn_fc2_w"]).then_inc(w_in, 16)

        @block.scalar
        def _(act):
            give_credit(act, act_r, act_sq, act_hh, act_y)

            def relu(n, e):
                act.wait_ge(act_sq, done(n - 2))
                act.wait_ge(pe_h, done(n))
                nc.scalar.activation(r[:, e % 2], HP[:, e % SLOTS], ACT.Relu).then_inc(act_r, 1)

            def square(n, e):
                act.wait_ge(dve_h, done(n - 2))
                act.wait_ge(act_r, done(n))
                nc.scalar.activation(sq[:, e % 2], r[:, e % 2], ACT.Square).then_inc(act_sq, 1)

            def high(n, e):
                act.wait_ge(pe_y, done(before(n, e)))
                act.wait_ge(dve_h, done(n))
                nc.scalar.activation(hh[:, e % SLOTS], h[:, e % 2], ACT.Copy).then_inc(act_hh, 1)

            def copy_y(g):
                act.wait_ge(pe_o, done(2 * g - 1))
                act.wait_ge(pe_y, done(g * E - 1))
                nc.scalar.activation(y[:], Y[:], ACT.Copy).then_inc(act_y, 1)

            relu(0, 0)
            act.wait_ge(y_set, 1)
            with act.Fori(0, CHUNKS) as g:
                for e in range(E):
                    n = g * E + e
                    relu(n + 1, (e + 1) % E)
                    square(n, e)
                    if e == COPY_AT:
                        copy_y(g)
                    if e:
                        high(n - 1, e - 1)
                high(g * E + E - 1, E - 1)
            copy_y(CHUNKS)

        @block.tensor
        def _(pe):
            give_credit(pe, pe_h, pe_cw, pe_y, pe_o)

            def up(n, e, g):
                cols = bass.ds(g * CHUNK, CHUNK)
                s = e % SLOTS
                pe.wait_ge(act_r, done(before(n, e)))
                nc.tensor.matmul(HP[:, s], W1H[:, e, :], LH[:, cols], start=True, stop=False)
                nc.tensor.matmul(HP[:, s], W1H[:, e, :], LL[:, cols], start=False, stop=False)
                nc.tensor.matmul(HP[:, s], W1L[:, e, :], LH[:, cols], start=False, stop=True).then_inc(pe_h, 1)
                pe.wait_ge(dve_h, done(before(n, e)))
                nc.tensor.matmul(CW[:, s], pick[:, e, :], CWT[:, cols], start=True, stop=True).then_inc(pe_cw, 1)

            def down(n, e):
                s = e % SLOTS
                pe.wait_ge(dve_hl, done(n))
                nc.tensor.matmul(Y[:], W2H[:, e, :], hh[:, s], start=(e == 0), stop=False)
                nc.tensor.matmul(Y[:], W2L[:, e, :], hh[:, s], start=False, stop=False)
                nc.tensor.matmul(Y[:], W2H[:, e, :], hl[:, s], start=False, stop=(e == E - 1)).then_inc(pe_y, 1)

            def out(n, half):
                pe.wait_ge(dve_x, done(n - 1))
                for j in range(2):
                    t = 2 * half + j
                    ins = nc.tensor.matmul(OP[:, j, :], y[:, t * P:(t + 1) * P], fc2[:], start=True, stop=True)
                ins.then_inc(pe_o, 1)

            for e in range(AHEAD):
                up(e, e, 0)
            pe.wait_ge(w_in, 16)
            with pe.Fori(0, CHUNKS) as g:
                for e in range(E):
                    n, ahead = g * E + e, (e + AHEAD) % E
                    up(n + AHEAD, ahead, g if e + AHEAD < E else (g + 1) % CHUNKS)
                    if e == 0:
                        pe.wait_ge(act_y, done(g))
                    down(n, e)
                    if e in OUT_AFTER:
                        half = OUT_AFTER.index(e)
                        out(2 * g + half, half)
            pe.wait_ge(act_y, done(CHUNKS))
            for half in range(2):
                out(2 * CHUNKS + half, half)

        @block.vector
        def _(dve):
            nc.vector.memset(Y[:], 0.0).then_inc(y_set, 1)
            give_credit(dve, dve_h, dve_hl, dve_x)

            def weigh(n, e):
                dve.wait_ge(dve_hl, done(n - 2))
                dve.wait_ge(pe_cw, done(n))
                dve.wait_ge(act_sq, done(n))
                nc.vector.tensor_tensor(h[:, e % 2], sq[:, e % 2], CW[:, e % SLOTS], ALU.mult).then_inc(dve_h, 1)

            def low(n, e):
                dve.wait_ge(act_hh, done(n))
                nc.vector.tensor_tensor(hl[:, e % SLOTS], h[:, e % 2], hh[:, e % SLOTS].bitcast(F32), ALU.subtract)\
                    .then_inc(dve_hl, 1)

            def add(n, g, half):
                dve.wait_ge(pe_o, done(n))
                xt = X[:, bass.ds(g * TPC + 2 * half, 2), :]
                nc.vector.tensor_tensor(xt, OP[:], xt, ALU.add).then_inc(dve_x, 1)

            with dve.Fori(0, CHUNKS) as g:
                for e in range(E):
                    weigh(g * E + e, e)
                    if e:
                        low(g * E + e - 1, e - 1)
                    if e - SLOTS in OUT_AFTER:
                        half = OUT_AFTER.index(e - SLOTS)
                        add(2 * g + half, (g + CHUNKS - 1) % CHUNKS, half)
                low(g * E + E - 1, E - 1)
            dve.sem_inc(dve_h, AHEAD - SLOTS)
            for half in range(2):
                add(2 * CHUNKS + half, CHUNKS - 1, half)


def latent_moe_layer(nc, a, X, ident, identb):
    with ExitStack() as c:
        LH = c.enter_context(nc.sbuf_tensor("B_LH", [P, T], F32R))
        LL = c.enter_context(nc.sbuf_tensor("B_LL", [P, T], F32R))
        CWT = c.enter_context(nc.sbuf_tensor("B_CWT", [CWR, T], BF16))
        scores = c.enter_context(nc.sbuf_tensor("B_scores", [P, TILES, EXPERTS], F32))
        with ExitStack() as c2:
            XH = c2.enter_context(nc.sbuf_tensor("B_XH", [P, KD, T], F32R))
            XL = c2.enter_context(nc.sbuf_tensor("B_XL", [P, KD, T], F32R))
            transpose_phase(nc, "lnB", X, XH, XL, ident, True)
            shared_phase(nc, a, X, XH, XL, LH, LL, scores)
        W1H, W1L, W2H, W2L = (c.enter_context(nc.sbuf_tensor(f"B_{n}", [P, EXPERTS, P], F32R))
                              for n in ("W1H", "W1L", "W2H", "W2L"))
        pick = c.enter_context(nc.sbuf_tensor("B_pick", [CWR, EXPERTS, P], BF16))
        group_routing_phase(nc, a, scores, CWT, identb, W1H, W1L, W2H, W2L, pick)
        experts_phase(nc, a, X, LH, LL, CWT, W1H, W1L, W2H, W2L, pick)
def linear_attention_phase(nc, X, XH, XL, ident, w_qkv, w_gate, w_out, rms_w, decays, kdec, bdec):
    H, DH, BLK = LH, 128, LBLK
    NBLK = SEQ // BLK
    HD = H * DH
    B4 = BATCH
    with Phase(nc, "lin") as ph:
        raw = ph.sb("raw", [P, 4, KD, DH])
        WH = ph.sb("WH", [P, 4, KD, DH], F32R)
        WL = ph.sb("WL", [P, 4, KD, DH], F32R)
        wo_raw = ph.sb("wo_raw", [P, D])
        WO = ph.sb("WO", [P, D])
        rms = ph.sb("rms", [P, H])
        dec_in = ph.sb("dec_in", [P, 2, BLK])
        dec = ph.sb("dec", [P, 2, BLK])
        ones = ph.sb("ones", [P, 2])
        acc = ph.sb("acc", [P, TILES, D])
        o2sum = ph.sb("o2sum", [P, NBLK, B4, BLK])
        rs = ph.sb("rs", [P, TILES])
        qT = ph.sb("qT", [P, 2, B4, BLK])
        kT = ph.sb("kT", [P, 2, B4, BLK])
        vT = ph.sb("vT", [P, B4, BLK])
        v = ph.sb("v", [P, B4, DH])
        gT = ph.sb("gT", [P, 2, B4, BLK])
        qd = ph.sb("qd", [P, B4, BLK])
        sd = ph.sb("sd", [P, B4, BLK])
        kd = ph.sb("kd", [P, B4, DH])
        kv = ph.sb("kv", [P, B4, DH])
        o2 = ph.sb("o2", [P, B4, BLK])
        go = ph.sb("go", [P, 2, B4, BLK])
        PJ = ph.ps("PJ", [P, 2, B4, P])
        S = ph.ps("S", [P, B4, P])
        KT = ph.ps("KT", [P, B4, P])
        O = ph.ps("O", [P, B4, P])
        OUT = ph.ps("OUT", [P, 2, 2, D])
        VT = ph.ps("VT", [P, B4, P])
        (w_in, wo_in, rms_in, dec_loaded, dec_ready, wh_ready, wl_ready, wo_ready, memsets, sum_set,
         pe_q, pe_k, pe_v, pe_g, pe_vt, pe_s, pe_kt, pe_o, pe_kv, pe_out0, pe_out1, pe_sum,
         act_q, act_k, act_v, act_g, act_vt, act_sq, pool_qd, pool_sum,
         dve_sd, dve_kd, dve_kv, dve_go, dve_acc0, dve_acc1, mean_ready, root_ready, rs_ready) = ph.sems(
            "w_in wo_in rms_in dec_loaded dec_ready wh_ready wl_ready wo_ready memsets sum_set "
            "pe_q pe_k pe_v pe_g pe_vt pe_s pe_kt pe_o pe_kv pe_out0 pe_out1 pe_sum "
            "act_q act_k act_v act_g act_vt act_sq pool_qd pool_sum "
            "dve_sd dve_kd dve_kv dve_go dve_acc0 dve_acc1 mean_ready root_ready rs_ready")
        pe_out = (pe_out0, pe_out1)
        dve_acc = (dve_acc0, dve_acc1)
        xh = XH[:].rearrange("p k (b c l) -> p k b c l", b=B4, c=NBLK)
        xl = XL[:].rearrange("p k (b c l) -> p k b c l", b=B4, c=NBLK)
        acc_v = acc[:].rearrange("p (b c) n -> p b c n", b=B4)
        wqkv_v = w_qkv.rearrange("(k p) n -> p k n", p=P)
        wg_v = w_gate.rearrange("(k p) n -> p k n", p=P)
        Q, K, V, G = range(4)
        PAIRS = (slice(0, 2), slice(2, 4))
        block = ph.block()

        @block.sync
        def _(sp):
            sp.dma_start(rms[:], rms_w.rearrange("(h p) -> p h", p=P), allow_slow_non_contiguous=True).then_inc(rms_in, 16)

            def load_head(h):
                for w in range(3):
                    sp.dma_start(raw[:, w], wqkv_v[:, :, bass.ds(h * DH + w * HD, DH)]).then_inc(w_in, 16)
                sp.dma_start(raw[:, G], wg_v[:, :, bass.ds(h * DH, DH)]).then_inc(w_in, 16)
                sp.dma_start(wo_raw[:], w_out[bass.ds(h * DH, DH), :]).then_inc(wo_in, 16)

            def load_decays(h):
                sp.dma_start(dec_in[:], decays[bass.ds(h, 1)].rearrange("o p w l -> p (o w) l")).then_inc(dec_loaded, 16)

            load_head(0)
            load_decays(0)
            with sp.Fori(0, H - 1) as h:
                sp.wait_ge(dec_ready, h + 1)
                load_decays(h + 1)
                sp.wait_ge(wl_ready, 2 * (h + 1))
                sp.wait_ge(wo_ready, h + 1)
                load_head(h + 1)
            sp.wait_ge(wl_ready, 2 * H)
            sp.wait_ge(wo_ready, H)
            load_head(0)
            sp.wait_ge(w_in, 64 * (H + 1))
            sp.wait_ge(wo_in, 16 * (H + 1))

        @block.gpsimd
        def _(pool):
            nc.gpsimd.memset(o2sum[:], 0.0).then_inc(sum_set, 1)
            pool.wait_ge(sum_set, 1)
            give_credit(pool, pool_qd, pool_sum)
            with pool.Fori(0, H) as h:
                for c in range(NBLK):
                    i, u = h * NBLK + c, c % 2
                    pool.wait_ge(act_q, done(i))
                    pool.wait_ge(pe_o, done(i - 1))
                    if c == 0:
                        pool.wait_ge(dec_ready, h + 1)
                    nc.gpsimd.tensor_tensor(qd[:], qT[:, u],
                                            dec[:, 0:1, :].to_broadcast([P, B4, BLK]), ALU.mult).then_inc(pool_qd, 1)
                    pool.wait_ge(act_sq, done(i))
                    pool.wait_ge(pool_sum, done(i - 1))
                    nc.gpsimd.tensor_tensor(o2sum[:, c], o2sum[:, c], o2[:], ALU.add).then_inc(pool_sum, 1)

        @block.scalar
        def _(act):
            act.preload_act_table(ACT.Silu)
            give_credit(act, act_q, act_k, act_v, act_g, act_vt, act_sq)

            def weights_high(load):
                act.wait_ge(w_in, (load + 1) * 64)
                act.wait_ge(pe_g, done(load * NBLK - 1))
                for pair in PAIRS:
                    nc.scalar.activation(WH[:, pair], raw[:, pair], ACT.Copy).then_inc(wh_ready, 1)

            def qk(n, u):
                act.wait_ge(pe_out1, done(n - 2))
                act.wait_ge(pool_qd, done(n - 2))
                act.wait_ge(pe_q, done(n))
                nc.scalar.activation(qT[:, u], PJ[:, 0], ACT.Silu).then_inc(act_q, 1)
                act.wait_ge(pe_k, done(n))
                nc.scalar.activation(kT[:, u], PJ[:, 1], ACT.Silu).then_inc(act_k, 1)

            def vg(n, u):
                act.wait_ge(pe_v, done(n))
                nc.scalar.activation(vT[:], PJ[:, 0], ACT.Silu).then_inc(act_v, 1)
                act.wait_ge(dve_go, done(n - 2))
                act.wait_ge(pe_g, done(n))
                nc.scalar.activation(gT[:, u], PJ[:, 1], ACT.Tanh, scale=0.5).then_inc(act_g, 1)
                act.wait_ge(pe_vt, done(n))
                nc.scalar.activation(v[:], VT[:], ACT.Copy).then_inc(act_vt, 1)

            def square(i):
                act.wait_ge(pe_o, done(i))
                act.wait_ge(pool_sum, done(i - 1))
                nc.scalar.activation(o2[:], O[:], ACT.Square).then_inc(act_sq, 1)

            weights_high(0)
            qk(0, 0)
            vg(0, 0)
            with act.Fori(0, H) as h:
                for c in range(NBLK):
                    i, u = h * NBLK + c, c % 2
                    if c < NBLK - 1:
                        qk(i + 1, 1 - u)
                        square(i)
                    else:
                        weights_high(h + 1)
                        square(i)
                        qk(i + 1, 1 - u)
                    vg(i + 1, 1 - u)
            act.wait_ge(mean_ready, 1)
            nc.scalar.activation(rs[:], rs[:], ACT.Sqrt).then_inc(root_ready, 1)

        @block.tensor
        def _(pe):
            give_credit(pe, pe_q, pe_k, pe_v, pe_g, pe_vt, pe_s, pe_kt, pe_o, pe_kv, pe_out0, pe_out1)

            def project(bank, w, c, sem):
                n = 0
                for a, x in ((WH, xh), (WH, xl), (WL, xh)):
                    for k in range(KD):
                        ins = nc.tensor.matmul(PJ[:, bank], a[:, w, k, :], x[:, k, :, c, :],
                                               start=(n == 0), stop=(n == 3 * KD - 1))
                        n += 1
                ins.then_inc(sem, 1)

            def project_qk(n, c, load):
                if c == 0:
                    pe.wait_ge(wl_ready, 2 * load + 1)
                pe.wait_ge(act_v, done(n - 1))
                project(0, Q, c, pe_q)
                pe.wait_ge(act_g, done(n - 1))
                project(1, K, c, pe_k)

            def project_vg(n, c, load):
                if c == 0:
                    pe.wait_ge(wl_ready, 2 * load + 2)
                pe.wait_ge(act_q, done(n))
                project(0, V, c, pe_v)
                pe.wait_ge(act_k, done(n))
                project(1, G, c, pe_g)
                pe.wait_ge(act_v, done(n))
                pe.wait_ge(act_vt, done(n - 1))
                for b in range(B4):
                    ins = nc.tensor.transpose(VT[:, b, :], vT[:, b, :], ident[:])
                ins.then_inc(pe_vt, 1)

            def output(i, u, h):
                pe.wait_ge(dve_go, done(i))
                pe.wait_ge(wo_ready, h + 1)
                for half in range(2):
                    pe.wait_ge(dve_acc[half], done(i - 1))
                    for b in range(2):
                        ins = nc.tensor.matmul(OUT[:, half, b, :], go[:, u, 2 * half + b, :], WO[:],
                                               start=True, stop=True)
                    ins.then_inc(pe_out[half], 1)

            project_qk(0, 0, 0)
            project_vg(0, 0, 0)
            with pe.Fori(0, H) as h:
                for c in range(NBLK):
                    i, u = h * NBLK + c, c % 2
                    pe.wait_ge(act_k, done(i))
                    pe.wait_ge(dve_sd, done(i - 1))
                    for b in range(B4):
                        ins = nc.tensor.matmul(S[:, b, :], kT[:, u, b, :], qT[:, u, b, :], start=True, stop=True)
                    ins.then_inc(pe_s, 1)
                    if c == 0:
                        pe.wait_ge(dve_kd, done(i - 1))
                    else:
                        pe.wait_ge(dve_kv, h * (NBLK - 1) + c)
                    for b in range(B4):
                        ins = nc.tensor.transpose(KT[:, b, :], kT[:, u, b, :], ident[:])
                    ins.then_inc(pe_kt, 1)
                    if c < NBLK - 1:
                        project_qk(i + 1, c + 1, h)
                    pe.wait_ge(act_vt, done(i))
                    pe.wait_ge(dve_sd, done(i))
                    pe.wait_ge(pool_qd, done(i))
                    pe.wait_ge(dve_go, done(i - 1))
                    for b in range(B4):
                        ins = nc.tensor.matmul(O[:, b, :], v[:, b, :], sd[:, b, :], start=True, stop=(c == 0))
                        if c:
                            ins = nc.tensor.matmul(O[:, b, :], kv[:, b, :], qd[:, b, :], start=False, stop=True)
                    ins.then_inc(pe_o, 1)
                    pe.wait_ge(dve_kd, done(i))
                    if c < NBLK - 1:
                        for b in range(B4):
                            ins = nc.tensor.matmul(KT[:, b, :], kd[:, b, :], v[:, b, :], start=True, stop=True)
                        ins.then_inc(pe_kv, 1)
                        project_vg(i + 1, c + 1, h)
                        output(i, u, h)
                    else:
                        project_qk(i + 1, 0, h + 1)
                        output(i, u, h)
                        project_vg(i + 1, 0, h + 1)
            pe.wait_ge(memsets, 2)
            pe.wait_ge(pool_sum, done(H * NBLK - 1))
            pe.wait_ge(act_vt, done(H * NBLK))
            VS = VT[:].rearrange("p b l -> p (b l)")
            for b in range(B4):
                for c in range(NBLK):
                    t = b * NBLK + c
                    ins = nc.tensor.matmul(VS[:, t:t + 1], o2sum[:, c, b, :], ones[:, 0:1], start=True, stop=True)
            ins.then_inc(pe_sum, 1)

        @block.vector
        def _(dve):
            nc.vector.memset(acc[:], 0.0).then_inc(memsets, 1)
            nc.vector.memset(ones[:], 1.0).then_inc(memsets, 1)
            dve.wait_ge(memsets, 2)
            dve.wait_ge(rms_in, 16)
            give_credit(dve, dve_sd, dve_kd, dve_go, dve_acc0, dve_acc1)

            def weights_low(load, part):
                dve.wait_ge(wh_ready, 2 * load + part + 1)
                pair = PAIRS[part]
                nc.vector.tensor_tensor(WL[:, pair], raw[:, pair], WH[:, pair].bitcast(F32), ALU.subtract)\
                    .then_inc(wl_ready, 1)

            def weights_out(load, rms_col):
                dve.wait_ge(wo_in, (load + 1) * 16)
                nc.vector.tensor_scalar(WO[:], wo_raw[:], rms_col, 0.5, ALU.mult, ALU.mult).then_inc(wo_ready, 1)

            weights_low(0, 0)
            weights_low(0, 1)
            weights_out(0, rms[:, 0:1])
            with dve.Fori(0, H) as h:
                for c in range(NBLK):
                    i, u = h * NBLK + c, c % 2
                    if c == 0:
                        dve.wait_ge(pool_qd, done(i - 1))
                        dve.wait_ge(dve_sd, done(i - 1))
                        dve.wait_ge(dec_loaded, (h + 1) * 16)
                        nc.vector.tensor_scalar(dec[:], dec_in[:], 1.0, None, ALU.mult).then_inc(dec_ready, 1)
                        dve.wait_ge(dec_ready, h + 1)
                    dve.wait_ge(pe_s, done(i))
                    dve.wait_ge(pe_o, done(i - 1))
                    nc.vector.tensor_tensor(sd[:], S[:], dec[:, 1:2, :].to_broadcast([P, B4, BLK]),
                                            ALU.mult).then_inc(dve_sd, 1)
                    dve.wait_ge(pe_kt, done(i))
                    if c > 0:
                        dve.wait_ge(pe_kv, done(h * (NBLK - 1) + c - 1))
                    nc.vector.tensor_scalar(kd[:], KT[:], kdec[:, bass.ds(h, 1)], None, ALU.mult)\
                        .then_inc(dve_kd, 1)
                    if c < NBLK - 1:
                        dve.wait_ge(pe_kv, done(h * (NBLK - 1) + c))
                        if c == 0:
                            nc.vector.tensor_copy(kv[:], KT[:]).then_inc(dve_kv, 1)
                        else:
                            dve.wait_ge(dve_kv, h * (NBLK - 1) + c)
                            nc.vector.scalar_tensor_tensor(kv[:], kv[:], bdec[:, bass.ds(h, 1)], KT[:],
                                                           ALU.mult, ALU.add).then_inc(dve_kv, 1)
                    else:
                        weights_low(h + 1, 0)
                        weights_low(h + 1, 1)
                    dve.wait_ge(act_sq, done(i))
                    dve.wait_ge(act_g, done(i))
                    dve.wait_ge(pe_out1, done(i - 2))
                    nc.vector.scalar_tensor_tensor(go[:, u], gT[:, u], 1.0, O[:], ALU.add, ALU.mult)\
                        .then_inc(dve_go, 1)
                    for half in range(2):
                        dve.wait_ge(pe_out[half], done(i))
                        dve.wait_ge(dve_acc[half], done(i - 1))
                        dst = acc_v[:, 2 * half:2 * half + 2, c, :]
                        nc.vector.tensor_tensor(dst, OUT[:, half], dst, ALU.add).then_inc(dve_acc[half], 1)
                    if c == NBLK - 1:
                        weights_out(h + 1, rms[:, bass.ds((h + 1) % H, 1)])
            dve.wait_ge(pe_sum, 1)
            nc.vector.tensor_scalar(rs[:], VT[:].rearrange("p b l -> p (b l)")[:, 0:TILES], 1.0 / HD, 1.0e-6,
                                    ALU.mult, ALU.add).then_inc(mean_ready, 1)
            dve.wait_ge(root_ready, 1)
            nc.vector.reciprocal(rs[:], rs[:]).then_inc(rs_ready, 1)
            dve.wait_ge(rs_ready, 1)
            for t in range(TILES):
                nc.vector.scalar_tensor_tensor(X[:, t, :], acc[:, t, :], rs[:, t:t + 1], X[:, t, :],
                                               ALU.mult, ALU.add)


def linear_attention_layer(nc, a, X, ident, decays, kdec, bdec):
    with ExitStack() as c:
        XH = c.enter_context(nc.sbuf_tensor("C_XH", [P, KD, T], F32R))
        XL = c.enter_context(nc.sbuf_tensor("C_XL", [P, KD, T], F32R))
        transpose_phase(nc, "lnC", X, XH, XL, ident, True)
        linear_attention_phase(nc, X, XH, XL, ident, a["L1_attn_w_qkv"], a["L1_attn_w_gate"],
                               a["L1_attn_w_out"], a["L1_attn_rms_weight"], decays, kdec, bdec)
KEPT, OLD, WIDTH, CAP, TOP_D = 48, 128, 96, 96, 8
ROW = D + KEPT
SLOTS = 4


def logits_phase(nc, a, XH, XL, ident, lg, known):
    with Phase(nc, "logit") as ph:
        raw = ph.sb("raw", [P, KD, OLD])
        GH = ph.sb("GH", [P, KD, OLD], F32R)
        GL = ph.sb("GL", [P, KD, OLD], F32R)
        o2n = ph.sb("o2n", [P, 1], I32)
        spread = ph.sb("spread", [P, P])
        pen = ph.sb("pen", [P, 1, OLD])
        LG = ph.ps("LG", [P, 4, TPC, OLD])
        PN = ph.ps("PN", [P, OLD])
        (g_in, known_ready, spread_ready, pen_part, pen_ready, pe_pn, gh_ready, gl_ready, pe_lg, masked) = ph.sems(
            "g_in known_ready spread_ready pen_part pen_ready pe_pn gh_ready gl_ready pe_lg masked")
        block = ph.block()

        @block.sync
        def _(sp):
            sp.dma_start(o2n[:], a["L1_ffn_old_to_new"].rearrange("(p o) -> p o", o=1)).then_inc(g_in, 16)
            sp.dma_start(raw[:], a["L1_ffn_gate_weight"].rearrange("(k p) n -> p k n", p=P)).then_inc(g_in, 16)

        @block.scalar
        def _(act):
            act.wait_ge(g_in, 32)
            nc.scalar.activation(GH[:], raw[:], ACT.Copy).then_inc(gh_ready, 1)

        @block.tensor
        def _(pe):
            pe.wait_ge(spread_ready, 1)
            nc.tensor.transpose(PN[:], spread[:], ident[:]).then_inc(pe_pn, 1)
            pe.wait_ge(gl_ready, 1)
            for g in range(CHUNKS):
                if g >= 4:
                    pe.wait_ge(masked, g - 3)
                for t in range(TPC):
                    tok = (g * TPC + t) * P
                    n = 0
                    for x, W in ((XH, GH), (XL, GH), (XH, GL)):
                        for k in range(KD):
                            ins = nc.tensor.matmul(LG[:, g % 4, t, :], x[:, k, tok:tok + P], W[:, k, :],
                                                   start=(n == 0), stop=(n == 3 * KD - 1))
                            n += 1
                ins.then_inc(pe_lg, 1)

        @block.vector
        def _(dve):
            dve.wait_ge(g_in, 32)
            nc.vector.tensor_copy(known[:], o2n[:]).then_inc(known_ready, 1)
            dve.wait_ge(known_ready, 1)
            nc.vector.tensor_scalar(pen[:, 0, 0:1], known[:], -1.0, NEG, ALU.is_equal, ALU.mult).then_inc(pen_part, 1)
            dve.wait_ge(pen_part, 1)
            nc.vector.tensor_copy(spread[:], pen[:, 0, 0:1].to_broadcast([P, P])).then_inc(spread_ready, 1)
            dve.wait_ge(gh_ready, 1)
            nc.vector.tensor_tensor(GL[:], raw[:], GH[:].bitcast(F32), ALU.subtract).then_inc(gl_ready, 1)
            dve.wait_ge(pe_pn, 1)
            nc.vector.tensor_copy(pen[:, 0, :], PN[:]).then_inc(pen_ready, 1)
            dve.wait_ge(pen_ready, 1)
            for g in range(CHUNKS):
                dve.wait_ge(pe_lg, g + 1)
                nc.vector.tensor_tensor(lg[:, g * TPC:(g + 1) * TPC, :], LG[:, g % 4],
                                        pen[:].to_broadcast([P, TPC, OLD]), ALU.add).then_inc(masked, 1)


def kept_router_phase(nc, a, X, lg, known, ident, identb, rows, out, idx):
    with Phase(nc, "keep") as ph:
        cols_i = ph.sb("cols_i", [P, KEPT], I32)
        cols = ph.sb("cols", [P, KEPT])
        perm = ph.sb("perm", [P, KEPT])
        permb = ph.sb("permb", [P, KEPT], BF16)
        stat = ph.sb("stat", [P, TILES, 1])
        top = ph.sb("top", [P, TILES, 8])
        left = ph.sb("left", [P, TILES, OLD])
        sel = ph.sb("sel", [P, TILES, OLD], BF16)
        wT = ph.sb("wT", [P, 2, CHUNK])
        sT = ph.sb("sT", [P, 2, CHUNK], BF16)
        w = ph.sb("w", [P, TILES, KEPT])
        down_i = ph.sb("down_i", [KEPT, T], I32)
        val = ph.sb("val", [KEPT, 2, T])
        first = ph.sb("first", [KEPT, CAP])
        slot_i = ph.sb("slot_i", [CAP, 1], I32)
        slot = ph.sb("slot", [CAP, 1])
        unused = ph.sb("unused", [CAP, KEPT])
        tok = ph.sb("tok", [CAP, KEPT])
        zero = ph.sb("zero", [SPARE, ROW])
        WT = ph.ps("WT", [P, 2, CHUNK])
        ST = ph.ps("ST", [P, 2, 2 * CHUNK], BF16)
        WN = ph.ps("WN", [P, TPC, OLD])
        SN = ph.ps("SN", [KEPT, 2, CHUNK])
        LT = ph.ps("LT", [CAP, KEPT])
        (iotas, chain, e_ready, act_e, w_ready, pe_t, act_w, act_s, pe_wn, pe_sn, dve_wn, dve_sn, list_ready, pe_lt,
         stored, zeroed) = ph.sems(
            "iotas chain e_ready act_e w_ready pe_t act_w act_s pe_wn pe_sn dve_wn dve_sn list_ready pe_lt "
            "stored zeroed")
        block = ph.block()

        @block.sync
        def _(sp):
            sp.dma_start(out[0:T, :].rearrange("(t p) n -> p t n", p=P), X[:]).then_inc(stored, 16)
            sp.wait_ge(zeroed, 1)
            sp.dma_start(out[T:T + SPARE, :], zero[:, 0:D]).then_inc(stored, 16)
            sp.dma_start(rows[T:T + SPARE, :], zero[:]).then_inc(stored, 16)
            sp.wait_ge(dve_wn, CHUNKS)
            sp.dma_start(rows[0:T, D:ROW].rearrange("(t p) n -> p t n", p=P), w[:]).then_inc(stored, 16)
            sp.wait_ge(stored, 64)

        @block.gpsimd
        def _(pool):
            nc.gpsimd.iota(cols_i[:], [[1, KEPT]], base=0, channel_multiplier=0).then_inc(iotas, 1)
            nc.gpsimd.iota(slot_i[:], [[0, 1]], base=0, channel_multiplier=1).then_inc(iotas, 1)
            nc.gpsimd.memset(zero[:], 0.0).then_inc(zeroed, 1)
            nc.gpsimd.iota(down_i[:], [[-1, T]], base=T, channel_multiplier=0).then_inc(iotas, 1)

        @block.tensor
        def _(pe):
            pe.wait_ge(w_ready, 1)
            for g in range(CHUNKS + 1):
                if g < CHUNKS:
                    b = g % 2
                    if g >= 2:
                        pe.wait_ge(act_s, g - 1)
                    for t in range(TPC):
                        nc.tensor.transpose(WT[:, b, t * P:(t + 1) * P], left[:, g * TPC + t, :], ident[:])
                        ins = nc.tensor.transpose(ST[:, b, t * P:(t + 1) * P], sel[:, g * TPC + t, :], identb[:])
                    ins.then_inc(pe_t, 1)
                if g >= 1:
                    q, b = g - 1, (g - 1) % 2
                    pe.wait_ge(act_s, q + 1)
                    if q >= 1:
                        pe.wait_ge(dve_wn, q)
                    for t in range(TPC):
                        ins = nc.tensor.matmul(WN[:, t, 0:KEPT], wT[:, b, t * P:(t + 1) * P], perm[:],
                                               start=True, stop=True)
                    ins.then_inc(pe_wn, 1)
                    if q >= 2:
                        pe.wait_ge(dve_sn, q - 1)
                    nc.tensor.matmul(SN[:, b, :], permb[:], sT[:, b, :], start=True, stop=True).then_inc(pe_sn, 1)
            pe.wait_ge(list_ready, 1)
            nc.tensor.transpose(LT[:], first[:], ident[0:KEPT, 0:KEPT]).then_inc(pe_lt, 1)

        @block.scalar
        def _(act):
            act.wait_ge(e_ready, 1)
            nc.scalar.activation(lg[:], lg[:], ACT.Exp).then_inc(act_e, 1)
            for g in range(CHUNKS):
                act.wait_ge(pe_t, g + 1)
                if g >= 2:
                    act.wait_ge(pe_sn, g - 1)
                nc.scalar.activation(wT[:, g % 2], WT[:, g % 2], ACT.Copy).then_inc(act_w, 1)
                nc.scalar.activation(sT[:, g % 2], ST[:, g % 2, 0:CHUNK], ACT.Copy).then_inc(act_s, 1)

        @block.vector
        def _(dve):
            n = [0]

            def step(ins):
                n[0] += 1
                ins.then_inc(chain, 1)
                dve.wait_ge(chain, n[0])

            tt, ts = nc.vector.tensor_tensor, nc.vector.tensor_scalar
            wide = [P, TILES, OLD]
            step(nc.vector.tensor_reduce(stat[:, :, 0], lg[:], AX.X, ALU.max))
            tt(lg[:], lg[:], stat[:].to_broadcast(wide), ALU.subtract).then_inc(e_ready, 1)
            dve.wait_ge(iotas, 3)
            step(nc.vector.tensor_copy(cols[:], cols_i[:]))
            step(nc.vector.tensor_copy(slot[:], slot_i[:]))
            step(ts(perm[:], cols[:], known[:, 0:1], None, ALU.is_equal))
            step(nc.vector.tensor_copy(permb[:], perm[:]))
            dve.wait_ge(act_e, 1)
            step(nc.vector.tensor_reduce(stat[:, :, 0], lg[:], AX.X, ALU.add))
            step(nc.vector.reciprocal(stat[:], stat[:]))
            step(tt(lg[:], lg[:], stat[:].to_broadcast(wide), ALU.mult))
            for t in range(TILES):
                ins = nc.vector.max(top[:, t, :], lg[:, t, :])
            step(ins)
            for t in range(TILES):
                ins = nc.vector.match_replace(left[:, t, :], top[:, t, :], lg[:, t, :], -1.0)
            step(ins)
            step(nc.vector.tensor_reduce(stat[:, :, 0], top[:], AX.X, ALU.add))
            step(nc.vector.reciprocal(stat[:], stat[:]))
            step(ts(sel[:], left[:], 0.0, None, ALU.is_lt))
            step(tt(left[:], lg[:], sel[:], ALU.mult))
            tt(left[:], left[:], stat[:].to_broadcast(wide), ALU.mult).then_inc(w_ready, 1)
            for g in range(CHUNKS):
                dve.wait_ge(pe_wn, g + 1)
                nc.vector.tensor_copy(w[:, g * TPC:(g + 1) * TPC, :], WN[:, :, 0:KEPT]).then_inc(dve_wn, 1)
                dve.wait_ge(pe_sn, g + 1)
                tt(val[:, 0, g * CHUNK:(g + 1) * CHUNK], SN[:, g % 2], down_i[:, g * CHUNK:(g + 1) * CHUNK], ALU.mult)\
                    .then_inc(dve_sn, 1)
            dve.wait_ge(dve_sn, CHUNKS)
            for r in range(CAP // 8):
                step(nc.vector.max(first[:, 8 * r:8 * r + 8], val[:, r % 2]))
                if r < CAP // 8 - 1:
                    step(nc.vector.match_replace(val[:, 1 - r % 2], first[:, 8 * r:8 * r + 8], val[:, r % 2], 0.0))
            dve.sem_inc(list_ready, 1)
            dve.wait_ge(pe_lt, 1)
            step(ts(unused[:], LT[:], 0.0, slot[:, 0:1], ALU.is_equal, ALU.mult))
            step(ts(tok[:], LT[:], -1.0, float(T), ALU.mult, ALU.add))
            tt(idx[:], tok[:], unused[:], ALU.add)


def kept_experts_phase(nc, a, rows, out, idx, ident):
    gu = a["L1_ffn_gate_up_proj"]
    dn = a["L1_ffn_down_proj"]
    S = SLOTS
    with Phase(nc, "kept") as ph:
        GU = ph.sb("GU", [P, S, KD, 2 * WIDTH])
        DN = ph.sb("DN", [WIDTH, S, D])
        ix = ph.sb("ix", [CAP, S, 1], U32)
        xg = ph.sb("xg", [CAP, S, ROW])
        xT = ph.sb("xT", [P, 2, KD, CAP])
        sg = ph.sb("sg", [WIDTH, 2, CAP])
        h = ph.sb("h", [WIDTH, 2, CAP])
        ys = ph.sb("ys", [CAP, S, D])
        XT = ph.ps("XT", [P, 2, 512])
        GP = ph.ps("GP", [WIDTH, 2, 512])
        YP = ph.ps("YP", [CAP, 2, 512])
        w_in = [ph.sem(f"w_in{u}") for u in range(S)]
        g_in = [ph.sem(f"g_in{u}") for u in range(S)]
        (ix_ready, pe_x, act_x, pe_gu, act_g, dve_h, pe_y, dve_y, added, pool_turns, slot_free) = ph.sems(
            "ix_ready pe_x act_x pe_gu act_g dve_h pe_y dve_y added pool_turns slot_free")
        block = ph.block()

        @block.sync
        def _(sp):
            def load(e, u):
                sp.dma_start(GU[:, u], gu[bass.ds(e, 1)].rearrange("e (k p) n -> p (e k) n", p=P)).then_inc(w_in[u], 16)
                sp.dma_start(DN[:, u], dn[bass.ds(e, 1)].rearrange("e i n -> i (e n)")).then_inc(w_in[u], 16)

            for u in range(S):
                load(u, u)
            with sp.Fori(0, KEPT // S - 1) as i:
                for u in range(S):
                    sp.wait_ge(pe_y, done(i * S + u))
                    load((i + 1) * S + u, u)

        @block.gpsimd
        def _(pool):
            def gather(e, u):
                pool.wait_ge(ix_ready, done(e))
                pool.sem_inc(pool_turns, 1)
                nc.gpsimd.indirect_dma_start(out=xg[:, u], out_offset=None, in_=rows,
                                             in_offset=bass.IndirectOffsetOnAxis(ap=ix[:, u], axis=0))\
                    .then_inc(g_in[u], 16)

            def scatter(e, u):
                pool.wait_ge(dve_y, done(e))
                pool.sem_inc(pool_turns, 1)
                nc.gpsimd.indirect_dma_start(out=out, out_offset=bass.IndirectOffsetOnAxis(ap=ix[:, u], axis=0),
                                             in_=ys[:, u], in_offset=None, compute_op=ALU.add).then_inc(added, 16)
                pool.wait_ge(added, (e + 1) * 16)
                pool.sem_inc(slot_free, 1)

            give_credit(pool, slot_free)
            gather(0, 0)
            gather(1, 1)
            with pool.Fori(0, KEPT // S) as i:
                for u in range(S):
                    e = i * S + u
                    gather(e + 2, (u + 2) % S)
                    scatter(e, u)
            pool.wait_ge(added, 16 * KEPT)
            pool.wait_ge(g_in[0], 16 * (KEPT // S + 1))
            pool.wait_ge(g_in[1], 16 * (KEPT // S + 1))

        @block.tensor
        def _(pe):
            give_credit(pe, pe_x, pe_gu, pe_y)

            def turn(e, u):
                b = u % 2
                pe.wait_ge(act_x, done(e - 2))
                for k in range(KD):
                    ins = nc.tensor.transpose(XT[:, b, k * CAP:(k + 1) * CAP], xg[:, u, k * P:(k + 1) * P],
                                              ident[0:CAP, 0:CAP])
                ins.then_inc(pe_x, 1)

            def products(e, u):
                b = u % 2
                pe.wait_ge(act_x, done(e))
                pe.wait_ge(dve_h, done(e - 2))
                for m in range(2):
                    for k in range(KD):
                        ins = nc.tensor.matmul(GP[:, b, m * CAP:(m + 1) * CAP],
                                               GU[:, u, k, m * WIDTH:(m + 1) * WIDTH], xT[:, b, k, :],
                                               start=(k == 0), stop=(k == KD - 1))
                ins.then_inc(pe_gu, 1)

            def outputs(e, u):
                b = u % 2
                pe.wait_ge(dve_h, done(e))
                pe.wait_ge(dve_y, done(e - 2))
                nc.tensor.matmul(YP[:, b, 0:D], h[:, b], DN[:, u], start=True, stop=True).then_inc(pe_y, 1)

            with pe.Fori(0, KEPT // S) as i:
                for u in range(S):
                    e = i * S + u
                    pe.wait_ge(g_in[u], (i + 1) * 16)
                    turn(e, u)
                    pe.wait_ge(w_in[u], (i + 1) * 32)
                    products(e, u)
                    outputs(e, u)

        @block.scalar
        def _(act):
            act.preload_act_table(ACT.Silu)
            give_credit(act, act_x, act_g)
            with act.Fori(0, KEPT // S) as i:
                for u in range(S):
                    e, b = i * S + u, u % 2
                    act.wait_ge(pe_gu, done(e - 2))
                    act.wait_ge(pe_x, done(e))
                    nc.scalar.activation(xT[:, b], XT[:, b, 0:KD * CAP].rearrange("p (k c) -> p k c", k=KD), ACT.Copy)\
                        .then_inc(act_x, 1)
                    act.wait_ge(dve_h, done(e - 2))
                    act.wait_ge(pe_gu, done(e))
                    nc.scalar.activation(sg[:, b], GP[:, b, 0:CAP], ACT.Silu).then_inc(act_g, 1)

        @block.vector
        def _(dve):
            give_credit(dve, ix_ready, dve_h, dve_y)

            def indices(e, u):
                nc.vector.tensor_scalar(ix[:, u], idx[:, bass.ds(e, 1)], 0.0, None, ALU.add).then_inc(ix_ready, 1)

            indices(0, 0)
            indices(1, 1)
            with dve.Fori(0, KEPT // S) as i:
                for u in range(S):
                    e, b = i * S + u, u % 2
                    dve.wait_ge(slot_free, done(e - 2))
                    indices((e + 2) % KEPT, (u + 2) % S)
                    dve.wait_ge(pe_y, done(e - 2))
                    dve.wait_ge(act_g, done(e))
                    nc.vector.tensor_tensor(h[:, b], sg[:, b], GP[:, b, CAP:2 * CAP], ALU.mult).then_inc(dve_h, 1)
                    dve.wait_ge(pe_y, done(e))
                    nc.vector.tensor_scalar(ys[:, u], YP[:, b, 0:D], xg[:, u, bass.ds(e + D, 1)], None, ALU.mult)\
                        .then_inc(dve_y, 1)


def capacity_moe_layer(nc, a, X, ident, identb, out):
    rows = nc.dram_tensor("token_rows", (T + SPARE, ROW), F32, kind="Internal").ap()
    with ExitStack() as c:
        idx = c.enter_context(nc.sbuf_tensor("D_idx", [CAP, KEPT], U32))
        lg = c.enter_context(nc.sbuf_tensor("D_lg", [P, TILES, OLD], F32))
        known = c.enter_context(nc.sbuf_tensor("D_known", [P, 1], F32))
        with ExitStack() as c2:
            XH = c2.enter_context(nc.sbuf_tensor("D_XH", [P, KD, T], F32R))
            XL = c2.enter_context(nc.sbuf_tensor("D_XL", [P, KD, T], F32R))
            transpose_phase(nc, "lnD", X, XH, XL, ident, True, normed=rows)
            logits_phase(nc, a, XH, XL, ident, lg, known)
        kept_router_phase(nc, a, X, lg, known, ident, identb, rows, out, idx)
        kept_experts_phase(nc, a, rows, out, idx, ident)
def build_program(nc, a, out):
    x = a["L0_attn_x"].rearrange("b s d -> (b s) d")
    with ExitStack() as ctx:
        def keep(name, shape, dt=F32):
            return ctx.enter_context(nc.sbuf_tensor(name, shape, dt))

        X = keep("X", [P, TILES, D])
        ident = keep("ident", [P, P])
        identb = keep("identb", [P, P], BF16)
        mask_q = keep("mask_q", [P, P], BF16)
        mask_k = keep("mask_k", [P, P], BF16)
        kdec = keep("kdec", [P, LH])
        bdec = keep("bdec", [P, LH])
        decays = nc.dram_tensor("decays", (LH, P, 2, LBLK), F32).ap()
        constants_phase(nc, x, a["L1_attn_slope_rate"], X, ident, identb, mask_q, mask_k, decays, kdec, bdec)
        attention_layer(nc, a, X, ident, identb, mask_q, mask_k)
        latent_moe_layer(nc, a, X, ident, identb)
        linear_attention_layer(nc, a, X, ident, decays, kdec, bdec)
        capacity_moe_layer(nc, a, X, ident, identb, out)


TRANSPOSED = ("L0_attn_W_Q", "L0_attn_W_K", "L0_attn_W_V", "L0_attn_W_O", "L0_ffn_gate_w", "L0_ffn_fc1_w",
              "L0_ffn_fc2_w", "L0_ffn_w1", "L0_ffn_w2", "L0_ffn_shared_up_w", "L0_ffn_shared_down_w",
              "L1_ffn_gate_weight", "L1_ffn_gate_up_proj", "L1_ffn_down_proj")
SPARE = 96


def kernel(**inputs):
    import numpy as np
    import concourse.bacc as bacc
    from concourse.bass_utils import run_bass_kernel_spmd

    nc = bacc.Bacc("TRN2", target_bir_lowering=False, num_devices=1)
    arrays, aps = {}, {}
    for name, value in inputs.items():
        v = np.asarray(value)
        if name in TRANSPOSED:
            v = np.swapaxes(v, -1, -2)
        if name == "L1_attn_slope_rate":
            v = v.reshape(-1)
        v = np.ascontiguousarray(v)
        arrays[name] = v
        aps[name] = nc.dram_tensor(name, v.shape, mybir.dt.from_np(v.dtype), kind="ExternalInput").ap()
    out = nc.dram_tensor("out", (T + SPARE, D), F32, kind="ExternalOutput").ap()
    build_program(nc, aps, out)
    r = run_bass_kernel_spmd(nc, [arrays], core_ids=[0])
    return np.asarray(r.results[0]["out"])[:T].reshape(BATCH, SEQ, D)
```

```python
from contextlib import ExitStack

import concourse.bass as bass
from concourse import mybir

F32 = mybir.dt.float32
F32R = mybir.dt.float32r
BF16 = mybir.dt.bfloat16
U32 = mybir.dt.uint32
I32 = mybir.dt.int32
ALU = mybir.AluOpType
ACT = mybir.ActivationFunctionType
AX = mybir.AxisListType

P = 128
D = 256
KD = D // P
BATCH, SEQ = 4, 1024
T = BATCH * SEQ
TILES = T // P
CHUNK = 512
CHUNKS = T // CHUNK
TPC = CHUNK // P
NEG = -1.0e30

CREDIT = 4


def done(step):
    return step + 1 + CREDIT


class Phase:

    def __init__(self, nc, name):
        self.nc, self.name, self.ctx = nc, name, ExitStack()
        self.owned = []

    def __enter__(self):
        return self

    def __exit__(self, *exc):
        self.ctx.close()
        self.nc.clear_and_free_semaphores(self.owned)
        self.nc.all_engine_barrier()

    def sb(self, name, shape, dt=F32):
        return self.ctx.enter_context(self.nc.sbuf_tensor(f"{self.name}_{name}", shape, dt))

    def ps(self, name, shape, dt=F32):
        return self.ctx.enter_context(self.nc.psum_tensor(f"{self.name}_{name}", shape, dt))

    def sem(self, name):
        self.owned.append(self.nc.alloc_semaphore(f"{self.name}_{name}"))
        return self.owned[-1]

    def sems(self, names):
        return [self.sem(n) for n in names.split()]

    def block(self):
        return self.ctx.enter_context(self.nc.Block())


def give_credit(eng, *sems):
    for s in sems:
        eng.sem_inc(s, CREDIT)


LH, LBLK = 16, 128


def constants_phase(nc, x, x_in, slope, tab, tab_stored, X, ident, identb, mask_q, mask_k, decays, kdec, bdec):
    with Phase(nc, "const") as ph:
        slopes = ph.sb("slopes", [P, LH])
        nslopes = ph.sb("nslopes", [P, LH])
        pos_i = ph.sb("pos_i", [P, 3, LBLK], I32)
        pos = ph.sb("pos", [P, 3, LBLK])
        (pool_set, pool_sel, f_ready, slope_in, iota_ready, pos_ready, tab_exp, tab_ready) = ph.sems(
            "pool_set pool_sel ident_ready slope_in iota_ready pos_ready tab_exp tab_ready")
        block = ph.block()

        @block.sync
        def _(sp):
            sp.dma_start(slopes[:], slope.rearrange("(o h) -> o h", o=1).to_broadcast([P, LH])).then_inc(slope_in, 16)
            src = x.rearrange("(t p) n -> p t n", p=P)
            n = TILES // len(x_in)
            for g, part_in in enumerate(x_in):
                sp.dma_start(X[:, n * g:n * (g + 1), :], src[:, n * g:n * (g + 1), :]).then_inc(part_in, 16)
            sp.wait_ge(tab_ready, LH)
            sp.dma_start(decays.rearrange("h p w l -> p h w l"), tab[:]).then_inc(tab_stored, 16)

        @block.scalar
        def _(act):
            act.wait_ge(pos_ready, 2)
            for h in range(LH):
                nc.scalar.activation(tab[:, h, :, :], pos[:, 0:2, :], ACT.Exp, scale=nslopes[:, h:h + 1])\
                    .then_inc(tab_exp, 1)
            nc.scalar.activation(kdec[:], nslopes[:], ACT.Exp, scale=pos[:, 2, 0:1])
            nc.scalar.activation(bdec[:], nslopes[:], ACT.Exp, scale=float(LBLK))

        @block.gpsimd
        def _(pool):
            nc.gpsimd.iota(pos_i[:, 0, :], [[1, LBLK]], base=1, channel_multiplier=0).then_inc(iota_ready, 1)
            nc.gpsimd.iota(pos_i[:, 1, :], [[1, LBLK]], base=0, channel_multiplier=-1).then_inc(iota_ready, 1)
            nc.gpsimd.iota(pos_i[:, 2, :], [[0, LBLK]], base=LBLK - 1, channel_multiplier=-1).then_inc(iota_ready, 1)
            nc.gpsimd.memset(ident[:], 0.0).then_inc(pool_set, 1)
            nc.gpsimd.memset(mask_q[:], 0.0).then_inc(pool_set, 1)
            nc.gpsimd.memset(mask_k[:], 0.0).then_inc(pool_set, 1)
            pool.wait_ge(pool_set, 3)
            nc.gpsimd.affine_select(out=ident[:], in_=ident[:], compare_op=ALU.not_equal, fill=1.0, base=0,
                                    pattern=[[-1, P]], channel_multiplier=1).then_inc(f_ready, 1)
            nc.gpsimd.affine_select(out=mask_q[:], in_=mask_q[:], compare_op=ALU.is_ge, fill=NEG, base=0,
                                    pattern=[[-1, P]], channel_multiplier=1).then_inc(pool_sel, 1)
            nc.gpsimd.affine_select(out=mask_k[:], in_=mask_k[:], compare_op=ALU.is_ge, fill=NEG, base=0,
                                    pattern=[[1, P]], channel_multiplier=-1).then_inc(pool_sel, 1)
            for h in range(LH):
                pool.wait_ge(tab_exp, h + 1)
                nc.gpsimd.affine_select(out=tab[:, h, 1, :], in_=tab[:, h, 1, :], compare_op=ALU.is_ge, fill=0.0,
                                        base=0, pattern=[[1, LBLK]], channel_multiplier=-1).then_inc(tab_ready, 1)

        @block.vector
        def _(dve):
            dve.wait_ge(iota_ready, 3)
            nc.vector.tensor_scalar(pos[:], pos_i[:], 0.0, None, ALU.max).then_inc(pos_ready, 1)
            dve.wait_ge(slope_in, 16)
            nc.vector.tensor_scalar(nslopes[:], slopes[:], -1.0, None, ALU.mult).then_inc(pos_ready, 1)
            dve.wait_ge(f_ready, 1)
            nc.vector.tensor_copy(identb[:], ident[:])


def transpose_phase(nc, name, SRC, XH, XL, ident, norm, normed=None, prefetch=(), x_in=(),
                    stored_before=()):
    RUNS = 4
    RT, RC = TILES // RUNS, CHUNKS // RUNS
    with Phase(nc, name) as ph:
        stats = ph.sb("stats", [P, TILES, 6])
        mv = ph.sb("mv", [P, TILES, 2])
        std = ph.sb("std", [P, TILES])
        rstd = ph.sb("rstd", [P, TILES])
        shift = ph.sb("shift", [P, TILES])
        rows = ph.sb("rows", [P, 2, TPC, D])
        tr = ph.ps("tr", [P, 2, KD, CHUNK])
        (stats_ready, mv_ready, var_ready, std_ready, rstd_ready, scale_ready, rows_ready, transposed, high_ready,
         low_ready, stored0, stored1) = ph.sems("stats_ready mv_ready var_ready std_ready rstd_ready scale_ready "
                                                "rows_ready transposed high_ready low_ready stored0 stored1")
        fetched = ph.sem("fetched")
        ph.owned += [*x_in, *stored_before]
        block = ph.block()

        @block.vector
        def _(dve):
            def variances(run):
                tiles = range(run * RT, (run + 1) * RT)
                for t in tiles:
                    if x_in and t % (TILES // len(x_in)) == 0:
                        dve.wait_ge(x_in[t * len(x_in) // TILES], 16)
                    nc.vector.bn_stats(stats[:, t, :], SRC[:, t, :]).then_inc(stats_ready, 1)
                dve.wait_ge(stats_ready, (run + 1) * RT)
                for t in tiles:
                    nc.vector.bn_aggr(mv[:, t, :], stats[:, t, :]).then_inc(mv_ready, 1)
                dve.wait_ge(mv_ready, (run + 1) * RT)
                cols = slice(run * RT, (run + 1) * RT)
                nc.vector.tensor_scalar(std[:, cols], mv[:, cols, 1], 1.0e-5, None, ALU.add).then_inc(var_ready, 1)

            def scales(run):
                cols = slice(run * RT, (run + 1) * RT)
                dve.wait_ge(std_ready, run + 1)
                nc.vector.reciprocal(rstd[:, cols], std[:, cols]).then_inc(rstd_ready, 1)
                dve.wait_ge(rstd_ready, run + 1)
                nc.vector.scalar_tensor_tensor(shift[:, cols], mv[:, cols, 0], -1.0, rstd[:, cols],
                                               ALU.mult, ALU.mult).then_inc(scale_ready, 1)

            give_credit(dve, low_ready)

            def make_low(g):
                dve.wait_ge(high_ready, g + 1)
                cols = slice(g * CHUNK, (g + 1) * CHUNK)
                nc.vector.tensor_tensor(XL[:, :, cols], tr[:, g % 2], XH[:, :, cols].bitcast(F32),
                                        ALU.subtract).then_inc(low_ready, 1)

            if norm:
                variances(0)
                scales(0)
                variances(1)
            for g in range(CHUNKS):
                run = (g + 1) // RC
                if norm and (g + 1) % RC == 0 and run < RUNS:
                    scales(run)
                    if run + 1 < RUNS:
                        variances(run + 1)
                make_low(g)

        @block.tensor
        def _(pe):
            give_credit(pe, transposed)
            with pe.Fori(0, CHUNKS // 2) as i:
                for u in range(2):
                    g = i * 2 + u
                    pe.wait_ge(rows_ready, done(g))
                    pe.wait_ge(low_ready, done(g - 2))
                    for k in range(KD):
                        for j in range(TPC):
                            ins = nc.tensor.transpose(tr[:, u, k, j * P:(j + 1) * P],
                                                      rows[:, u, j, k * P:(k + 1) * P], ident[:])
                    ins.then_inc(transposed, 1)

        @block.scalar
        def _(act):
            give_credit(act, rows_ready)

            def make_rows(g):
                u = g % 2
                if norm and g % RC == 0:
                    run = g // RC
                    cols = slice(run * RT, (run + 1) * RT)
                    act.wait_ge(var_ready, run + 1)
                    nc.scalar.activation(std[:, cols], std[:, cols], ACT.Sqrt).then_inc(std_ready, 1)
                    act.wait_ge(scale_ready, run + 1)
                act.wait_ge(transposed, done(g - 2))
                if normed is not None:
                    act.wait_ge((stored0, stored1)[u], (g // 2 + 1) * 16)
                for j in range(TPC):
                    t = g * TPC + j
                    if norm:
                        ins = nc.scalar.activation(rows[:, u, j, :], SRC[:, t, :], ACT.Identity,
                                                   bias=shift[:, t:t + 1], scale=rstd[:, t:t + 1])
                if not norm:
                    ins = nc.scalar.activation(rows[:, u], SRC[:, g * TPC:(g + 1) * TPC, :], ACT.Copy)
                ins.then_inc(rows_ready, 1)

            def make_high(g):
                act.wait_ge(transposed, done(g))
                nc.scalar.activation(XH[:, :, g * CHUNK:(g + 1) * CHUNK], tr[:, g % 2], ACT.Copy)\
                    .then_inc(high_ready, 1)

            for g in range(CHUNKS + 1):
                if g < CHUNKS:
                    make_rows(g)
                if g:
                    make_high(g - 1)

        @block.sync
        def _(sp):
            for to, source in prefetch:
                sp.dma_start(to, source).then_inc(fetched, 16)
            if normed is not None:
                sp.sem_inc(stored0, 16)
                sp.sem_inc(stored1, 16)
                with sp.Fori(0, CHUNKS // 2) as i:
                    for u in range(2):
                        g = i * 2 + u
                        sp.wait_ge(rows_ready, done(g))
                        sp.dma_start(normed[bass.ds(g * CHUNK, CHUNK), 0:D].rearrange("(t p) n -> p t n", p=P),
                                     rows[:, u]).then_inc((stored0, stored1)[u], 16)
                sp.wait_ge(stored0, 16 * (CHUNKS // 2 + 1))
                sp.wait_ge(stored1, 16 * (CHUNKS // 2 + 1))
            if prefetch:
                sp.wait_ge(fetched, 16 * len(prefetch))
            for sem in stored_before:
                sp.wait_ge(sem, 16)
AH, AD = 16, 16
HG = 4
UNITS = BATCH * AH // HG
TERMS = 3
QK_TERMS = ((0, 0), (0, 1), (1, 0), (1, 1), (0, 2), (2, 0))
ROWS_QK = len(QK_TERMS) * AD
ROWS_ALL = ROWS_QK + TERMS
VW = 32


def qkv_phase(nc, raw, XH, XL, q_parts, k_parts, v_rows):
    S = 4
    with Phase(nc, "qkv") as ph:
        WH = ph.sb("WH", [P, KD, 3, D], F32R)
        WL = ph.sb("WL", [P, KD, 3, D], F32R)
        parts = ph.sb("parts", [P, S, TERMS, CHUNK], BF16)
        rest = ph.sb("rest", [P, S, CHUNK])
        vt = ph.sb("vt", [P, S, AH, VW])
        PQ = ph.ps("PQ", [P, S, CHUNK])
        PV = ph.ps("PV", [P, S, 512])
        (wh_ready, wl_ready, projected, high, rest1, mid, low, v_set, v_proj, v_copied) = ph.sems(
            "wh_ready wl_ready projected high rest1 mid low v_set v_proj v_copied")
        stored = [ph.sem(f"stored{u}") for u in range(S)]
        v_stored = [ph.sem(f"v_stored{u}") for u in range(S)]
        block = ph.block()
        RUNS = [(w, m) for w in range(2) for m in range(2)]

        def steps(eng, r):
            with eng.Fori(0, CHUNKS // S) as i:
                for u in range(S):
                    yield i, i * S + u, i * S + u + r * CHUNKS, u

        @block.sync
        def _(sp):
            for s in stored:
                sp.sem_inc(s, 16)
            for r, (w, m) in enumerate(RUNS):
                dst = (q_parts, k_parts)[w]
                for i, g, n, u in steps(sp, r):
                    sp.wait_ge(low, done(n))
                    sp.dma_start(dst[:, m * P:(m + 1) * P, bass.ds(g * CHUNK, CHUNK)]
                                 .rearrange("t p n -> p t n"), parts[:, u]).then_inc(stored[u], 16)
            for t in range(TILES):
                u = t % S
                sp.wait_ge(v_copied, t + 1)
                sp.dma_start(v_rows[:, t * P:(t + 1) * P, :].rearrange("g p n -> p g n"),
                             vt[:, u].rearrange("p (g h) d -> p g (h d)", g=AH // HG)).then_inc(v_stored[u], 16)
            for u in range(S):
                sp.wait_ge(stored[u], 16 * (1 + len(RUNS) * CHUNKS // S))
                sp.wait_ge(v_stored[u], 16 * TILES // S)

        @block.scalar
        def _(act):
            nc.scalar.activation(WH[:], raw[:], ACT.Copy).then_inc(wh_ready, 1)
            give_credit(act, high)
            for r in range(len(RUNS)):
                for i, g, n, u in steps(act, r):
                    act.wait_ge(stored[u], (i + r * CHUNKS // S + 1) * 16)
                    act.wait_ge(projected, done(n))
                    nc.scalar.activation(parts[:, u, 0], PQ[:, u], ACT.Copy).then_inc(high, 1)
            act.wait_ge(v_set, 2)
            for t in range(TILES):
                u = t % S
                act.wait_ge(v_proj, t + 1)
                if t >= S:
                    act.wait_ge(v_stored[u], 16 * (t // S))
                nc.scalar.activation(vt[:, u, :, 0:AD], PV[:, u, 0:D].rearrange("p (h d) -> p h d", d=AD), ACT.Copy)\
                    .then_inc(v_copied, 1)

        @block.vector
        def _(dve):
            dve.wait_ge(wh_ready, 1)
            nc.vector.tensor_tensor(WL[:], raw[:], WH[:].bitcast(F32), ALU.subtract).then_inc(wl_ready, 1)
            nc.vector.memset(vt[:], 0.0).then_inc(v_set, 1)
            dve.wait_ge(v_set, 1)
            nc.vector.memset(vt[:, :, :, AD:AD + 1], 1.0).then_inc(v_set, 1)
            give_credit(dve, rest1, mid)
            for r in range(len(RUNS)):
                for i, g, n, u in steps(dve, r):
                    dve.wait_ge(high, done(n))
                    dve.wait_ge(low, done(n - S))
                    nc.vector.tensor_tensor(rest[:, u], PQ[:, u], parts[:, u, 0], ALU.subtract).then_inc(rest1, 1)
                    nc.vector.tensor_tensor(parts[:, u, 1], PQ[:, u], parts[:, u, 0], ALU.subtract).then_inc(mid, 1)

        @block.gpsimd
        def _(pool):
            give_credit(pool, low)
            for r in range(len(RUNS)):
                for i, g, n, u in steps(pool, r):
                    pool.wait_ge(rest1, done(n))
                    pool.wait_ge(mid, done(n))
                    nc.gpsimd.tensor_tensor(parts[:, u, 2], rest[:, u], parts[:, u, 1], ALU.subtract).then_inc(low, 1)

        @block.tensor
        def _(pe):
            pe.wait_ge(wl_ready, 1)
            give_credit(pe, projected)
            for r, (w, m) in enumerate(RUNS):
                for i, g, n, u in steps(pe, r):
                    pe.wait_ge(mid, done(n - S))
                    s = 0
                    for W, x in ((WH, XH), (WH, XL), (WL, XH)):
                        for k in range(KD):
                            ins = nc.tensor.matmul(PQ[:, u], W[:, k, w, m * P:(m + 1) * P],
                                                   x[:, k, bass.ds(g * CHUNK, CHUNK)],
                                                   start=(s == 0), stop=(s == 3 * KD - 1))
                            s += 1
                    ins.then_inc(projected, 1)
            for t in range(TILES):
                u = t % S
                if t >= S:
                    pe.wait_ge(v_copied, t - S + 1)
                s = 0
                for x, W in ((XH, WH), (XL, WH), (XH, WL)):
                    for k in range(KD):
                        ins = nc.tensor.matmul(PV[:, u, 0:D], x[:, k, t * P:(t + 1) * P], W[:, k, 2, :],
                                               start=(s == 0), stop=(s == 3 * KD - 1))
                        s += 1
                ins.then_inc(v_proj, 1)


def score_phase(nc, q_parts, k_parts, v_rows, max_rows, AO, ident, identb, mask_q, mask_k):
    QT = SEQ // P
    SCALE = 1.0 / float(AD) ** 0.5
    PIECES = []
    for t in range(QT):
        for k0 in range(0, (t + 1) * P, CHUNK):
            nk = min(CHUNK, (t + 1) * P - k0)
            nh = {1: 4, 2: 2}.get(nk // P, 1)
            PIECES += [(t, k0, nk, h0, nh) for h0 in range(0, HG, nh)]
    GROUPS = ([[0], [1, 3], [2]], [[0, 1], [2, 3], [4, 5, 7], [6]])

    def span(half, kt):
        q0 = max(0, kt * P - half * CHUNK)
        return q0, CHUNK - q0

    def layout(half, group):
        at, out = 0, []
        for kt in group:
            q0, n = span(half, kt)
            if at % CHUNK and at % CHUNK + n > CHUNK:
                at = (at // CHUNK + 1) * CHUNK
            out.append((kt, q0, n, at))
            at += n
        return out, at

    STEPS = [(half, g) for half in range(2) for g in range(len(GROUPS[half]))]
    NS = len(STEPS) * HG
    NP = len(PIECES)
    assert NP % 2 == 0
    SHIFT = 27
    SLOTS = 4
    LAST = len(STEPS) - 1
    HALF0 = len(GROUPS[0])
    TURN = []
    NSTEPS = len(STEPS)
    for st in range(1, NSTEPS):
        TURN += [("scores", st, h) for h in range(HG)]
        TURN += [("values", st - 1, j) for j in range(len(GROUPS[STEPS[st - 1][0]][STEPS[st - 1][1]]))]
    TURN += [("scores", NSTEPS, 0), ("scores", NSTEPS, 1)]
    TURN += [("values", LAST, j) for j in range(len(GROUPS[1][-1]))]
    TURN += [("scores", NSTEPS, 2), ("scores", NSTEPS, 3)]

    def columns(kind, st, j):
        half, g = STEPS[st % NSTEPS]
        items, width = layout(half, GROUPS[half][g])
        return width if kind == "scores" else 4 * items[j][2]

    total = sum(columns(*part) for part in TURN)
    OUT = [NP * sum(columns(*part) for part in TURN[:i + 1]) // total for i in range(len(TURN))]
    ROWS_AT = TURN.index(("scores", HALF0 + 1, 2))
    HALF_AT = TURN.index(("values", HALF0 + 1, len(GROUPS[1][1]) - 1))
    assert OUT[ROWS_AT] > NP - SHIFT
    with Phase(nc, "score") as ph:
        QR = ph.sb("QR", [P, SLOTS, HG, SEQ], BF16)
        KR = ph.sb("KR", [P, SLOTS, HG, SEQ], BF16)
        V = ph.sb("V", [P, SLOTS, QT, HG, VW])
        pm = ph.sb("pm", [P, 2, HG, QT, 2])
        mx = ph.sb("mx", [P, QT, HG])
        mrest = ph.sb("mrest", [P, QT, HG])
        mparts = ph.sb("mparts", [P, QT, TERMS, HG], BF16)
        mrow = ph.sb("mrow", [TERMS * HG, SEQ], BF16)
        PR = ph.sb("PR", [P, 2, HG, 2 * CHUNK])
        OS = ph.sb("OS", [P, CHUNK])
        rc = ph.sb("rc", [P, TPC, HG, 1])
        minus_one = ph.sb("minus_one", [P, HG])
        SM = ph.ps("SM", [P, 2, CHUNK])
        SE = ph.ps("SE", [P, 2, 2 * CHUNK])
        PV = ph.ps("PV", [P, CHUNK])
        TR = ph.ps("TR", [P, CHUNK])
        TRB = TR[:].bitcast(BF16)
        loaded = [ph.sem(f"loaded{u}") for u in range(SLOTS)]
        m_in = [ph.sem(f"m_in{u}") for u in range(SLOTS)]
        (ones_set, rows_set, pe_m, dve_m, pm_done, mx_done, mh, mr1, mm, ml, m_tr, m_row, m_out,
         pe_s, act_p, pe_pv, act_o, pe_ot, dve_rc, dve_o) = ph.sems(
            "ones_set rows_set pe_m dve_m pm_done mx_done mh mr1 mm ml m_tr m_row m_out "
            "pe_s act_p pe_pv act_o pe_ot dve_rc dve_o")
        NLOAD = 2 * len(QK_TERMS) + 1
        block = ph.block()

        def turn_piece(u, k):
            ahead, p = divmod(NP + SHIFT + k, NP)
            return ahead, (u + ahead) % SLOTS, p

        @block.sync
        def _(sp):
            sp.sem_inc(m_out, 16)

            def load(n, u):
                b, hg = n // (AH // HG), n % (AH // HG)
                for j, (tq, tk) in enumerate(QK_TERMS):
                    for parts, t, dst in ((q_parts, tq, QR), (k_parts, tk, KR)):
                        src = parts[t, bass.ds(hg * HG * AD, HG * AD), bass.ds(b * SEQ, SEQ)]
                        sp.dma_start(dst[j * AD:(j + 1) * AD, u], src.rearrange("(h d) n -> d h n", d=AD))\
                            .then_inc(loaded[u], 16)
                sp.dma_start(V[:, u].rearrange("p t h d -> p t (h d)"),
                             v_rows[bass.ds(hg, 1), bass.ds(b * SEQ, SEQ), :].rearrange("o (t p) n -> p (o t) n", p=P))\
                    .then_inc(loaded[u], 16)

            def maxima(n, u):
                sp.wait_ge(m_row, done(n))
                sp.dma_start(max_rows, mrow[:]).then_inc(m_out, 16)
                sp.wait_ge(m_out, (n + 2) * 16)
                sp.dma_start(QR[ROWS_QK:ROWS_ALL, u], max_rows.rearrange("(t h) n -> t h n", t=TERMS))\
                    .then_inc(m_in[u], 16)

            for n in range(3):
                load(n, n)
            maxima(0, 0)
            with sp.Fori(0, UNITS // SLOTS) as i:
                for u in range(SLOTS):
                    n = i * SLOTS + u
                    sp.wait_ge(pe_pv, done(n * len(STEPS) - 1))
                    load((n + 3) % UNITS, (u + 3) % SLOTS)
                    maxima(n + 1, (u + 1) % SLOTS)
            for u in range(SLOTS):
                sp.wait_ge(loaded[u], 16 * NLOAD * (UNITS // SLOTS + (u < 3)))
                sp.wait_ge(m_in[u], 16 * (UNITS // SLOTS + (u < 1)))

        @block.gpsimd
        def _(pool):
            nc.gpsimd.memset(minus_one[:], -1.0).then_inc(ones_set, 1)
            pool.wait_ge(ones_set, 1)
            give_credit(pool, mx_done, mh, mr1, mm, ml)

            def max_parts(n, w):
                pool.wait_ge(pm_done, done(n))
                top = pm[:, w, :, :, 0].rearrange("p h t -> p t h")
                minus = minus_one[:].rearrange("p (o l) -> p o l", o=1).to_broadcast([P, QT, HG])
                nc.gpsimd.tensor_tensor(mx[:], top, minus, ALU.mult).then_inc(mx_done, 1)
                pool.wait_ge(m_tr, done(n - 1))
                nc.gpsimd.tensor_tensor(mparts[:, :, 0, :], top, minus, ALU.mult).then_inc(mh, 1)
                pool.wait_ge(mx_done, done(n))
                pool.wait_ge(mh, done(n))
                nc.gpsimd.tensor_tensor(mrest[:], mx[:], mparts[:, :, 0, :], ALU.subtract).then_inc(mr1, 1)
                nc.gpsimd.tensor_tensor(mparts[:, :, 1, :], mx[:], mparts[:, :, 0, :], ALU.subtract).then_inc(mm, 1)
                pool.wait_ge(mr1, done(n))
                pool.wait_ge(mm, done(n))
                nc.gpsimd.tensor_tensor(mparts[:, :, 2, :], mrest[:], mparts[:, :, 1, :], ALU.subtract)\
                    .then_inc(ml, 1)

            max_parts(0, 0)
            with pool.Fori(0, UNITS // SLOTS) as i:
                for u in range(SLOTS):
                    max_parts(i * SLOTS + u + 1, (u + 1) % 2)

        def score_columns(pe_out, lhs, rhs, diagonal, mask):
            ins = nc.tensor.matmul(pe_out, lhs, rhs, start=True, stop=diagonal is None)
            if diagonal is not None:
                ins = nc.tensor.matmul(diagonal, identb[:], mask[:], start=False, stop=True)
            return ins

        @block.tensor
        def _(pe):
            give_credit(pe, pe_m, m_tr, pe_s, pe_pv, pe_ot)

            def max_piece(count, u, p):
                t, k0, nk, h0, nh = PIECES[p]
                bank = p % 2
                pe.wait_ge(dve_m, done(count - 2))
                for j in range(nh):
                    end = (j + 1) * nk
                    diag = SM[:, bank, end - P:end] if k0 + nk == (t + 1) * P else None
                    ins = score_columns(SM[:, bank, end - nk:end], QR[0:ROWS_QK, u, h0 + j, t * P:(t + 1) * P],
                                        KR[0:ROWS_QK, u, h0 + j, k0:k0 + nk], diag, mask_q)
                ins.then_inc(pe_m, 1)

            def max_rows_out(n):
                pe.wait_ge(ml, done(n))
                for t in range(QT):
                    ins = nc.tensor.transpose(TRB[0:TERMS * HG, t * P:(t + 1) * P],
                                              mparts[:, t].rearrange("p a h -> p (a h)"), identb[:])
                ins.then_inc(m_tr, 1)

            def scores(n, u, s, h):
                half, g = STEPS[s]
                e = s * HG + h
                pe.wait_ge(act_p, done(n * NS + e - 2))
                items, _ = layout(half, GROUPS[half][g])
                for kt, q0, nq, at in items:
                    q = half * CHUNK + q0
                    cols = SE[:, e % 2, at:at + nq]
                    diag = SE[:, e % 2, at:at + P] if q == kt * P else None
                    ins = score_columns(cols, KR[0:ROWS_ALL, u, h, kt * P:(kt + 1) * P],
                                        QR[0:ROWS_ALL, u, h, q:q + nq], diag, mask_k)
                ins.then_inc(pe_s, 1)

            def values(n, u, s, j):
                half, g = STEPS[s]
                if j == 0:
                    if g == 0:
                        pe.wait_ge(act_o, done(2 * n + half - 1))
                    pe.wait_ge(act_p, done(n * NS + (s + 1) * HG - 1))
                items, _ = layout(half, GROUPS[half][g])
                last = g == len(GROUPS[half]) - 1
                kt, q0, nq, at = items[j]
                for h in range(HG):
                    ins = nc.tensor.matmul(PV[VW * h:VW * (h + 1), q0:q0 + nq], V[:, u, kt, h, :],
                                           PR[:, (u + s) % 2, h, at:at + nq], start=(g == 0 and j == 0),
                                           stop=(last and j == len(items) - 1), skip_group_check=True)
                if j == len(items) - 1:
                    ins.then_inc(pe_pv, 1)

            def outputs(n, half):
                pe.wait_ge(act_o, done(2 * n + half))
                pe.wait_ge(dve_o, done(2 * n + half - 1))
                if half == 0:
                    pe.wait_ge(m_row, done(n + 1))
                for t in range(TPC):
                    ins = nc.tensor.transpose(TR[:, t * P:(t + 1) * P], OS[:, t * P:(t + 1) * P], ident[:])
                ins.then_inc(pe_ot, 1)

            pe.wait_ge(loaded[0], 16 * NLOAD)
            pe.wait_ge(rows_set, 1)
            for g in range(NP + SHIFT):
                if g == NP:
                    pe.wait_ge(loaded[1], 16 * NLOAD)
                max_piece(g, g // NP, g % NP)
                if g == NP + SHIFT // 3:
                    max_rows_out(0)
            pe.wait_ge(m_in[0], 16)
            for h in range(HG):
                scores(0, 0, 0, h)
            with pe.Fori(0, UNITS // SLOTS) as i:
                for u in range(SLOTS):
                    n = i * SLOTS + u
                    k = 0
                    for at, (kind, s, j) in enumerate(TURN):
                        if kind == "values":
                            values(n, u, s, j)
                        elif s < NSTEPS:
                            scores(n, u, s, j)
                        else:
                            if j == 0:
                                pe.wait_ge(m_in[(u + 1) % SLOTS], (i + 1 + (u + 1) // SLOTS) * 16)
                            scores(n + 1, (u + 1) % SLOTS, 0, j)
                        while k < OUT[at]:
                            ahead, slot, p = turn_piece(u, k)
                            if ahead == 2 and p == 0:
                                pe.wait_ge(loaded[slot], (i + 1 + (u + 2) // SLOTS) * (16 * NLOAD))
                            max_piece((n + 1) * NP + SHIFT + k, slot, p)
                            k += 1
                        if at == ROWS_AT:
                            pe.wait_ge(dve_o, done(2 * n - 1))
                            max_rows_out(n + 1)
                        if at == HALF_AT:
                            outputs(n, 0)
                    outputs(n, 1)

        @block.scalar
        def _(act):
            act.preload_act_table(ACT.Exp)
            give_credit(act, act_p, act_o, m_row)

            def exps(n, u, s, h):
                half, g = STEPS[s]
                e = s * HG + h
                items, width = layout(half, GROUPS[half][g])
                act.wait_ge(pe_pv, done(n * len(STEPS) + s - 2))
                act.wait_ge(pe_s, done(n * NS + e))
                nc.scalar.activation(PR[:, (u + s) % 2, h, 0:width], SE[:, e % 2, 0:width], ACT.Exp, scale=SCALE)\
                    .then_inc(act_p, 1)

            def copy_out(n, half):
                act.wait_ge(pe_ot, done(2 * n + half - 1))
                act.wait_ge(pe_pv, done(n * len(STEPS) + (HALF0 if half == 0 else len(STEPS)) - 1))
                nc.scalar.activation(OS[:], PV[:], ACT.Copy).then_inc(act_o, 1)

            def max_row(n):
                act.wait_ge(m_tr, done(n))
                act.wait_ge(m_out, (n + 1) * 16)
                nc.scalar.activation(mrow[:], TRB[0:TERMS * HG, :], ACT.Copy).then_inc(m_row, 1)

            max_row(0)
            for h in range(HG):
                exps(0, 0, 0, h)
            with act.Fori(0, UNITS // SLOTS) as i:
                for u in range(SLOTS):
                    n = i * SLOTS + u
                    for s in range(1, len(STEPS)):
                        if s == HALF0 + 1:
                            copy_out(n, 0)
                        for h in range(HG):
                            exps(n, u, s, h)
                        if s == HALF0 + 1:
                            max_row(n + 1)
                    for h in range(HG):
                        exps(n + 1, u + 1, 0, h)
                        if h == 0:
                            copy_out(n, 1)

        @block.vector
        def _(dve):
            give_credit(dve, dve_m, pm_done, dve_rc, dve_o)

            def max_piece(count, w, p):
                t, k0, nk, h0, nh = PIECES[p]
                dve.wait_ge(pe_m, done(count))
                nc.vector.tensor_reduce(pm[:, w, h0:h0 + nh, t, k0 // CHUNK],
                                        SM[:, p % 2, 0:nh * nk].rearrange("p (h k) -> p h k", h=nh), AX.X,
                                        ALU.max).then_inc(dve_m, 1)

            def join_pieces(n, w):
                dve.wait_ge(dve_m, done((n + 1) * NP - 1))
                nc.vector.tensor_tensor(pm[:, w, :, QT // 2:QT, 0], pm[:, w, :, QT // 2:QT, 0],
                                        pm[:, w, :, QT // 2:QT, 1], ALU.max).then_inc(pm_done, 1)

            def normalise(n, half):
                tr = TR[:].rearrange("p (t h d) -> p t h d", t=TPC, h=HG)
                dve.wait_ge(pe_ot, done(2 * n + half))
                nc.vector.reciprocal(rc[:], tr[:, :, :, AD:AD + 1]).then_inc(dve_rc, 1)
                dve.wait_ge(dve_rc, done(2 * n + half))
                for t in range(TPC):
                    b, hg = n // (AH // HG), n % (AH // HG)
                    dst = AO[:, bass.ds(b * QT + half * TPC + t, 1), bass.ds(hg * HG * AD, HG * AD)]
                    ins = nc.vector.tensor_tensor(dst.rearrange("p o (h d) -> p (o h) d", d=AD), tr[:, t, :, 0:AD],
                                                  rc[:, t].to_broadcast([P, HG, AD]), ALU.mult)
                ins.then_inc(dve_o, 1)

            nc.vector.memset(KR[ROWS_QK:P], 1.0).then_inc(rows_set, 1)
            for g in range(NP + SHIFT):
                max_piece(g, g // NP % 2, g % NP)
                if g == NP - 1:
                    join_pieces(0, 0)
            with dve.Fori(0, UNITS // SLOTS) as i:
                for u in range(SLOTS):
                    n = i * SLOTS + u
                    for k in range(NP):
                        ahead, slot, p = turn_piece(u, k)
                        if ahead == 2 and p == 0:
                            dve.wait_ge(ml, done(n))
                        max_piece((n + 1) * NP + SHIFT + k, slot % 2, p)
                        if p == NP - 1:
                            join_pieces(n + 1, slot % 2)
                        if k == OUT[HALF_AT] - 1:
                            normalise(n, 0)
                    normalise(n, 1)


def output_phase(nc, raw, X, XH, XL):
    with Phase(nc, "proj") as ph:
        WH = ph.sb("WH", [P, KD, D], F32R)
        WL = ph.sb("WL", [P, KD, D], F32R)
        Y = ph.ps("Y", [P, 2, 512])
        wh_ready, wl_ready, made, added = ph.sems("wh_ready wl_ready made added")
        block = ph.block()

        @block.scalar
        def _(act):
            nc.scalar.activation(WH[:], raw[:], ACT.Copy).then_inc(wh_ready, 1)

        @block.tensor
        def _(pe):
            pe.wait_ge(wl_ready, 1)
            for t in range(TILES):
                if t >= 2:
                    pe.wait_ge(added, t - 1)
                s = 0
                for x, W in ((XH, WH), (XL, WH), (XH, WL)):
                    for k in range(KD):
                        ins = nc.tensor.matmul(Y[:, t % 2, 0:D], x[:, k, t * P:(t + 1) * P], W[:, k, :],
                                               start=(s == 0), stop=(s == 3 * KD - 1))
                        s += 1
                ins.then_inc(made, 1)

        @block.vector
        def _(dve):
            dve.wait_ge(wh_ready, 1)
            nc.vector.tensor_tensor(WL[:], raw[:], WH[:].bitcast(F32), ALU.subtract).then_inc(wl_ready, 1)
            for t in range(TILES):
                dve.wait_ge(made, t + 1)
                nc.vector.tensor_tensor(X[:, t, :], Y[:, t % 2, 0:D], X[:, t, :], ALU.add).then_inc(added, 1)


def attention_layer(nc, a, x, X, ident, identb, decays, kdec, bdec):
    q_parts = nc.dram_tensor("q_parts", (TERMS, D, T), BF16, kind="Internal").ap()
    k_parts = nc.dram_tensor("k_parts", (TERMS, D, T), BF16, kind="Internal").ap()
    v_rows = nc.dram_tensor("v_rows", (AH // HG, T, HG * VW), F32, kind="Internal").ap()
    max_rows = nc.dram_tensor("max_rows", (TERMS * HG, SEQ), BF16, kind="Internal").ap()
    masks = ExitStack()
    mask_q = masks.enter_context(nc.sbuf_tensor("mask_q", [P, P], BF16))
    mask_k = masks.enter_context(nc.sbuf_tensor("mask_k", [P, P], BF16))
    with ExitStack() as c:
        tab = c.enter_context(nc.sbuf_tensor("A_decays", [P, LH, 2, LBLK], F32))
        x_in = [nc.alloc_semaphore(f"x_in{g}") for g in range(4)]
        tab_stored = nc.alloc_semaphore("tab_stored")
        constants_phase(nc, x, x_in, a["L1_attn_slope_rate"], tab, tab_stored, X, ident, identb, mask_q, mask_k,
                        decays, kdec, bdec)
        XH = c.enter_context(nc.sbuf_tensor("A_XH", [P, KD, T], F32R))
        XL = c.enter_context(nc.sbuf_tensor("A_XL", [P, KD, T], F32R))
        raw = c.enter_context(nc.sbuf_tensor("A_w_qkv", [P, KD, 3, D], F32))
        weights = [(raw[:, :, n, :], a[f"L0_attn_W_{w}"].rearrange("(k p) n -> p k n", p=P))
                   for n, w in enumerate(("Q", "K", "V"))]
        transpose_phase(nc, "lnA", X, XH, XL, ident, True, prefetch=weights, x_in=x_in,
                        stored_before=[tab_stored])
        qkv_phase(nc, raw, XH, XL, q_parts, k_parts, v_rows)
    with ExitStack() as c:
        AO = c.enter_context(nc.sbuf_tensor("AO", [P, TILES, D], F32))
        score_phase(nc, q_parts, k_parts, v_rows, max_rows, AO, ident, identb, mask_q, mask_k)
        XH = c.enter_context(nc.sbuf_tensor("A2_XH", [P, KD, T], F32R))
        XL = c.enter_context(nc.sbuf_tensor("A2_XL", [P, KD, T], F32R))
        raw = c.enter_context(nc.sbuf_tensor("A_w_o", [P, KD, D], F32))
        transpose_phase(nc, "trA", AO, XH, XL, ident, False,
                        prefetch=[(raw[:], a["L0_attn_W_O"].rearrange("(k p) n -> p k n", p=P))])
        output_phase(nc, raw, X, XH, XL)
    masks.close()
EXPERTS, LAT, INTER, SHARED = 32, 128, 128, 512
GROUPS_E, PER_GROUP, TOP_GROUPS, TOP_K = 4, 8, 2, 8
ROUTED_SCALE = 2.5
SB = SHARED // P
NW = LAT + SHARED
CWR = TERMS * EXPERTS


def shared_phase(nc, raw, graw, down, X, XH, XL, LH, LL, scores):
    with Phase(nc, "shared") as ph:
        WH = ph.sb("WH", [P, KD, NW], F32R)
        WL = ph.sb("WL", [P, KD, NW], F32R)
        GH = ph.sb("GH", [P, KD, EXPERTS], F32R)
        GL = ph.sb("GL", [P, KD, EXPERTS], F32R)
        r = ph.sb("r", [P, 2, CHUNK])
        su = ph.sb("su", [P, 2, SB, CHUNK])
        HP = ph.ps("HP", [P, 3, CHUNK])
        OP = ph.ps("OP", [P, 2, 512])
        LG = ph.ps("LG", [P, TILES, EXPERTS])
        (wh_ready, wl_ready, pe_l, pe_h, act_lh, dve_ll, act_r, act_su, pe_o, dve_x, pe_lg,
         act_lg) = ph.sems("wh_ready wl_ready pe_l pe_h act_lh dve_ll act_r act_su pe_o dve_x pe_lg act_lg")
        block = ph.block()

        @block.scalar
        def _(act):
            nc.scalar.activation(WH[:], raw[:], ACT.Copy).then_inc(wh_ready, 1)
            nc.scalar.activation(GH[:], graw[:], ACT.Copy).then_inc(wh_ready, 1)
            give_credit(act, act_lh, act_r, act_su)

            def first(g, u, slot_used):
                act.wait_ge(pe_l, done(g))
                act.wait_ge(act_lh, CREDIT)
                nc.scalar.activation(LH[:, bass.ds(g * CHUNK, CHUNK)], HP[:, 2], ACT.Copy).then_inc(act_lh, 1)
                for s in range(SB):
                    n = g * SB + s
                    act.wait_ge(pe_h, done(n))
                    nc.scalar.activation(r[:, s % 2], HP[:, s % 2], ACT.Relu).then_inc(act_r, 1)
                    if slot_used:
                        act.wait_ge(pe_o, done((g - 1) * TPC - 1))
                    act.wait_ge(act_r, done(n))
                    nc.scalar.activation(su[:, u, s], r[:, s % 2], ACT.Square).then_inc(act_su, 1)

            first(0, 0, False)
            first(1, 1, False)
            with act.Fori(1, CHUNKS // 2) as i:
                for u in range(2):
                    first(i * 2 + u, u, True)
            act.wait_ge(pe_lg, 1)
            nc.scalar.activation(scores[:], LG[:], ACT.Sigmoid).then_inc(act_lg, 1)

        @block.tensor
        def _(pe):
            pe.wait_ge(wl_ready, 2)
            give_credit(pe, pe_l, pe_h, pe_o)

            def first_product(bank, c0, g):
                n = 0
                for W, x in ((WH, XH), (WH, XL), (WL, XH)):
                    for k in range(KD):
                        ins = nc.tensor.matmul(HP[:, bank], W[:, k, c0:c0 + P], x[:, k, bass.ds(g * CHUNK, CHUNK)],
                                               start=(n == 0), stop=(n == 3 * KD - 1))
                        n += 1
                return ins

            def first(g):
                pe.wait_ge(dve_ll, done(g - 1))
                first_product(2, 0, g).then_inc(pe_l, 1)
                for s in range(SB):
                    pe.wait_ge(act_r, done(g * SB + s - 2))
                    first_product(s % 2, LAT + s * P, g).then_inc(pe_h, 1)

            def second(g, u):
                pe.wait_ge(act_su, done(g * SB + SB - 1))
                for t in range(TPC):
                    pe.wait_ge(dve_x, done(g * TPC + t - 2))
                    for s in range(SB):
                        ins = nc.tensor.matmul(OP[:, t % 2, 0:D], su[:, u, s, t * P:(t + 1) * P], down[:, s, :],
                                               start=(s == 0), stop=(s == SB - 1))
                    ins.then_inc(pe_o, 1)

            first(0)
            with pe.Fori(0, CHUNKS // 2 - 1) as i:
                for u in range(2):
                    first(i * 2 + u + 1)
                    second(i * 2 + u, u)
            first(CHUNKS - 1)
            second(CHUNKS - 2, 0)
            second(CHUNKS - 1, 1)
            for t in range(TILES):
                n = 0
                for x, W in ((XH, GH), (XL, GH), (XH, GL)):
                    for k in range(KD):
                        ins = nc.tensor.matmul(LG[:, t, :], x[:, k, t * P:(t + 1) * P], W[:, k, :],
                                               start=(n == 0), stop=(n == 3 * KD - 1))
                        n += 1
            ins.then_inc(pe_lg, 1)

        @block.vector
        def _(dve):
            dve.wait_ge(wh_ready, 2)
            nc.vector.tensor_tensor(WL[:], raw[:], WH[:].bitcast(F32), ALU.subtract).then_inc(wl_ready, 1)
            nc.vector.tensor_tensor(GL[:], graw[:], GH[:].bitcast(F32), ALU.subtract).then_inc(wl_ready, 1)
            give_credit(dve, dve_ll, dve_x)

            def latent_low(g):
                cols = bass.ds(g * CHUNK, CHUNK)
                dve.wait_ge(act_lh, done(g))
                nc.vector.tensor_tensor(LL[:, cols], HP[:, 2], LH[:, cols].bitcast(F32), ALU.subtract)\
                    .then_inc(dve_ll, 1)

            def add(g):
                for t in range(TPC):
                    dve.wait_ge(pe_o, done(g * TPC + t))
                    xt = X[:, bass.ds(g * TPC + t, 1), :]
                    nc.vector.tensor_tensor(xt, OP[:, t % 2:t % 2 + 1, 0:D], xt, ALU.add).then_inc(dve_x, 1)

            latent_low(0)
            with dve.Fori(0, CHUNKS - 1) as g:
                latent_low(g + 1)
                add(g)
            add(CHUNKS - 1)


def group_routing_phase(nc, a, scores, CWT, identb, W1H, W1L, W2H, W2L, pick):
    E, G, N = EXPERTS, GROUPS_E, PER_GROUP
    QE = 8
    LOADS = [(w, e) for w in range(2) for e in range(0, E, QE)]
    bias = a["L0_ffn_gate_bias"]
    TAKEN = -3.0e38
    with Phase(nc, "route") as ph:
        bias_b = ph.sb("bias", [P, 1, E])
        sb_ = ph.sb("biased", [P, TILES, E])
        hi1 = ph.sb("hi1", [P, TILES * G, 4])
        lo1 = ph.sb("lo1", [P, TILES * G, 4])
        hi2 = ph.sb("hi2", [P, TILES * G, 2])
        lo2 = ph.sb("lo2", [P, TILES * G, 2])
        t2 = ph.sb("t2", [P, TILES * G, 2])
        u2 = ph.sb("u2", [P, TILES * G, 2])
        hi3 = ph.sb("hi3", [P, TILES * G, 1])
        lo3 = ph.sb("lo3", [P, TILES * G, 1])
        gs = ph.sb("gs", [P, TILES, G])
        beats = ph.sb("beats", [P, TILES, G, G - 1])
        rank = ph.sb("rank", [P, TILES, G])
        gm = ph.sb("gm", [P, TILES * G, 1])
        pen = ph.sb("pen", [P, TILES * G, 1])
        masked = ph.sb("masked", [P, TILES, E])
        top = ph.sb("top", [P, TILES, 8])
        left = ph.sb("left", [P, TILES, E])
        w = ph.sb("w", [P, TILES, E])
        total = ph.sb("total", [P, TILES, 1])
        rest = ph.sb("rest", [P, TILES, E])
        parts = ph.sb("parts", [P, TILES, TERMS, E], BF16)
        raw = ph.sb("raw", [P, 2, QE, P])
        TB = ph.ps("TB", [CWR, 4, 1024], BF16)
        (b_in, chain, parts_ready, transposed, copied, w_in0, w_in1, w_high, w_low, zero, picked) = ph.sems(
            "b_in chain parts_ready transposed copied w_in0 w_in1 w_high w_low zero picked")
        w_in = (w_in0, w_in1)
        block = ph.block()

        @block.sync
        def _(sp):
            sp.dma_start(bias_b[:, 0, :], bias.rearrange("(o e) -> o e", o=1).to_broadcast([P, E])).then_inc(b_in, 16)
            views = (a["L0_ffn_w1"].rearrange("e l i -> l e i"), a["L0_ffn_w2"].rearrange("e i l -> i e l"))
            for n, (w, e) in enumerate(LOADS):
                if n >= 2:
                    sp.wait_ge(w_low, n - 1)
                sp.dma_start(raw[:, n % 2], views[w][:, e:e + QE, :]).then_inc(w_in[n % 2], 16)

        @block.gpsimd
        def _(pool):
            nc.gpsimd.memset(pick[:], 0.0).then_inc(zero, 1)
            pool.wait_ge(zero, 1)
            for j in range(TERMS):
                rows = pick[j * E:(j + 1) * E]
                nc.gpsimd.affine_select(out=rows, in_=rows, compare_op=ALU.not_equal, fill=1.0, base=0,
                                        pattern=[[-1, E], [0, P]], channel_multiplier=1).then_inc(picked, 1)
            pool.wait_ge(picked, TERMS)
            for n, (w, e) in enumerate(LOADS):
                high, low = ((W1H, W1L), (W2H, W2L))[w]
                pool.wait_ge(w_high, n + 1)
                nc.gpsimd.tensor_tensor(low[:, e:e + QE, :], raw[:, n % 2], high[:, e:e + QE, :].bitcast(F32),
                                        ALU.subtract).then_inc(w_low, 1)

        @block.vector
        def _(dve):
            n = [0]

            def step(ins):
                n[0] += 1
                ins.then_inc(chain, 1)
                dve.wait_ge(chain, n[0])

            tt = nc.vector.tensor_tensor
            dve.wait_ge(b_in, 16)
            step(tt(sb_[:], scores[:], bias_b[:].to_broadcast([P, TILES, E]), ALU.add))
            v = sb_[:].rearrange("p t (g n) -> p (t g) n", g=G)
            step(tt(hi1[:], v[:, :, 0:4], v[:, :, 4:8], ALU.max))
            step(tt(lo1[:], v[:, :, 0:4], v[:, :, 4:8], ALU.min))
            for hi, lo, hi_n, lo_n, m in ((hi1, lo1, hi2, lo2, 2), (hi2, lo2, hi3, lo3, 1)):
                step(tt(hi_n[:], hi[:, :, 0:m], hi[:, :, m:2 * m], ALU.max))
                step(tt(t2[:, :, 0:m], hi[:, :, 0:m], hi[:, :, m:2 * m], ALU.min))
                step(tt(u2[:, :, 0:m], lo[:, :, 0:m], lo[:, :, m:2 * m], ALU.max))
                step(tt(lo_n[:], t2[:, :, 0:m], u2[:, :, 0:m], ALU.max))
            step(tt(gs[:].rearrange("p t g -> p (t g)"), hi3[:, :, 0], lo3[:, :, 0], ALU.add))
            for g in range(G):
                own = gs[:, :, g:g + 1]
                if g:
                    step(tt(beats[:, :, g, 0:g], gs[:, :, 0:g], own.to_broadcast([P, TILES, g]), ALU.is_ge))
                if g < G - 1:
                    step(tt(beats[:, :, g, g:G - 1], gs[:, :, g + 1:G], own.to_broadcast([P, TILES, G - 1 - g]),
                            ALU.is_gt))
            step(nc.vector.tensor_reduce(rank[:], beats[:], AX.X, ALU.add))
            r2 = rank[:].rearrange("p t (g o) -> p (t g) o", o=1)
            step(nc.vector.tensor_scalar(gm[:], r2, float(TOP_GROUPS), None, ALU.is_lt))
            step(nc.vector.tensor_scalar(pen[:], gm[:], 1.0, -NEG, ALU.subtract, ALU.mult))
            mv = masked[:].rearrange("p t (g n) -> p (t g) n", g=G)
            step(tt(mv, v, gm[:].to_broadcast([P, TILES * G, N]), ALU.mult))
            step(tt(mv, mv, pen[:].to_broadcast([P, TILES * G, N]), ALU.add))
            for t in range(TILES):
                ins = nc.vector.max(top[:, t, :], masked[:, t, :])
            step(ins)
            for t in range(TILES):
                ins = nc.vector.match_replace(left[:, t, :], top[:, t, :], masked[:, t, :], TAKEN)
            step(ins)
            step(nc.vector.tensor_scalar(left[:], left[:], TAKEN, None, ALU.is_equal))
            step(tt(w[:], scores[:], left[:], ALU.mult))
            step(nc.vector.tensor_reduce(total[:, :, 0], w[:], AX.X, ALU.add))
            step(nc.vector.reciprocal(total[:], total[:]))
            step(nc.vector.tensor_scalar(total[:], total[:], ROUTED_SCALE, None, ALU.mult))
            step(tt(w[:], w[:], total[:].to_broadcast([P, TILES, E]), ALU.mult))
            step(nc.vector.tensor_copy(parts[:, :, 0, :], w[:]))
            step(tt(rest[:], w[:], parts[:, :, 0, :], ALU.subtract))
            step(nc.vector.tensor_copy(parts[:, :, 1, :], rest[:]))
            tt(parts[:, :, 2, :], rest[:], parts[:, :, 1, :], ALU.subtract).then_inc(parts_ready, 1)

        @block.tensor
        def _(pe):
            pe.wait_ge(parts_ready, 1)
            for t in range(TILES):
                ins = nc.tensor.transpose(TB[:, t // 8, (t % 8) * P:(t % 8 + 1) * P],
                                          parts[:, t].rearrange("p s e -> p (s e)"), identb[:])
                if t % 8 == 7:
                    ins.then_inc(transposed, 1)

        @block.scalar
        def _(act):
            for n, (w, e) in enumerate(LOADS):
                act.wait_ge(w_in[n % 2], 16 * (n // 2 + 1))
                nc.scalar.activation((W1H, W2H)[w][:, e:e + QE, :], raw[:, n % 2], ACT.Copy).then_inc(w_high, 1)
            for j in range(4):
                act.wait_ge(transposed, j + 1)
                nc.scalar.activation(CWT[:, j * 1024:(j + 1) * 1024], TB[:, j], ACT.Copy).then_inc(copied, 1)


def experts_phase(nc, a, X, LH, LL, CWT, W1H, W1L, W2H, W2L, pick):
    E = EXPERTS
    AHEAD = 4
    SLOTS = 3

    def before(n, e):
        return n - (2 if e < 2 else SLOTS)

    with Phase(nc, "experts") as ph:
        fc2 = ph.sb("fc2", [P, D])
        r = ph.sb("r", [P, 2, CHUNK])
        sq = ph.sb("sq", [P, 2, CHUNK])
        h = ph.sb("h", [P, 2, CHUNK])
        hh = ph.sb("hh", [P, SLOTS, CHUNK], F32R)
        hl = ph.sb("hl", [P, SLOTS, CHUNK], F32R)
        y = ph.sb("y", [P, CHUNK])
        HP = ph.ps("HP", [P, SLOTS, CHUNK])
        CW = ph.ps("CW", [P, SLOTS, CHUNK])
        Y = ph.ps("Y", [P, CHUNK])
        OP = ph.ps("OP", [P, 2, D])
        (w_in, y_set, pe_h, pe_cw, act_r, act_sq, dve_h, act_hh, dve_hl, pe_y, act_y, pe_o, dve_x) = ph.sems(
            "w_in y_set pe_h pe_cw act_r act_sq dve_h act_hh dve_hl pe_y act_y pe_o dve_x")
        block = ph.block()
        COPY_AT, OUT_AFTER = AHEAD - 2, (1, 4)

        @block.sync
        def _(sp):
            sp.dma_start(fc2[:], a["L0_ffn_fc2_w"]).then_inc(w_in, 16)

        @block.scalar
        def _(act):
            give_credit(act, act_r, act_sq, act_hh, act_y)

            def relu(n, e):
                act.wait_ge(act_sq, done(n - 2))
                act.wait_ge(pe_h, done(n))
                nc.scalar.activation(r[:, e % 2], HP[:, e % SLOTS], ACT.Relu).then_inc(act_r, 1)

            def square(n, e):
                act.wait_ge(dve_h, done(n - 2))
                act.wait_ge(act_r, done(n))
                nc.scalar.activation(sq[:, e % 2], r[:, e % 2], ACT.Square).then_inc(act_sq, 1)

            def high(n, e):
                act.wait_ge(pe_y, done(before(n, e)))
                act.wait_ge(dve_h, done(n))
                nc.scalar.activation(hh[:, e % SLOTS], h[:, e % 2], ACT.Copy).then_inc(act_hh, 1)

            def copy_y(g):
                act.wait_ge(pe_o, done(2 * g - 1))
                act.wait_ge(pe_y, done(g * E - 1))
                nc.scalar.activation(y[:], Y[:], ACT.Copy).then_inc(act_y, 1)

            relu(0, 0)
            act.wait_ge(y_set, 1)
            with act.Fori(0, CHUNKS) as g:
                for e in range(E):
                    n = g * E + e
                    relu(n + 1, (e + 1) % E)
                    square(n, e)
                    if e == COPY_AT:
                        copy_y(g)
                    if e:
                        high(n - 1, e - 1)
                high(g * E + E - 1, E - 1)
            copy_y(CHUNKS)

        @block.tensor
        def _(pe):
            give_credit(pe, pe_h, pe_cw, pe_y, pe_o)

            def up(n, e, g):
                cols = bass.ds(g * CHUNK, CHUNK)
                s = e % SLOTS
                pe.wait_ge(act_r, done(before(n, e)))
                nc.tensor.matmul(HP[:, s], W1H[:, e, :], LH[:, cols], start=True, stop=False)
                nc.tensor.matmul(HP[:, s], W1H[:, e, :], LL[:, cols], start=False, stop=False)
                nc.tensor.matmul(HP[:, s], W1L[:, e, :], LH[:, cols], start=False, stop=True).then_inc(pe_h, 1)
                pe.wait_ge(dve_h, done(before(n, e)))
                nc.tensor.matmul(CW[:, s], pick[:, e, :], CWT[:, cols], start=True, stop=True).then_inc(pe_cw, 1)

            def down(n, e):
                s = e % SLOTS
                pe.wait_ge(dve_hl, done(n))
                nc.tensor.matmul(Y[:], W2H[:, e, :], hh[:, s], start=(e == 0), stop=False)
                nc.tensor.matmul(Y[:], W2L[:, e, :], hh[:, s], start=False, stop=False)
                nc.tensor.matmul(Y[:], W2H[:, e, :], hl[:, s], start=False, stop=(e == E - 1)).then_inc(pe_y, 1)

            def out(n, half):
                pe.wait_ge(dve_x, done(n - 1))
                for j in range(2):
                    t = 2 * half + j
                    ins = nc.tensor.matmul(OP[:, j, :], y[:, t * P:(t + 1) * P], fc2[:], start=True, stop=True)
                ins.then_inc(pe_o, 1)

            for e in range(AHEAD):
                up(e, e, 0)
            pe.wait_ge(w_in, 16)
            with pe.Fori(0, CHUNKS) as g:
                for e in range(E):
                    n, ahead = g * E + e, (e + AHEAD) % E
                    up(n + AHEAD, ahead, g if e + AHEAD < E else (g + 1) % CHUNKS)
                    if e == 0:
                        pe.wait_ge(act_y, done(g))
                    down(n, e)
                    if e in OUT_AFTER:
                        half = OUT_AFTER.index(e)
                        out(2 * g + half, half)
            pe.wait_ge(act_y, done(CHUNKS))
            for half in range(2):
                out(2 * CHUNKS + half, half)

        @block.vector
        def _(dve):
            nc.vector.memset(Y[:], 0.0).then_inc(y_set, 1)
            give_credit(dve, dve_h, dve_hl, dve_x)

            def weigh(n, e):
                dve.wait_ge(dve_hl, done(n - 2))
                dve.wait_ge(pe_cw, done(n))
                dve.wait_ge(act_sq, done(n))
                nc.vector.tensor_tensor(h[:, e % 2], sq[:, e % 2], CW[:, e % SLOTS], ALU.mult).then_inc(dve_h, 1)

            def low(n, e):
                dve.wait_ge(act_hh, done(n))
                nc.vector.tensor_tensor(hl[:, e % SLOTS], h[:, e % 2], hh[:, e % SLOTS].bitcast(F32), ALU.subtract)\
                    .then_inc(dve_hl, 1)

            def add(n, g, half):
                dve.wait_ge(pe_o, done(n))
                xt = X[:, bass.ds(g * TPC + 2 * half, 2), :]
                nc.vector.tensor_tensor(xt, OP[:], xt, ALU.add).then_inc(dve_x, 1)

            with dve.Fori(0, CHUNKS) as g:
                for e in range(E):
                    weigh(g * E + e, e)
                    if e:
                        low(g * E + e - 1, e - 1)
                    if e - SLOTS in OUT_AFTER:
                        half = OUT_AFTER.index(e - SLOTS)
                        add(2 * g + half, (g + CHUNKS - 1) % CHUNKS, half)
                low(g * E + E - 1, E - 1)
            dve.sem_inc(dve_h, AHEAD - SLOTS)
            for half in range(2):
                add(2 * CHUNKS + half, CHUNKS - 1, half)


def latent_moe_layer(nc, a, X, ident, identb):
    with ExitStack() as c:
        LH = c.enter_context(nc.sbuf_tensor("B_LH", [P, T], F32R))
        LL = c.enter_context(nc.sbuf_tensor("B_LL", [P, T], F32R))
        CWT = c.enter_context(nc.sbuf_tensor("B_CWT", [CWR, T], BF16))
        scores = c.enter_context(nc.sbuf_tensor("B_scores", [P, TILES, EXPERTS], F32))
        with ExitStack() as c2:
            XH = c2.enter_context(nc.sbuf_tensor("B_XH", [P, KD, T], F32R))
            XL = c2.enter_context(nc.sbuf_tensor("B_XL", [P, KD, T], F32R))
            raw = c2.enter_context(nc.sbuf_tensor("B_w_first", [P, KD, NW], F32))
            graw = c2.enter_context(nc.sbuf_tensor("B_w_gate", [P, KD, EXPERTS], F32))
            down = c2.enter_context(nc.sbuf_tensor("B_w_down", [P, SB, D], F32))
            weights = [(raw[:, :, 0:LAT], a["L0_ffn_fc1_w"].rearrange("(k p) n -> p k n", p=P)),
                       (raw[:, :, LAT:NW], a["L0_ffn_shared_up_w"].rearrange("(k p) n -> p k n", p=P)),
                       (graw[:], a["L0_ffn_gate_w"].rearrange("(k p) n -> p k n", p=P)),
                       (down[:], a["L0_ffn_shared_down_w"].rearrange("(s p) n -> p s n", p=P))]
            transpose_phase(nc, "lnB", X, XH, XL, ident, True, prefetch=weights)
            shared_phase(nc, raw, graw, down, X, XH, XL, LH, LL, scores)
        W1H, W1L, W2H, W2L = (c.enter_context(nc.sbuf_tensor(f"B_{n}", [P, EXPERTS, P], F32R))
                              for n in ("W1H", "W1L", "W2H", "W2L"))
        pick = c.enter_context(nc.sbuf_tensor("B_pick", [CWR, EXPERTS, P], BF16))
        group_routing_phase(nc, a, scores, CWT, identb, W1H, W1L, W2H, W2L, pick)
        experts_phase(nc, a, X, LH, LL, CWT, W1H, W1L, W2H, W2L, pick)
def linear_attention_phase(nc, X, XH, XL, ident, raw, wo_raw, dec_in, w_qkv, w_gate, w_out, rms_w, decays, kdec, bdec):
    H, DH, BLK = LH, 128, LBLK
    NBLK = SEQ // BLK
    HD = H * DH
    B4 = BATCH
    with Phase(nc, "lin") as ph:
        WH = ph.sb("WH", [P, 4, KD, DH], F32R)
        WL = ph.sb("WL", [P, 4, KD, DH], F32R)
        WO = ph.sb("WO", [P, D])
        WOH = ph.sb("WOH", [P, D], F32R)
        WOL = ph.sb("WOL", [P, D], F32R)
        rms = ph.sb("rms", [P, H])
        dec = ph.sb("dec", [P, 2, BLK])
        ones = ph.sb("ones", [P, 2])
        acc = ph.sb("acc", [P, TILES, D])
        o2sum = ph.sb("o2sum", [P, NBLK, B4, BLK])
        rs = ph.sb("rs", [P, TILES])
        qT = ph.sb("qT", [P, 2, B4, BLK])
        kT = ph.sb("kT", [P, 2, B4, BLK])
        vT = ph.sb("vT", [P, B4, BLK])
        v = ph.sb("v", [P, B4, DH])
        gT = ph.sb("gT", [P, 2, B4, BLK])
        qd = ph.sb("qd", [P, B4, BLK])
        sd = ph.sb("sd", [P, B4, BLK])
        kd = ph.sb("kd", [P, B4, DH])
        kv = ph.sb("kv", [P, B4, DH])
        o2 = ph.sb("o2", [P, B4, BLK])
        go = ph.sb("go", [P, B4, BLK])
        goh = ph.sb("goh", [P, B4, BLK], F32R)
        gol = ph.sb("gol", [P, B4, BLK], F32R)
        PJ = ph.ps("PJ", [P, 2, B4, P])
        S = ph.ps("S", [P, B4, P])
        KT = ph.ps("KT", [P, B4, P])
        O = ph.ps("O", [P, B4, P])
        OUT = ph.ps("OUT", [P, 2, 2, D])
        VT = ph.ps("VT", [P, B4, P])
        (w_in, wo_in, wo_scaled, woh_ready, act_goh, dve_gol, rms_in, dec_loaded, dec_ready, wh_ready, wl_ready, wo_ready, memsets, sum_set,
         pe_q, pe_k, pe_v, pe_g, pe_vt, pe_s, pe_kt, pe_o, pe_kv, pe_out0, pe_out1, pe_sum,
         act_q, act_k, act_v, act_g, act_vt, act_sq, pool_qd, pool_sum,
         dve_sd, dve_kd, dve_kv, dve_go, dve_acc0, dve_acc1, mean_ready, root_ready, rs_ready) = ph.sems(
            "w_in wo_in wo_scaled woh_ready act_goh dve_gol rms_in dec_loaded dec_ready wh_ready wl_ready wo_ready memsets sum_set "
            "pe_q pe_k pe_v pe_g pe_vt pe_s pe_kt pe_o pe_kv pe_out0 pe_out1 pe_sum "
            "act_q act_k act_v act_g act_vt act_sq pool_qd pool_sum "
            "dve_sd dve_kd dve_kv dve_go dve_acc0 dve_acc1 mean_ready root_ready rs_ready")
        pe_out = (pe_out0, pe_out1)
        dve_acc = (dve_acc0, dve_acc1)
        xh = XH[:].rearrange("p k (b c l) -> p k b c l", b=B4, c=NBLK)
        xl = XL[:].rearrange("p k (b c l) -> p k b c l", b=B4, c=NBLK)
        acc_v = acc[:].rearrange("p (b c) n -> p b c n", b=B4)
        wqkv_v = w_qkv.rearrange("(k p) n -> p k n", p=P)
        wg_v = w_gate.rearrange("(k p) n -> p k n", p=P)
        Q, K, V, G = range(4)
        PAIRS = (slice(0, 2), slice(2, 4))
        block = ph.block()

        @block.sync
        def _(sp):
            sp.dma_start(rms[:], rms_w.rearrange("(h p) -> p h", p=P), allow_slow_non_contiguous=True).then_inc(rms_in, 16)

            def load_head(h):
                for w in range(3):
                    sp.dma_start(raw[:, w], wqkv_v[:, :, bass.ds(h * DH + w * HD, DH)]).then_inc(w_in, 16)
                sp.dma_start(raw[:, G], wg_v[:, :, bass.ds(h * DH, DH)]).then_inc(w_in, 16)
                sp.dma_start(wo_raw[:], w_out[bass.ds(h * DH, DH), :]).then_inc(wo_in, 16)

            def load_decays(h):
                sp.dma_start(dec_in[:], decays[bass.ds(h, 1)].rearrange("o p w l -> p (o w) l")).then_inc(dec_loaded, 16)

            sp.sem_inc(w_in, 64)
            sp.sem_inc(wo_in, 16)
            sp.sem_inc(dec_loaded, 16)
            with sp.Fori(0, H - 1) as h:
                sp.wait_ge(dec_ready, h + 1)
                load_decays(h + 1)
                sp.wait_ge(wl_ready, 2 * (h + 1))
                sp.wait_ge(wo_ready, h + 1)
                load_head(h + 1)
            sp.wait_ge(wl_ready, 2 * H)
            sp.wait_ge(wo_ready, H)
            load_head(0)
            sp.wait_ge(w_in, 64 * (H + 1))
            sp.wait_ge(wo_in, 16 * (H + 1))

        @block.gpsimd
        def _(pool):
            nc.gpsimd.memset(o2sum[:], 0.0).then_inc(sum_set, 1)
            pool.wait_ge(sum_set, 1)
            give_credit(pool, pool_qd, pool_sum)
            with pool.Fori(0, H) as h:
                for c in range(NBLK):
                    i, u = h * NBLK + c, c % 2
                    pool.wait_ge(act_q, done(i))
                    pool.wait_ge(pe_o, done(i - 1))
                    if c == 0:
                        pool.wait_ge(dec_ready, h + 1)
                    nc.gpsimd.tensor_tensor(qd[:], qT[:, u],
                                            dec[:, 0:1, :].to_broadcast([P, B4, BLK]), ALU.mult).then_inc(pool_qd, 1)
                    pool.wait_ge(act_sq, done(i))
                    pool.wait_ge(pool_sum, done(i - 1))
                    nc.gpsimd.tensor_tensor(o2sum[:, c], o2sum[:, c], o2[:], ALU.add).then_inc(pool_sum, 1)

        @block.scalar
        def _(act):
            act.preload_act_table(ACT.Silu)
            give_credit(act, act_q, act_k, act_v, act_g, act_vt, act_sq, act_goh)

            def weights_high(load):
                act.wait_ge(w_in, (load + 1) * 64)
                act.wait_ge(pe_g, done(load * NBLK - 1))
                for pair in PAIRS:
                    nc.scalar.activation(WH[:, pair], raw[:, pair], ACT.Copy).then_inc(wh_ready, 1)

            def qk(n, u):
                act.wait_ge(pe_out1, done(n - 2))
                act.wait_ge(pool_qd, done(n - 2))
                act.wait_ge(pe_q, done(n))
                nc.scalar.activation(qT[:, u], PJ[:, 0], ACT.Silu).then_inc(act_q, 1)
                act.wait_ge(pe_k, done(n))
                nc.scalar.activation(kT[:, u], PJ[:, 1], ACT.Silu).then_inc(act_k, 1)

            def vg(n, u):
                act.wait_ge(pe_v, done(n))
                nc.scalar.activation(vT[:], PJ[:, 0], ACT.Silu).then_inc(act_v, 1)
                act.wait_ge(dve_go, done(n - 2))
                act.wait_ge(pe_g, done(n))
                nc.scalar.activation(gT[:, u], PJ[:, 1], ACT.Tanh, scale=0.5).then_inc(act_g, 1)
                act.wait_ge(pe_vt, done(n))
                nc.scalar.activation(v[:], VT[:], ACT.Copy).then_inc(act_vt, 1)

            def square(i):
                act.wait_ge(pe_o, done(i))
                act.wait_ge(pool_sum, done(i - 1))
                nc.scalar.activation(o2[:], O[:], ACT.Square).then_inc(act_sq, 1)

            def gated_high(i):
                act.wait_ge(pe_out1, done(i - 1))
                act.wait_ge(dve_go, done(i))
                nc.scalar.activation(goh[:], go[:], ACT.Copy).then_inc(act_goh, 1)

            weights_high(0)
            qk(0, 0)
            vg(0, 0)
            with act.Fori(0, H) as h:
                for c in range(NBLK):
                    i, u = h * NBLK + c, c % 2
                    if c < NBLK - 1:
                        qk(i + 1, 1 - u)
                        square(i)
                        gated_high(i)
                    else:
                        weights_high(h + 1)
                        square(i)
                        gated_high(i)
                        qk(i + 1, 1 - u)
                    vg(i + 1, 1 - u)
            act.wait_ge(mean_ready, 1)
            nc.scalar.activation(rs[:], rs[:], ACT.Sqrt).then_inc(root_ready, 1)

        @block.tensor
        def _(pe):
            give_credit(pe, pe_q, pe_k, pe_v, pe_g, pe_vt, pe_s, pe_kt, pe_o, pe_kv, pe_out0, pe_out1)

            def project(bank, w, c, sem):
                n = 0
                for a, x in ((WH, xh), (WH, xl), (WL, xh)):
                    for k in range(KD):
                        ins = nc.tensor.matmul(PJ[:, bank], a[:, w, k, :], x[:, k, :, c, :],
                                               start=(n == 0), stop=(n == 3 * KD - 1))
                        n += 1
                ins.then_inc(sem, 1)

            def project_qk(n, c, load):
                if c == 0:
                    pe.wait_ge(wl_ready, 2 * load + 1)
                pe.wait_ge(act_v, done(n - 1))
                project(0, Q, c, pe_q)
                pe.wait_ge(act_g, done(n - 1))
                project(1, K, c, pe_k)

            def project_vg(n, c, load):
                if c == 0:
                    pe.wait_ge(wl_ready, 2 * load + 2)
                pe.wait_ge(act_q, done(n))
                project(0, V, c, pe_v)
                pe.wait_ge(act_k, done(n))
                project(1, G, c, pe_g)
                pe.wait_ge(act_v, done(n))
                pe.wait_ge(act_vt, done(n - 1))
                for b in range(B4):
                    ins = nc.tensor.transpose(VT[:, b, :], vT[:, b, :], ident[:])
                ins.then_inc(pe_vt, 1)

            def output(i, h):
                pe.wait_ge(dve_gol, done(i))
                pe.wait_ge(wo_ready, h + 1)
                for half in range(2):
                    pe.wait_ge(dve_acc[half], done(i - 1))
                    for b in range(2):
                        for n, (x, w) in enumerate(((goh, WOH), (goh, WOL), (gol, WOH))):
                            ins = nc.tensor.matmul(OUT[:, half, b, :], x[:, 2 * half + b, :], w[:],
                                                   start=(n == 0), stop=(n == 2))
                    ins.then_inc(pe_out[half], 1)

            project_qk(0, 0, 0)
            project_vg(0, 0, 0)
            with pe.Fori(0, H) as h:
                for c in range(NBLK):
                    i, u = h * NBLK + c, c % 2
                    pe.wait_ge(act_k, done(i))
                    pe.wait_ge(dve_sd, done(i - 1))
                    for b in range(B4):
                        ins = nc.tensor.matmul(S[:, b, :], kT[:, u, b, :], qT[:, u, b, :], start=True, stop=True)
                    ins.then_inc(pe_s, 1)
                    if c == 0:
                        pe.wait_ge(dve_kd, done(i - 1))
                    else:
                        pe.wait_ge(dve_kv, h * (NBLK - 1) + c)
                    for b in range(B4):
                        ins = nc.tensor.transpose(KT[:, b, :], kT[:, u, b, :], ident[:])
                    ins.then_inc(pe_kt, 1)
                    if c < NBLK - 1:
                        project_qk(i + 1, c + 1, h)
                    pe.wait_ge(act_vt, done(i))
                    pe.wait_ge(dve_sd, done(i))
                    pe.wait_ge(pool_qd, done(i))
                    pe.wait_ge(dve_go, done(i - 1))
                    for b in range(B4):
                        ins = nc.tensor.matmul(O[:, b, :], v[:, b, :], sd[:, b, :], start=True, stop=(c == 0))
                        if c:
                            ins = nc.tensor.matmul(O[:, b, :], kv[:, b, :], qd[:, b, :], start=False, stop=True)
                    ins.then_inc(pe_o, 1)
                    pe.wait_ge(dve_kd, done(i))
                    if c < NBLK - 1:
                        for b in range(B4):
                            ins = nc.tensor.matmul(KT[:, b, :], kd[:, b, :], v[:, b, :], start=True, stop=True)
                        ins.then_inc(pe_kv, 1)
                        project_vg(i + 1, c + 1, h)
                        output(i, h)
                    else:
                        project_qk(i + 1, 0, h + 1)
                        output(i, h)
                        project_vg(i + 1, 0, h + 1)
            pe.wait_ge(memsets, 2)
            pe.wait_ge(pool_sum, done(H * NBLK - 1))
            pe.wait_ge(act_vt, done(H * NBLK))
            VS = VT[:].rearrange("p b l -> p (b l)")
            for b in range(B4):
                for c in range(NBLK):
                    t = b * NBLK + c
                    ins = nc.tensor.matmul(VS[:, t:t + 1], o2sum[:, c, b, :], ones[:, 0:1], start=True, stop=True)
            ins.then_inc(pe_sum, 1)

        @block.vector
        def _(dve):
            nc.vector.memset(acc[:], 0.0).then_inc(memsets, 1)
            nc.vector.memset(ones[:], 1.0).then_inc(memsets, 1)
            dve.wait_ge(memsets, 2)
            dve.wait_ge(rms_in, 16)
            give_credit(dve, dve_sd, dve_kd, dve_go, dve_gol, dve_acc0, dve_acc1)

            def weights_low(load, part):
                dve.wait_ge(wh_ready, 2 * load + part + 1)
                pair = PAIRS[part]
                nc.vector.tensor_tensor(WL[:, pair], raw[:, pair], WH[:, pair].bitcast(F32), ALU.subtract)\
                    .then_inc(wl_ready, 1)

            def weights_out(load, rms_col):
                dve.wait_ge(wo_in, (load + 1) * 16)
                nc.vector.tensor_scalar(WO[:], wo_raw[:], rms_col, 0.5, ALU.mult, ALU.mult).then_inc(wo_scaled, 1)
                dve.wait_ge(wo_scaled, load + 1)
                nc.vector.tensor_scalar(WOH[:], WO[:], 1.0, None, ALU.mult).then_inc(woh_ready, 1)
                dve.wait_ge(woh_ready, load + 1)
                nc.vector.tensor_tensor(WOL[:], WO[:], WOH[:].bitcast(F32), ALU.subtract).then_inc(wo_ready, 1)

            weights_low(0, 0)
            weights_low(0, 1)
            weights_out(0, rms[:, 0:1])
            with dve.Fori(0, H) as h:
                for c in range(NBLK):
                    i, u = h * NBLK + c, c % 2
                    if c == 0:
                        dve.wait_ge(pool_qd, done(i - 1))
                        dve.wait_ge(dve_sd, done(i - 1))
                        dve.wait_ge(dec_loaded, (h + 1) * 16)
                        nc.vector.tensor_scalar(dec[:], dec_in[:], 1.0, None, ALU.mult).then_inc(dec_ready, 1)
                        dve.wait_ge(dec_ready, h + 1)
                    dve.wait_ge(pe_s, done(i))
                    dve.wait_ge(pe_o, done(i - 1))
                    nc.vector.tensor_tensor(sd[:], S[:], dec[:, 1:2, :].to_broadcast([P, B4, BLK]),
                                            ALU.mult).then_inc(dve_sd, 1)
                    dve.wait_ge(pe_kt, done(i))
                    if c > 0:
                        dve.wait_ge(pe_kv, done(h * (NBLK - 1) + c - 1))
                    nc.vector.tensor_scalar(kd[:], KT[:], kdec[:, bass.ds(h, 1)], None, ALU.mult)\
                        .then_inc(dve_kd, 1)
                    if c == NBLK - 1:
                        weights_low(h + 1, 0)
                        weights_low(h + 1, 1)
                    dve.wait_ge(act_sq, done(i))
                    dve.wait_ge(act_g, done(i))
                    dve.wait_ge(dve_gol, done(i - 1))
                    nc.vector.scalar_tensor_tensor(go[:], gT[:, u], 1.0, O[:], ALU.add, ALU.mult)\
                        .then_inc(dve_go, 1)
                    if c < NBLK - 1:
                        dve.wait_ge(pe_kv, done(h * (NBLK - 1) + c))
                        if c == 0:
                            nc.vector.tensor_copy(kv[:], KT[:]).then_inc(dve_kv, 1)
                        else:
                            dve.wait_ge(dve_kv, h * (NBLK - 1) + c)
                            nc.vector.scalar_tensor_tensor(kv[:], kv[:], bdec[:, bass.ds(h, 1)], KT[:],
                                                           ALU.mult, ALU.add).then_inc(dve_kv, 1)
                    dve.wait_ge(act_goh, done(i))
                    dve.wait_ge(pe_out1, done(i - 1))
                    nc.vector.tensor_tensor(gol[:], go[:], goh[:].bitcast(F32), ALU.subtract).then_inc(dve_gol, 1)
                    for half in range(2):
                        dve.wait_ge(pe_out[half], done(i))
                        dve.wait_ge(dve_acc[half], done(i - 1))
                        dst = acc_v[:, 2 * half:2 * half + 2, c, :]
                        nc.vector.tensor_tensor(dst, OUT[:, half], dst, ALU.add).then_inc(dve_acc[half], 1)
                    if c == NBLK - 1:
                        weights_out(h + 1, rms[:, bass.ds((h + 1) % H, 1)])
            dve.wait_ge(pe_sum, 1)
            nc.vector.tensor_scalar(rs[:], VT[:].rearrange("p b l -> p (b l)")[:, 0:TILES], 1.0 / HD, 1.0e-6,
                                    ALU.mult, ALU.add).then_inc(mean_ready, 1)
            dve.wait_ge(root_ready, 1)
            nc.vector.reciprocal(rs[:], rs[:]).then_inc(rs_ready, 1)
            dve.wait_ge(rs_ready, 1)
            for t in range(TILES):
                nc.vector.scalar_tensor_tensor(X[:, t, :], acc[:, t, :], rs[:, t:t + 1], X[:, t, :],
                                               ALU.mult, ALU.add)


def linear_attention_layer(nc, a, X, ident, decays, kdec, bdec):
    with ExitStack() as c:
        XH = c.enter_context(nc.sbuf_tensor("C_XH", [P, KD, T], F32R))
        XL = c.enter_context(nc.sbuf_tensor("C_XL", [P, KD, T], F32R))
        raw = c.enter_context(nc.sbuf_tensor("C_w", [P, 4, KD, P], F32))
        wo_raw = c.enter_context(nc.sbuf_tensor("C_w_out", [P, D], F32))
        dec_in = c.enter_context(nc.sbuf_tensor("C_dec", [P, 2, LBLK], F32))
        w_qkv, w_gate, w_out = a["L1_attn_w_qkv"], a["L1_attn_w_gate"], a["L1_attn_w_out"]
        first = [(raw[:, w], w_qkv[:, w * LH * P:w * LH * P + P].rearrange("(k p) n -> p k n", p=P)) for w in range(3)]
        first += [(raw[:, 3], w_gate[:, 0:P].rearrange("(k p) n -> p k n", p=P)),
                  (wo_raw[:], w_out[0:P, :]),
                  (dec_in[:], decays[0:1].rearrange("o p w l -> p (o w) l"))]
        transpose_phase(nc, "lnC", X, XH, XL, ident, True, prefetch=first)
        linear_attention_phase(nc, X, XH, XL, ident, raw, wo_raw, dec_in, w_qkv, w_gate, w_out,
                               a["L1_attn_rms_weight"], decays, kdec, bdec)
KEPT, OLD, WIDTH, CAP, TOP_D = 48, 128, 96, 96, 8
ROW = D + KEPT
SLOTS = 6


def logits_phase(nc, raw, o2n, XH, XL, ident, lg, known):
    with Phase(nc, "logit") as ph:
        GH = ph.sb("GH", [P, KD, OLD], F32R)
        GL = ph.sb("GL", [P, KD, OLD], F32R)
        spread = ph.sb("spread", [P, P])
        pen = ph.sb("pen", [P, 1, OLD])
        LG = ph.ps("LG", [P, 4, TPC, OLD])
        PN = ph.ps("PN", [P, OLD])
        (known_ready, spread_ready, pen_part, pen_ready, pe_pn, gh_ready, gl_ready, pe_lg, masked) = ph.sems(
            "known_ready spread_ready pen_part pen_ready pe_pn gh_ready gl_ready pe_lg masked")
        block = ph.block()

        @block.scalar
        def _(act):
            nc.scalar.activation(GH[:], raw[:], ACT.Copy).then_inc(gh_ready, 1)

        @block.tensor
        def _(pe):
            pe.wait_ge(spread_ready, 1)
            nc.tensor.transpose(PN[:], spread[:], ident[:]).then_inc(pe_pn, 1)
            pe.wait_ge(gl_ready, 1)
            for g in range(CHUNKS):
                if g >= 4:
                    pe.wait_ge(masked, g - 3)
                for t in range(TPC):
                    tok = (g * TPC + t) * P
                    n = 0
                    for x, W in ((XH, GH), (XL, GH), (XH, GL)):
                        for k in range(KD):
                            ins = nc.tensor.matmul(LG[:, g % 4, t, :], x[:, k, tok:tok + P], W[:, k, :],
                                                   start=(n == 0), stop=(n == 3 * KD - 1))
                            n += 1
                ins.then_inc(pe_lg, 1)

        @block.vector
        def _(dve):
            nc.vector.tensor_copy(known[:], o2n[:]).then_inc(known_ready, 1)
            dve.wait_ge(known_ready, 1)
            nc.vector.tensor_scalar(pen[:, 0, 0:1], known[:], -1.0, NEG, ALU.is_equal, ALU.mult).then_inc(pen_part, 1)
            dve.wait_ge(pen_part, 1)
            nc.vector.tensor_copy(spread[:], pen[:, 0, 0:1].to_broadcast([P, P])).then_inc(spread_ready, 1)
            dve.wait_ge(gh_ready, 1)
            nc.vector.tensor_tensor(GL[:], raw[:], GH[:].bitcast(F32), ALU.subtract).then_inc(gl_ready, 1)
            dve.wait_ge(pe_pn, 1)
            nc.vector.tensor_copy(pen[:, 0, :], PN[:]).then_inc(pen_ready, 1)
            dve.wait_ge(pen_ready, 1)
            for g in range(CHUNKS):
                dve.wait_ge(pe_lg, g + 1)
                nc.vector.tensor_tensor(lg[:, g * TPC:(g + 1) * TPC, :], LG[:, g % 4],
                                        pen[:].to_broadcast([P, TPC, OLD]), ALU.add).then_inc(masked, 1)


def kept_router_phase(nc, a, X, lg, known, ident, identb, rows, out, idx):
    TH = T // 2
    HCH = CHUNKS // 2
    with Phase(nc, "keep") as ph:
        cols_i = ph.sb("cols_i", [P, KEPT], I32)
        cols = ph.sb("cols", [P, KEPT])
        perm = ph.sb("perm", [P, KEPT])
        permb = ph.sb("permb", [P, 3 * KEPT], BF16)
        stat = ph.sb("stat", [P, TILES, 1])
        top = ph.sb("top", [P, TILES, 8])
        left = ph.sb("left", [P, TILES, OLD])
        sel = ph.sb("sel", [P, TILES, OLD], BF16)
        wT = ph.sb("wT", [P, 2, CHUNK])
        sT = ph.sb("sT", [P, CHUNKS, CHUNK], BF16)
        w = ph.sb("w", [P, TILES, KEPT])
        down_i = ph.sb("down_i", [2 * KEPT, TH], I32)
        val = ph.sb("val", [2 * KEPT, 2, TH])
        early = ph.sb("early", [2 * KEPT, CAP])
        later = ph.sb("later", [KEPT, CAP])
        both = ph.sb("both", [KEPT, 2, 2 * CAP])
        first = ph.sb("first", [KEPT, CAP])
        slot_i = ph.sb("slot_i", [CAP, 1], I32)
        slot = ph.sb("slot", [CAP, 1])
        unused = ph.sb("unused", [CAP, KEPT])
        tok = ph.sb("tok", [CAP, KEPT])
        zero = ph.sb("zero", [SPARE, ROW])
        WT = ph.ps("WT", [P, 2, CHUNK])
        ST = ph.ps("ST", [P, 2, 2 * CHUNK], BF16)
        WN = ph.ps("WN", [P, TPC, OLD])
        SN = ph.ps("SN", [2 * KEPT, 2, CHUNK])
        LT = ph.ps("LT", [CAP, CAP])
        (iotas, chain, e_ready, act_e, w_ready, pe_t, act_w, act_s, pe_wn, pe_sn, dve_wn, dve_sn, early_ready, pe_later,
         list_ready, pe_lt, stored, zeroed) = ph.sems(
            "iotas chain e_ready act_e w_ready pe_t act_w act_s pe_wn pe_sn dve_wn dve_sn early_ready pe_later "
            "list_ready pe_lt "
            "stored zeroed")
        block = ph.block()

        @block.sync
        def _(sp):
            sp.dma_start(out[0:T, :].rearrange("(t p) n -> p t n", p=P), X[:]).then_inc(stored, 16)
            sp.wait_ge(zeroed, 1)
            sp.dma_start(out[T:T + SPARE, :], zero[:, 0:D]).then_inc(stored, 16)
            sp.dma_start(rows[T:T + SPARE, :], zero[:]).then_inc(stored, 16)
            sp.wait_ge(dve_wn, CHUNKS)
            sp.dma_start(rows[0:T, D:ROW].rearrange("(t p) n -> p t n", p=P), w[:]).then_inc(stored, 16)
            sp.wait_ge(stored, 64)

        @block.gpsimd
        def _(pool):
            nc.gpsimd.iota(cols_i[:], [[1, KEPT]], base=0, channel_multiplier=0).then_inc(iotas, 1)
            nc.gpsimd.iota(slot_i[:], [[0, 1]], base=0, channel_multiplier=1).then_inc(iotas, 1)
            nc.gpsimd.memset(zero[:], 0.0).then_inc(zeroed, 1)
            nc.gpsimd.iota(down_i[:], [[-1, TH]], base=T, channel_multiplier=0).then_inc(iotas, 1)

        @block.tensor
        def _(pe):
            for g in range(CHUNKS + 1):
                if g % (CHUNKS // 2) == 0 and g < CHUNKS:
                    pe.wait_ge(w_ready, g // (CHUNKS // 2) + 1)
                if g < CHUNKS:
                    b = g % 2
                    if g >= 2:
                        pe.wait_ge(act_s, g - 1)
                    for t in range(TPC):
                        nc.tensor.transpose(WT[:, b, t * P:(t + 1) * P], left[:, g * TPC + t, :], ident[:])
                        ins = nc.tensor.transpose(ST[:, b, t * P:(t + 1) * P], sel[:, g * TPC + t, :], identb[:])
                    ins.then_inc(pe_t, 1)
                if g >= 1:
                    q, b = g - 1, (g - 1) % 2
                    pe.wait_ge(act_s, q + 1)
                    if q >= 1:
                        pe.wait_ge(dve_wn, q)
                    for t in range(TPC):
                        ins = nc.tensor.matmul(WN[:, t, 0:KEPT], wT[:, b, t * P:(t + 1) * P], perm[:],
                                               start=True, stop=True)
                    ins.then_inc(pe_wn, 1)
                    if q >= HCH:
                        c = q - HCH
                        if c >= 2:
                            pe.wait_ge(dve_sn, c - 1)
                        nc.tensor.matmul(SN[:, c % 2, :], permb[:, KEPT:3 * KEPT], sT[:, c, :],
                                         start=True, stop=False)
                        nc.tensor.matmul(SN[:, c % 2, :], permb[:, 0:2 * KEPT], sT[:, q, :],
                                         start=False, stop=True).then_inc(pe_sn, 1)
            pe.wait_ge(early_ready, 1)
            nc.tensor.matmul(LT[0:KEPT, 0:CAP], ident[0:2 * KEPT, KEPT:2 * KEPT], early[:], start=True, stop=True)\
                .then_inc(pe_later, 1)
            pe.wait_ge(list_ready, 1)
            nc.tensor.transpose(LT[:, 0:KEPT], first[:], ident[0:KEPT, 0:KEPT]).then_inc(pe_lt, 1)

        @block.scalar
        def _(act):
            act.wait_ge(e_ready, 1)
            nc.scalar.activation(lg[:], lg[:], ACT.Exp).then_inc(act_e, 1)
            for g in range(CHUNKS):
                act.wait_ge(pe_t, g + 1)
                if g >= 2:
                    act.wait_ge(pe_wn, g - 1)
                nc.scalar.activation(wT[:, g % 2], WT[:, g % 2], ACT.Copy).then_inc(act_w, 1)
                nc.scalar.activation(sT[:, g], ST[:, g % 2, 0:CHUNK], ACT.Copy).then_inc(act_s, 1)

        @block.vector
        def _(dve):
            n = [0]

            def step(ins):
                n[0] += 1
                ins.then_inc(chain, 1)
                dve.wait_ge(chain, n[0])

            tt, ts = nc.vector.tensor_tensor, nc.vector.tensor_scalar
            wide = [P, TILES, OLD]
            step(nc.vector.tensor_reduce(stat[:, :, 0], lg[:], AX.X, ALU.max))
            tt(lg[:], lg[:], stat[:].to_broadcast(wide), ALU.subtract).then_inc(e_ready, 1)
            dve.wait_ge(iotas, 3)
            step(nc.vector.tensor_copy(cols[:], cols_i[:]))
            step(nc.vector.tensor_copy(slot[:], slot_i[:]))
            step(ts(perm[:], cols[:], known[:, 0:1], None, ALU.is_equal))
            step(nc.vector.memset(permb[:], 0.0))
            step(nc.vector.tensor_copy(permb[:, KEPT:2 * KEPT], perm[:]))
            dve.wait_ge(act_e, 1)
            step(nc.vector.tensor_reduce(stat[:, :, 0], lg[:], AX.X, ALU.add))
            step(nc.vector.reciprocal(stat[:], stat[:]))
            step(tt(lg[:], lg[:], stat[:].to_broadcast(wide), ALU.mult))
            for t in range(TILES):
                ins = nc.vector.max(top[:, t, :], lg[:, t, :])
            step(ins)
            for t in range(TILES):
                ins = nc.vector.match_replace(left[:, t, :], top[:, t, :], lg[:, t, :], -1.0)
            step(ins)
            step(nc.vector.tensor_reduce(stat[:, :, 0], top[:], AX.X, ALU.add))
            step(nc.vector.reciprocal(stat[:], stat[:]))
            for part in (slice(0, TILES // 2), slice(TILES // 2, TILES)):
                step(ts(sel[:, part], left[:, part], 0.0, None, ALU.is_lt))
                tt(left[:, part], lg[:, part], sel[:, part], ALU.mult).then_inc(w_ready, 1)
            for g in range(CHUNKS):
                dve.wait_ge(pe_wn, g + 1)
                tiles = slice(g * TPC, (g + 1) * TPC)
                tt(w[:, tiles, :], WN[:, :, 0:KEPT], stat[:, tiles].to_broadcast([P, TPC, KEPT]), ALU.mult)\
                    .then_inc(dve_wn, 1)
                if g >= HCH:
                    c = g - HCH
                    part = slice(c * CHUNK, (c + 1) * CHUNK)
                    dve.wait_ge(pe_sn, c + 1)
                    tt(val[:, 0, part], SN[:, c % 2], down_i[:, part], ALU.mult).then_inc(dve_sn, 1)
            dve.wait_ge(dve_sn, HCH)

            def earliest(to, src):
                for r in range(CAP // 8):
                    best = to[:, 8 * r:8 * r + 8]
                    step(nc.vector.max(best, src[:, r % 2]))
                    if r < CAP // 8 - 1:
                        step(nc.vector.match_replace(src[:, 1 - r % 2], best, src[:, r % 2], 0.0))

            earliest(early, val)
            dve.sem_inc(early_ready, 1)
            step(nc.vector.tensor_copy(both[:, 0, 0:CAP], early[0:KEPT]))
            dve.wait_ge(pe_later, 1)
            step(ts(later[:], LT[0:KEPT, 0:CAP], 0.0, -float(TH), ALU.is_gt, ALU.mult))
            step(tt(both[:, 0, CAP:2 * CAP], LT[0:KEPT, 0:CAP], later[:], ALU.add))
            earliest(first, both)
            dve.sem_inc(list_ready, 1)
            dve.wait_ge(pe_lt, 1)
            step(ts(unused[:], LT[:, 0:KEPT], 0.0, slot[:, 0:1], ALU.is_equal, ALU.mult))
            step(ts(tok[:], LT[:, 0:KEPT], -1.0, float(T), ALU.mult, ALU.add))
            tt(idx[:], tok[:], unused[:], ALU.add)


def kept_experts_phase(nc, a, rows, out, idx, ident):
    gu = a["L1_ffn_gate_up_proj"]
    dn = a["L1_ffn_down_proj"]
    S = SLOTS
    with Phase(nc, "kept") as ph:
        GU = ph.sb("GU", [P, S, KD, 2 * WIDTH])
        DN = ph.sb("DN", [WIDTH, S, D])
        ix = ph.sb("ix", [CAP, S, 1], U32)
        xg = ph.sb("xg", [CAP, S, ROW])
        xT = ph.sb("xT", [P, 2, KD, CAP])
        sg = ph.sb("sg", [WIDTH, 2, CAP])
        h = ph.sb("h", [WIDTH, 2, CAP])
        ys = ph.sb("ys", [CAP, S, D])
        XT = ph.ps("XT", [P, 2, 512])
        GP = ph.ps("GP", [WIDTH, 2, 512])
        YP = ph.ps("YP", [CAP, 2, 512])
        w_in = [ph.sem(f"w_in{u}") for u in range(S)]
        g_in = [ph.sem(f"g_in{u}") for u in range(S)]
        (ix_ready, pe_x, act_x, pe_gu, act_g, dve_h, pe_y, dve_y, added, pool_turns, slot_free) = ph.sems(
            "ix_ready pe_x act_x pe_gu act_g dve_h pe_y dve_y added pool_turns slot_free")
        block = ph.block()

        @block.sync
        def _(sp):
            def load(e, u):
                sp.dma_start(GU[:, u], gu[bass.ds(e, 1)].rearrange("e (k p) n -> p (e k) n", p=P)).then_inc(w_in[u], 16)
                sp.dma_start(DN[:, u], dn[bass.ds(e, 1)].rearrange("e i n -> i (e n)")).then_inc(w_in[u], 16)

            for u in range(S):
                load(u, u)
            with sp.Fori(0, KEPT // S - 1) as i:
                for u in range(S):
                    sp.wait_ge(pe_y, done(i * S + u))
                    load((i + 1) * S + u, u)

        @block.gpsimd
        def _(pool):
            def gather(e, u):
                pool.wait_ge(ix_ready, done(e))
                pool.sem_inc(pool_turns, 1)
                nc.gpsimd.indirect_dma_start(out=xg[:, u], out_offset=None, in_=rows,
                                             in_offset=bass.IndirectOffsetOnAxis(ap=ix[:, u], axis=0))\
                    .then_inc(g_in[u], 16)

            def scatter(e, u):
                pool.wait_ge(dve_y, done(e))
                pool.sem_inc(pool_turns, 1)
                nc.gpsimd.indirect_dma_start(out=out, out_offset=bass.IndirectOffsetOnAxis(ap=ix[:, u], axis=0),
                                             in_=ys[:, u], in_offset=None, compute_op=ALU.add).then_inc(added, 16)

            give_credit(pool, slot_free)
            for e in range(S - 1):
                gather(e, e)
            with pool.Fori(0, KEPT // S) as i:
                for u in range(S):
                    e = i * S + u
                    scatter(e, u)
                    gather(e + S - 1, (u + S - 1) % S)
                    pool.wait_ge(added, (e + 1) * 16)
                    pool.sem_inc(slot_free, 1)
            for u in range(S - 1):
                pool.wait_ge(g_in[u], 16 * (KEPT // S + 1))

        @block.tensor
        def _(pe):
            give_credit(pe, pe_x, pe_gu, pe_y)

            def turn(e, u):
                b = u % 2
                pe.wait_ge(act_x, done(e - 2))
                for k in range(KD):
                    ins = nc.tensor.transpose(XT[:, b, k * CAP:(k + 1) * CAP], xg[:, u, k * P:(k + 1) * P],
                                              ident[0:CAP, 0:CAP])
                ins.then_inc(pe_x, 1)

            def products(e, u):
                b = u % 2
                pe.wait_ge(act_x, done(e))
                pe.wait_ge(dve_h, done(e - 2))
                for m in range(2):
                    for k in range(KD):
                        ins = nc.tensor.matmul(GP[:, b, m * CAP:(m + 1) * CAP],
                                               GU[:, u, k, m * WIDTH:(m + 1) * WIDTH], xT[:, b, k, :],
                                               start=(k == 0), stop=(k == KD - 1))
                ins.then_inc(pe_gu, 1)

            def outputs(e, u):
                b = u % 2
                pe.wait_ge(dve_h, done(e))
                pe.wait_ge(dve_y, done(e - 2))
                nc.tensor.matmul(YP[:, b, 0:D], h[:, b], DN[:, u], start=True, stop=True).then_inc(pe_y, 1)

            def first(i, u):
                pe.wait_ge(g_in[u], (i + 1) * 16)
                turn(i * S + u, u)
                pe.wait_ge(w_in[u], (i + 1) * 32)
                products(i * S + u, u)

            first(0, 0)
            with pe.Fori(0, KEPT // S - 1) as i:
                for u in range(S):
                    first(i + (u + 1) // S, (u + 1) % S)
                    outputs(i * S + u, u)
            for u in range(S):
                if u + 1 < S:
                    first(KEPT // S - 1, u + 1)
                outputs(KEPT - S + u, u)

        @block.scalar
        def _(act):
            act.preload_act_table(ACT.Silu)
            give_credit(act, act_x, act_g)
            with act.Fori(0, KEPT // S) as i:
                for u in range(S):
                    e, b = i * S + u, u % 2
                    act.wait_ge(pe_gu, done(e - 2))
                    act.wait_ge(pe_x, done(e))
                    nc.scalar.activation(xT[:, b], XT[:, b, 0:KD * CAP].rearrange("p (k c) -> p k c", k=KD), ACT.Copy)\
                        .then_inc(act_x, 1)
                    act.wait_ge(dve_h, done(e - 2))
                    act.wait_ge(pe_gu, done(e))
                    nc.scalar.activation(sg[:, b], GP[:, b, 0:CAP], ACT.Silu).then_inc(act_g, 1)

        @block.vector
        def _(dve):
            give_credit(dve, ix_ready, dve_h, dve_y)

            def indices(e, u):
                nc.vector.tensor_scalar(ix[:, u], idx[:, bass.ds(e, 1)], 0.0, None, ALU.add).then_inc(ix_ready, 1)

            for e in range(S - 1):
                indices(e, e)
            with dve.Fori(0, KEPT // S) as i:
                for u in range(S):
                    e, b = i * S + u, u % 2
                    dve.wait_ge(pe_y, done(e - 2))
                    dve.wait_ge(act_g, done(e))
                    nc.vector.tensor_tensor(h[:, b], sg[:, b], GP[:, b, CAP:2 * CAP], ALU.mult).then_inc(dve_h, 1)
                    dve.wait_ge(pe_y, done(e))
                    nc.vector.tensor_scalar(ys[:, u], YP[:, b, 0:D], xg[:, u, bass.ds(e + D, 1)], None, ALU.mult)\
                        .then_inc(dve_y, 1)
                    dve.wait_ge(slot_free, done(e - 1))
                    indices((e + S - 1) % KEPT, (u + S - 1) % S)


def capacity_moe_layer(nc, a, X, ident, identb, out):
    rows = nc.dram_tensor("token_rows", (T + SPARE, ROW), F32, kind="Internal").ap()
    with ExitStack() as c:
        idx = c.enter_context(nc.sbuf_tensor("D_idx", [CAP, KEPT], U32))
        lg = c.enter_context(nc.sbuf_tensor("D_lg", [P, TILES, OLD], F32))
        known = c.enter_context(nc.sbuf_tensor("D_known", [P, 1], F32))
        with ExitStack() as c2:
            XH = c2.enter_context(nc.sbuf_tensor("D_XH", [P, KD, T], F32R))
            XL = c2.enter_context(nc.sbuf_tensor("D_XL", [P, KD, T], F32R))
            raw = c2.enter_context(nc.sbuf_tensor("D_w_gate", [P, KD, OLD], F32))
            o2n = c2.enter_context(nc.sbuf_tensor("D_o2n", [P, 1], I32))
            weights = [(o2n[:], a["L1_ffn_old_to_new"].rearrange("(p o) -> p o", o=1)),
                       (raw[:], a["L1_ffn_gate_weight"].rearrange("(k p) n -> p k n", p=P))]
            transpose_phase(nc, "lnD", X, XH, XL, ident, True, normed=rows, prefetch=weights)
            logits_phase(nc, raw, o2n, XH, XL, ident, lg, known)
        kept_router_phase(nc, a, X, lg, known, ident, identb, rows, out, idx)
        kept_experts_phase(nc, a, rows, out, idx, ident)
def build_program(nc, a, out):
    x = a["L0_attn_x"].rearrange("b s d -> (b s) d")
    with ExitStack() as ctx:
        def keep(name, shape, dt=F32):
            return ctx.enter_context(nc.sbuf_tensor(name, shape, dt))

        X = keep("X", [P, TILES, D])
        ident = keep("ident", [P, P])
        identb = keep("identb", [P, P], BF16)
        kdec = keep("kdec", [P, LH])
        bdec = keep("bdec", [P, LH])
        decays = nc.dram_tensor("decays", (LH, P, 2, LBLK), F32).ap()
        attention_layer(nc, a, x, X, ident, identb, decays, kdec, bdec)
        latent_moe_layer(nc, a, X, ident, identb)
        linear_attention_layer(nc, a, X, ident, decays, kdec, bdec)
        capacity_moe_layer(nc, a, X, ident, identb, out)


TRANSPOSED = ("L0_attn_W_Q", "L0_attn_W_K", "L0_attn_W_V", "L0_attn_W_O", "L0_ffn_gate_w", "L0_ffn_fc1_w",
              "L0_ffn_fc2_w", "L0_ffn_w1", "L0_ffn_w2", "L0_ffn_shared_up_w", "L0_ffn_shared_down_w",
              "L1_ffn_gate_weight", "L1_ffn_gate_up_proj", "L1_ffn_down_proj")
SPARE = 96


def kernel(**inputs):
    import numpy as np
    import concourse.bacc as bacc
    from concourse.bass_utils import run_bass_kernel_spmd

    nc = bacc.Bacc("TRN2", target_bir_lowering=False, num_devices=1)
    arrays, aps = {}, {}
    for name, value in inputs.items():
        v = np.asarray(value)
        if name in TRANSPOSED:
            v = np.swapaxes(v, -1, -2)
        if name == "L1_attn_slope_rate":
            v = v.reshape(-1)
        v = np.ascontiguousarray(v)
        arrays[name] = v
        aps[name] = nc.dram_tensor(name, v.shape, mybir.dt.from_np(v.dtype), kind="ExternalInput").ap()
    out = nc.dram_tensor("out", (T + SPARE, D), F32, kind="ExternalOutput").ap()
    build_program(nc, aps, out)
    r = run_bass_kernel_spmd(nc, [arrays], core_ids=[0])
    return np.asarray(r.results[0]["out"])[:T].reshape(BATCH, SEQ, D)
```
